# Optimizing a Trainium2 kernel written in Bass

```python
import numpy as np
import jax
import jax.numpy as jnp

def _softmax(x, axis=-1):
    return jax.nn.softmax(x, axis=axis)

def _gelu(x):
    return jax.nn.gelu(x, approximate=True)

def _silu(x):
    return jax.nn.silu(x)

def _sigmoid(x):
    return jax.nn.sigmoid(x)

def _layernorm(x, axis=-1, eps=1e-05):
    m = jnp.mean(x, axis=axis, keepdims=True)
    v = jnp.var(x, axis=axis, keepdims=True)
    return (x - m) / jnp.sqrt(v + eps)

def _scatter_add(tgt, idx, src, axis=0):
    return tgt.at[idx].add(src)

def _segment_sum(src, seg, n):
    return jax.ops.segment_sum(src, seg, n)
kernel_name = 'mk_flamingo_gated_d4_seqx_r4_3e9163'

def setup_inputs(seed: int=0):
    np.random.seed(seed)
    _w = jnp.asarray

    def _rec_inputs():
        import jax
        import jax.numpy as jnp
        _rk = jax.random.key(seed)
        x = -0.0002928 + 1 * jax.random.normal(jax.random.fold_in(_rk, 1), (4, 512, 256), jnp.float32)
        _lenS = 512 - jax.random.randint(jax.random.fold_in(_rk, 7), (4,), 0, max(1, 512 // 4) + 1, jnp.int32)
        _lenS2 = 64 - jax.random.randint(jax.random.fold_in(_rk, 8), (4,), 0, max(1, 64 // 4) + 1, jnp.int32)
        _ctx_1024P = jax.random.normal(jax.random.fold_in(_rk, 11), (4, 16, 256), jnp.float32)
        _ctx_1024c = jax.random.dirichlet(jax.random.fold_in(_rk, 511), 0.3 * jnp.ones((16,), jnp.float32), (4, 64))
        _ctx_1024t = jnp.einsum('bsk,bkd->bsd', _ctx_1024c, _ctx_1024P)
        _ctx_1024t = _ctx_1024t * jax.lax.rsqrt(jnp.mean(jnp.square(_ctx_1024t)) + 1e-12) * 0.953939
        ctx_1024 = -1.39393e-06 + 0.999914 * (_ctx_1024t + 0.3 * jax.random.normal(jax.random.fold_in(_rk, 611), (4, 64, 256), jnp.float32))
        _validS = jnp.arange(512)[None, :] < _lenS[:, None]
        _validS2 = jnp.arange(64)[None, :] < _lenS2[:, None]
        _causal = jnp.tril(jnp.ones((512, 512), dtype=bool))
        mask_BxSxS2_bk1 = jnp.broadcast_to(_validS2[:, None, :], (4, 512, 64))
        mask_BxS_ik1 = jnp.where(jnp.broadcast_to(_validS[:, :], (4, 512)), 1, 0).astype(jnp.int32)
        _g = jax.random.normal(jax.random.fold_in(_rk, 9001), (2, 4), jnp.float32)
        _g = jnp.sign(_g) * jnp.maximum(jnp.abs(_g), 1.0) + (_g == 0) * 1.0
        g_xattn = _g[0]
        g_ffn = _g[1]
        return (x, ctx_1024, mask_BxSxS2_bk1, mask_BxS_ik1, g_xattn, g_ffn)
    x, ctx_1024, mask_BxSxS2_bk1, mask_BxS_ik1, g_xattn, g_ffn = _rec_inputs()

    def _L0_xattn_setup():
        import jax, jax.numpy as jnp
        import numpy as np
        DIM = 256
        HEADS = 16
        DIM_HEAD = 64
        INNER = HEADS * DIM_HEAD
        B, N = (2, 512)
        key = jax.random.key(seed)
        ks = jax.random.split(key, 8)
        q = jax.random.normal(ks[0], (B, N, DIM), dtype=jnp.float32)
        k = jax.random.normal(ks[1], (B, N, DIM), dtype=jnp.float32)
        v = jax.random.normal(ks[2], (B, N, DIM), dtype=jnp.float32)
        causal = jnp.triu(jnp.ones((N, N), dtype=jnp.bool_), k=1)
        mask = jnp.broadcast_to(causal, (B, N, N))
        s = 0.02
        Wq = jax.random.normal(ks[3], (DIM, INNER), dtype=jnp.float32) * s
        Wk = jax.random.normal(ks[4], (DIM, INNER), dtype=jnp.float32) * s
        Wv = jax.random.normal(ks[5], (DIM, INNER), dtype=jnp.float32) * s
        Wo = jax.random.normal(ks[6], (INNER, DIM), dtype=jnp.float32) * s
        bo = jnp.zeros((DIM,), dtype=jnp.float32)
        return {'q': q, 'k': k, 'v': v, 'mask': mask, 'Wq': Wq, 'Wk': Wk, 'Wv': Wv, 'Wo': Wo, 'bo': bo}
    _L0_xattn_all = _L0_xattn_setup()
    _L0_xattn_in = {k: v for k, v in _L0_xattn_all.items() if k in ('Wq', 'Wk', 'Wv', 'Wo', 'bo')}
    del _L0_xattn_all

    def _L0_ffn_setup():
        import jax, jax.numpy as jnp
        import numpy as np
        QMAX = 127.0

        def _ste_round(v):
            return v + jax.lax.stop_gradient(jnp.round(v) - v)

        def _act_fake_quant(x, clip_factor):
            scale = jax.nn.sigmoid(clip_factor) * jnp.max(jnp.abs(x)) / QMAX
            return jnp.clip(_ste_round(x / scale), -QMAX - 1.0, QMAX) * scale

        def _weight_fake_quant(w):
            scale = jnp.max(jnp.abs(w), axis=1, keepdims=True) / QMAX
            return jnp.clip(_ste_round(w / scale), -QMAX - 1.0, QMAX) * scale
        key = jax.random.key(seed)
        k1, k2, k3, k4 = jax.random.split(key, 4)
        B, S, H, I = (8, 2048, 256, 704)
        return {'x': jax.random.normal(k1, (B, S, H), dtype=jnp.float32), 'clip_x': jnp.full((1,), 4.0, dtype=jnp.float32), 'clip_down': jnp.full((1,), 4.0, dtype=jnp.float32), 'w_gate': jax.random.normal(k2, (I, H), dtype=jnp.float32) * 0.02, 'w_up': jax.random.normal(k3, (I, H), dtype=jnp.float32) * 0.02, 'w_down': jax.random.normal(k4, (H, I), dtype=jnp.float32) * 0.02}
    _L0_ffn_all = _L0_ffn_setup()
    _L0_ffn_in = {k: v for k, v in _L0_ffn_all.items() if k in ('clip_x', 'clip_down', 'w_gate', 'w_up', 'w_down')}
    del _L0_ffn_all

    def _L1_xattn_setup():
        import jax, jax.numpy as jnp
        import numpy as np
        DIM = 256
        B, TQ, TK = (8, 512, 512)
        key = jax.random.key(seed)
        ks = jax.random.split(key, 8)
        s = 1.0 / np.sqrt(DIM)
        return {'texto': jax.random.normal(ks[0], (B, TQ, DIM), dtype=jnp.float32), 'imagen': jax.random.normal(ks[1], (B, TK, DIM), dtype=jnp.float32), 'Wq': jax.random.normal(ks[2], (DIM, DIM), dtype=jnp.float32) * s, 'bq': jnp.zeros((DIM,), dtype=jnp.float32), 'Wk': jax.random.normal(ks[3], (DIM, DIM), dtype=jnp.float32) * s, 'bk': jnp.zeros((DIM,), dtype=jnp.float32), 'Wv': jax.random.normal(ks[4], (DIM, DIM), dtype=jnp.float32) * s, 'bv': jnp.zeros((DIM,), dtype=jnp.float32)}
    _L1_xattn_all = _L1_xattn_setup()
    _L1_xattn_in = {k: v for k, v in _L1_xattn_all.items() if k in ('Wq', 'bq', 'Wk', 'bk', 'Wv', 'bv')}
    del _L1_xattn_all

    def _L1_ffn_setup():
        import jax, jax.numpy as jnp
        import numpy as np
        E = 8
        K = 2
        D = 256
        H = 256
        B, T = (2, 256)
        key = jax.random.key(seed)
        ks = jax.random.split(key, 6)
        s = 0.02
        return {'x': jax.random.normal(ks[0], (B, T, D), dtype=jnp.float32), 'gate_w': jax.random.normal(ks[1], (E, D), dtype=jnp.float32) * s, 'lb_bias': jnp.zeros((E,), dtype=jnp.float32), 'w1': jax.random.normal(ks[2], (E, H, D), dtype=jnp.float32) * s, 'w2': jax.random.normal(ks[3], (E, D, H), dtype=jnp.float32) * s, 'cfc': jax.random.normal(ks[4], (H, D), dtype=jnp.float32) * s, 'cproj': jax.random.normal(ks[5], (D, H), dtype=jnp.float32) * s}
    _L1_ffn_all = _L1_ffn_setup()
    _L1_ffn_in = {k: v for k, v in _L1_ffn_all.items() if k in ('gate_w', 'lb_bias', 'w1', 'w2', 'cfc', 'cproj')}
    del _L1_ffn_all

    def _L2_xattn_setup():
        import jax, jax.numpy as jnp
        import numpy as np
        HID_DIM = 256
        B, S = (8, 512)
        SCALE = float(np.sqrt(HID_DIM))
        NEG = -10000000000.0
        key = jax.random.key(seed)
        ks = jax.random.split(key, 13)
        d = HID_DIM
        std = 1.0 / np.sqrt(d)
        return {'query': jax.random.normal(ks[0], (B, S, d), jnp.float32), 'key_': jax.random.normal(ks[1], (B, S, d), jnp.float32), 'value': jax.random.normal(ks[2], (B, S, d), jnp.float32), 'mask': jax.random.randint(ks[3], (B, S), 0, 2, jnp.int32), 'Wq': jax.random.uniform(ks[4], (d, d), jnp.float32, -std, std), 'bq': jax.random.uniform(ks[5], (d,), jnp.float32, -std, std), 'Wk': jax.random.uniform(ks[6], (d, d), jnp.float32, -std, std), 'bk': jax.random.uniform(ks[7], (d,), jnp.float32, -std, std), 'Wv': jax.random.uniform(ks[8], (d, d), jnp.float32, -std, std), 'bv': jax.random.uniform(ks[9], (d,), jnp.float32, -std, std), 'Wfc': jax.random.uniform(ks[10], (d, d), jnp.float32, -std, std), 'bfc': jax.random.uniform(ks[11], (d,), jnp.float32, -std, std)}
    _L2_xattn_all = _L2_xattn_setup()
    _L2_xattn_in = {k: v for k, v in _L2_xattn_all.items() if k in ('Wq', 'bq', 'Wk', 'bk', 'Wv', 'bv', 'Wfc', 'bfc')}
    del _L2_xattn_all

    def _L2_ffn_setup():
        import jax, jax.numpy as jnp
        import numpy as np
        EXPERT_NUM = 8
        CAPACITY = 100
        key = jax.random.key(seed)
        k1, k2, k3 = jax.random.split(key, 3)
        B, S, H, E = (8, 512, 256, EXPERT_NUM)
        x = jax.random.normal(k1, (B, S, H), dtype=jnp.float32)
        w_gate = jax.random.normal(k2, (H, E), dtype=jnp.float32) * 0.02
        w_expert = jax.random.normal(k3, (H, H), dtype=jnp.float32) * 0.02
        b_expert = jnp.zeros((H,), dtype=jnp.float32)
        return {'x': x, 'w_gate': w_gate, 'w_expert': w_expert, 'b_expert': b_expert}
    _L2_ffn_all = _L2_ffn_setup()
    _L2_ffn_in = {k: v for k, v in _L2_ffn_all.items() if k in ('w_gate', 'w_expert', 'b_expert')}
    del _L2_ffn_all

    def _L3_xattn_setup():
        import jax, jax.numpy as jnp
        import numpy as np
        DIM = 256
        H = 16
        D = 64
        INNER = H * D
        EPS = 1e-05

        def layernorm(x, w, b):
            mu = jnp.mean(x, axis=-1, keepdims=True)
            var = jnp.var(x, axis=-1, keepdims=True)
            return (x - mu) * jax.lax.rsqrt(var + EPS) * w + b
        key = jax.random.key(seed)
        ks = jax.random.split(key, 8)
        B, N, S = (4, 64, 2048)
        s = 1.0 / np.sqrt(DIM)
        return {'latents': jax.random.normal(ks[0], (B, N, DIM), jnp.float32), 'context': jax.random.normal(ks[1], (B, S, DIM), jnp.float32), 'ln_l_w': jnp.ones((DIM,), jnp.float32), 'ln_l_b': jnp.zeros((DIM,), jnp.float32), 'ln_c_w': jnp.ones((DIM,), jnp.float32), 'ln_c_b': jnp.zeros((DIM,), jnp.float32), 'Wq': jax.random.normal(ks[2], (DIM, INNER), jnp.float32) * s, 'Wkv': jax.random.normal(ks[3], (DIM, 2 * INNER), jnp.float32) * s, 'Wo': jax.random.normal(ks[4], (INNER, DIM), jnp.float32) * (1.0 / np.sqrt(INNER)), 'bo': jnp.zeros((DIM,), jnp.float32)}
    _L3_xattn_all = _L3_xattn_setup()
    _L3_xattn_in = {k: v for k, v in _L3_xattn_all.items() if k in ('ln_l_w', 'ln_l_b', 'ln_c_w', 'ln_c_b', 'Wq', 'Wkv', 'Wo', 'bo')}
    del _L3_xattn_all

    def _L3_ffn_setup():
        import jax, jax.numpy as jnp
        import numpy as np
        D = 256
        F = 256
        E = 8
        K = 2
        B, T = (2, 512)

        def _moe_forward(x, router_w, w1, w2, shared_gate_up, shared_down, shared_gate_w):
            b, t, d = x.shape
            xf = x.reshape(-1, d)
            n = xf.shape[0]
            logits = xf @ router_w
            probs = jax.nn.softmax(logits, axis=-1)
            topw, topi = jax.lax.top_k(probs, K)
            combine = jnp.zeros((n, E), dtype=probs.dtype).at[jnp.arange(n)[:, None], topi].add(topw)
            h = jax.nn.silu(jnp.einsum('nd,edf->nef', xf, w1))
            ye = jnp.einsum('nef,efd->ned', h, w2)
            routed = jnp.einsum('ne,ned->nd', combine, ye)
            gu = xf @ shared_gate_up
            gate, up = (gu[:, :F], gu[:, F:])
            shared = jax.nn.silu(gate) * up @ shared_down
            shared = jax.nn.sigmoid(xf @ shared_gate_w) * shared
            return (routed + shared).reshape(b, t, d)
        key = jax.random.key(seed)
        ks = jax.random.split(key, 7)
        std = 0.02
        x = jax.random.normal(ks[0], (B, T, D), dtype=jnp.float32)
        router_w = jax.random.normal(ks[1], (D, E), dtype=jnp.float32) * std
        w1 = jax.random.normal(ks[2], (E, D, F), dtype=jnp.float32) * std
        w2 = jax.random.normal(ks[3], (E, F, D), dtype=jnp.float32) * std
        shared_gate_up = jax.random.normal(ks[4], (D, 2 * F), dtype=jnp.float32) * std
        shared_down = jax.random.normal(ks[5], (F, D), dtype=jnp.float32) * std
        shared_gate_w = jax.random.normal(ks[6], (D, 1), dtype=jnp.float32) * std
        return {'x': x, 'router_w': router_w, 'w1': w1, 'w2': w2, 'shared_gate_up': shared_gate_up, 'shared_down': shared_down, 'shared_gate_w': shared_gate_w}
    _L3_ffn_all = _L3_ffn_setup()
    _L3_ffn_in = {k: v for k, v in _L3_ffn_all.items() if k in ('router_w', 'w1', 'w2', 'shared_gate_up', 'shared_down', 'shared_gate_w')}
    del _L3_ffn_all
    return {'x': x, 'ctx_1024': ctx_1024, 'mask_BxSxS2_bk1': mask_BxSxS2_bk1, 'mask_BxS_ik1': mask_BxS_ik1, 'g_xattn': g_xattn, 'g_ffn': g_ffn, 'L0_xattn_Wq': _L0_xattn_in['Wq'], 'L0_xattn_Wk': _L0_xattn_in['Wk'], 'L0_xattn_Wv': _L0_xattn_in['Wv'], 'L0_xattn_Wo': _L0_xattn_in['Wo'], 'L0_xattn_bo': _L0_xattn_in['bo'], 'L0_ffn_clip_x': _L0_ffn_in['clip_x'], 'L0_ffn_clip_down': _L0_ffn_in['clip_down'], 'L0_ffn_w_gate': _L0_ffn_in['w_gate'], 'L0_ffn_w_up': _L0_ffn_in['w_up'], 'L0_ffn_w_down': _L0_ffn_in['w_down'], 'L1_xattn_Wq': _L1_xattn_in['Wq'], 'L1_xattn_bq': _L1_xattn_in['bq'], 'L1_xattn_Wk': _L1_xattn_in['Wk'], 'L1_xattn_bk': _L1_xattn_in['bk'], 'L1_xattn_Wv': _L1_xattn_in['Wv'], 'L1_xattn_bv': _L1_xattn_in['bv'], 'L1_ffn_gate_w': _L1_ffn_in['gate_w'], 'L1_ffn_lb_bias': _L1_ffn_in['lb_bias'], 'L1_ffn_w1': _L1_ffn_in['w1'], 'L1_ffn_w2': _L1_ffn_in['w2'], 'L1_ffn_cfc': _L1_ffn_in['cfc'], 'L1_ffn_cproj': _L1_ffn_in['cproj'], 'L2_xattn_Wq': _L2_xattn_in['Wq'], 'L2_xattn_bq': _L2_xattn_in['bq'], 'L2_xattn_Wk': _L2_xattn_in['Wk'], 'L2_xattn_bk': _L2_xattn_in['bk'], 'L2_xattn_Wv': _L2_xattn_in['Wv'], 'L2_xattn_bv': _L2_xattn_in['bv'], 'L2_xattn_Wfc': _L2_xattn_in['Wfc'], 'L2_xattn_bfc': _L2_xattn_in['bfc'], 'L2_ffn_w_gate': _L2_ffn_in['w_gate'], 'L2_ffn_w_expert': _L2_ffn_in['w_expert'], 'L2_ffn_b_expert': _L2_ffn_in['b_expert'], 'L3_xattn_ln_l_w': _L3_xattn_in['ln_l_w'], 'L3_xattn_ln_l_b': _L3_xattn_in['ln_l_b'], 'L3_xattn_ln_c_w': _L3_xattn_in['ln_c_w'], 'L3_xattn_ln_c_b': _L3_xattn_in['ln_c_b'], 'L3_xattn_Wq': _L3_xattn_in['Wq'], 'L3_xattn_Wkv': _L3_xattn_in['Wkv'], 'L3_xattn_Wo': _L3_xattn_in['Wo'], 'L3_xattn_bo': _L3_xattn_in['bo'], 'L3_ffn_router_w': _L3_ffn_in['router_w'], 'L3_ffn_w1': _L3_ffn_in['w1'], 'L3_ffn_w2': _L3_ffn_in['w2'], 'L3_ffn_shared_gate_up': _L3_ffn_in['shared_gate_up'], 'L3_ffn_shared_down': _L3_ffn_in['shared_down'], 'L3_ffn_shared_gate_w': _L3_ffn_in['shared_gate_w']}

def reference(x, ctx_1024, mask_BxSxS2_bk1, mask_BxS_ik1, g_xattn, g_ffn, L0_xattn_Wq, L0_xattn_Wk, L0_xattn_Wv, L0_xattn_Wo, L0_xattn_bo, L0_ffn_clip_x, L0_ffn_clip_down, L0_ffn_w_gate, L0_ffn_w_up, L0_ffn_w_down, L1_xattn_Wq, L1_xattn_bq, L1_xattn_Wk, L1_xattn_bk, L1_xattn_Wv, L1_xattn_bv, L1_ffn_gate_w, L1_ffn_lb_bias, L1_ffn_w1, L1_ffn_w2, L1_ffn_cfc, L1_ffn_cproj, L2_xattn_Wq, L2_xattn_bq, L2_xattn_Wk, L2_xattn_bk, L2_xattn_Wv, L2_xattn_bv, L2_xattn_Wfc, L2_xattn_bfc, L2_ffn_w_gate, L2_ffn_w_expert, L2_ffn_b_expert, L3_xattn_ln_l_w, L3_xattn_ln_l_b, L3_xattn_ln_c_w, L3_xattn_ln_c_b, L3_xattn_Wq, L3_xattn_Wkv, L3_xattn_Wo, L3_xattn_bo, L3_ffn_router_w, L3_ffn_w1, L3_ffn_w2, L3_ffn_shared_gate_up, L3_ffn_shared_down, L3_ffn_shared_gate_w):
    import jax
    import jax.numpy as jnp

    def _L0_xattn_ref(q, k, v, mask, Wq, Wk, Wv, Wo, bo):
        import jax, jax.numpy as jnp
        import numpy as np
        DIM = 256
        HEADS = 16
        DIM_HEAD = 64
        INNER = HEADS * DIM_HEAD
        B, N = (2, 512)
        h, d = (HEADS, DIM_HEAD)
        scale = d ** (-0.5)
        b, n, _ = q.shape

        def heads_split(x):
            return x.reshape(b, -1, h, d).transpose(0, 2, 1, 3)
        qh = heads_split(q @ Wq)
        kh = heads_split(k @ Wk)
        vh = heads_split(v @ Wv)
        dots = jnp.einsum('bhid,bhjd->bhij', qh, kh) * scale
        mask_value = -jnp.finfo(dots.dtype).max
        dots = jnp.where(mask[:, None, :, :], mask_value, dots)
        attn = jax.nn.softmax(dots, axis=-1)
        out = jnp.einsum('bhij,bhjd->bhid', attn, vh)
        out = out.transpose(0, 2, 1, 3).reshape(b, n, h * d)
        out = out @ Wo + bo
        return out

    def _L0_ffn_ref(x, clip_x, clip_down, w_gate, w_up, w_down):
        import jax, jax.numpy as jnp
        import numpy as np
        QMAX = 127.0

        def _ste_round(v):
            return v + jax.lax.stop_gradient(jnp.round(v) - v)

        def _act_fake_quant(x, clip_factor):
            scale = jax.nn.sigmoid(clip_factor) * jnp.max(jnp.abs(x)) / QMAX
            return jnp.clip(_ste_round(x / scale), -QMAX - 1.0, QMAX) * scale

        def _weight_fake_quant(w):
            scale = jnp.max(jnp.abs(w), axis=1, keepdims=True) / QMAX
            return jnp.clip(_ste_round(w / scale), -QMAX - 1.0, QMAX) * scale
        xq = _act_fake_quant(x, clip_x[0])
        gate = jnp.einsum('bsh,ih->bsi', xq, _weight_fake_quant(w_gate))
        up = jnp.einsum('bsh,ih->bsi', xq, _weight_fake_quant(w_up))
        h = _act_fake_quant(jax.nn.silu(gate) * up, clip_down[0])
        return jnp.einsum('bsi,hi->bsh', h, _weight_fake_quant(w_down))

    def _L1_xattn_ref(texto, imagen, Wq, bq, Wk, bk, Wv, bv):
        import jax, jax.numpy as jnp
        import numpy as np
        DIM = 256
        B, TQ, TK = (8, 512, 512)
        q = texto @ Wq + bq
        k = imagen @ Wk + bk
        v = imagen @ Wv + bv
        scale = 1.0 / jnp.sqrt(jnp.asarray(texto.shape[-1], dtype=q.dtype))
        scores = jnp.einsum('bqd,bkd->bqk', q, k) * scale
        attn = jax.nn.softmax(scores, axis=-1)
        return jnp.einsum('bqk,bkd->bqd', attn, v)

    def _L1_ffn_ref(x, gate_w, lb_bias, w1, w2, cfc, cproj):
        import jax, jax.numpy as jnp
        import numpy as np
        E = 8
        K = 2
        D = 256
        H = 256
        B, T = (2, 256)
        Bx, Tx, Dx = x.shape
        logits = jnp.einsum('btd,ed->bte', x, gate_w)
        _, idx = jax.lax.top_k(logits + lb_bias, K)
        sel_logits = jnp.take_along_axis(logits, idx, axis=-1)
        w = jax.nn.sigmoid(sel_logits)
        w = w / (jnp.sum(w, axis=-1, keepdims=True) + 1e-06)
        xf = x.reshape(-1, Dx)
        idxf = idx.reshape(-1, K)
        wf = w.reshape(-1, K)
        onehot = jax.nn.one_hot(idxf, E, dtype=wf.dtype)
        we = jnp.einsum('nke,nk->ne', onehot, wf)
        hidden = jnp.square(jax.nn.relu(jnp.einsum('nd,ehd->neh', xf, w1)))
        expert_out = jnp.einsum('neh,edh->ned', hidden, w2)
        moe_out = jnp.einsum('ned,ne->nd', expert_out, we).reshape(Bx, Tx, Dx)
        sh = jnp.square(jax.nn.relu(jnp.einsum('btd,hd->bth', x, cfc)))
        shared = jnp.einsum('bth,dh->btd', sh, cproj)
        return moe_out + shared

    def _L2_xattn_ref(query, key_, value, mask, Wq, bq, Wk, bk, Wv, bv, Wfc, bfc):
        import jax, jax.numpy as jnp
        import numpy as np
        HID_DIM = 256
        B, S = (8, 512)
        SCALE = float(np.sqrt(HID_DIM))
        NEG = -10000000000.0
        Q = jnp.einsum('bsd,ed->bse', query, Wq) + bq
        K = jnp.einsum('bsd,ed->bse', key_, Wk) + bk
        V = jnp.einsum('bsd,ed->bse', value, Wv) + bv
        energy = jnp.einsum('bqd,bkd->bqk', Q, K) / SCALE
        energy = jnp.where(mask[:, :, None] == 0, NEG, energy)
        attention = jax.nn.softmax(energy, axis=-1)
        x = jnp.einsum('bqk,bkd->bqd', attention, V)
        out = jnp.einsum('bsd,ed->bse', x, Wfc) + bfc
        return out

    def _L2_ffn_ref(x, w_gate, w_expert, b_expert):
        import jax, jax.numpy as jnp
        import numpy as np
        EXPERT_NUM = 8
        CAPACITY = 100
        B, S, H = x.shape
        E, C = (EXPERT_NUM, CAPACITY)
        hs = x.reshape(-1, H)
        logits = hs @ w_gate
        probs = jax.nn.softmax(logits, axis=1)
        best = jnp.argmax(probs, axis=1)
        mask = jax.nn.one_hot(best, E, dtype=jnp.int32)
        gate = jnp.sum(probs * mask.astype(probs.dtype), axis=1)
        locations = jnp.cumsum(mask, axis=0) - 1
        mask = mask * (locations < C).astype(jnp.int32)
        loc_sum = jnp.sum(locations * mask, axis=1)
        new_gates = gate[:, None] * mask.astype(probs.dtype)
        loc_oh = jax.nn.one_hot(loc_sum, C, dtype=probs.dtype)
        combine = new_gates[:, :, None] * loc_oh[:, None, :]
        dispatch = (combine != 0).astype(hs.dtype)
        dispatched = jnp.einsum('tec,th->ech', dispatch, hs).reshape(E * C, H)
        expert_out = dispatched @ w_expert + b_expert
        combined = combine.reshape(-1, E * C) @ expert_out
        return combined.reshape(B, S, H)

    def _L3_xattn_ref(latents, context, ln_l_w, ln_l_b, ln_c_w, ln_c_b, Wq, Wkv, Wo, bo):
        import jax, jax.numpy as jnp
        import numpy as np
        DIM = 256
        H = 16
        D = 64
        INNER = H * D
        EPS = 1e-05

        def layernorm(x, w, b):
            mu = jnp.mean(x, axis=-1, keepdims=True)
            var = jnp.var(x, axis=-1, keepdims=True)
            return (x - mu) * jax.lax.rsqrt(var + EPS) * w + b
        b, n, _ = latents.shape
        s = context.shape[1]
        lat = layernorm(latents, ln_l_w, ln_l_b)
        ctx = layernorm(context, ln_c_w, ln_c_b)
        q = (lat @ Wq).reshape(b, n, H, D).transpose(0, 2, 1, 3)
        kv = ctx @ Wkv
        k, v = jnp.split(kv, 2, axis=-1)
        k = k.reshape(b, s, H, D).transpose(0, 2, 1, 3)
        v = v.reshape(b, s, H, D).transpose(0, 2, 1, 3)
        scale = D ** (-0.5)
        attn = jnp.einsum('bhnd,bhsd->bhns', q, k) * scale
        attn = jnp.clip(attn, -11.0, 11.0)
        attn = jax.nn.softmax(attn, axis=-1)
        out = jnp.einsum('bhns,bhsd->bhnd', attn, v)
        out = out.transpose(0, 2, 1, 3).reshape(b, n, INNER)
        return out @ Wo + bo

    def _L3_ffn_ref(x, router_w, w1, w2, shared_gate_up, shared_down, shared_gate_w):
        import jax, jax.numpy as jnp
        import numpy as np
        D = 256
        F = 256
        E = 8
        K = 2
        B, T = (2, 512)

        def _moe_forward(x, router_w, w1, w2, shared_gate_up, shared_down, shared_gate_w):
            b, t, d = x.shape
            xf = x.reshape(-1, d)
            n = xf.shape[0]
            logits = xf @ router_w
            probs = jax.nn.softmax(logits, axis=-1)
            topw, topi = jax.lax.top_k(probs, K)
            combine = jnp.zeros((n, E), dtype=probs.dtype).at[jnp.arange(n)[:, None], topi].add(topw)
            h = jax.nn.silu(jnp.einsum('nd,edf->nef', xf, w1))
            ye = jnp.einsum('nef,efd->ned', h, w2)
            routed = jnp.einsum('ne,ned->nd', combine, ye)
            gu = xf @ shared_gate_up
            gate, up = (gu[:, :F], gu[:, F:])
            shared = jax.nn.silu(gate) * up @ shared_down
            shared = jax.nn.sigmoid(xf @ shared_gate_w) * shared
            return (routed + shared).reshape(b, t, d)
        return _moe_forward(x, router_w, w1, w2, shared_gate_up, shared_down, shared_gate_w)
    x = x + jnp.tanh(g_xattn[0]) * _L0_xattn_ref(_layernorm(x, axis=-1), ctx_1024, ctx_1024, mask_BxSxS2_bk1, L0_xattn_Wq, L0_xattn_Wk, L0_xattn_Wv, L0_xattn_Wo, L0_xattn_bo)
    x = x + jnp.tanh(g_ffn[0]) * _L0_ffn_ref(_layernorm(x, axis=-1), L0_ffn_clip_x, L0_ffn_clip_down, L0_ffn_w_gate, L0_ffn_w_up, L0_ffn_w_down)
    x = x + jnp.tanh(g_xattn[1]) * _L1_xattn_ref(_layernorm(x, axis=-1), ctx_1024, L1_xattn_Wq, L1_xattn_bq, L1_xattn_Wk, L1_xattn_bk, L1_xattn_Wv, L1_xattn_bv)
    x = x + jnp.tanh(g_ffn[1]) * _L1_ffn_ref(_layernorm(x, axis=-1), L1_ffn_gate_w, L1_ffn_lb_bias, L1_ffn_w1, L1_ffn_w2, L1_ffn_cfc, L1_ffn_cproj)
    x = x + jnp.tanh(g_xattn[2]) * _L2_xattn_ref(_layernorm(x, axis=-1), ctx_1024, ctx_1024, mask_BxS_ik1, L2_xattn_Wq, L2_xattn_bq, L2_xattn_Wk, L2_xattn_bk, L2_xattn_Wv, L2_xattn_bv, L2_xattn_Wfc, L2_xattn_bfc)
    x = x + jnp.tanh(g_ffn[2]) * _L2_ffn_ref(_layernorm(x, axis=-1), L2_ffn_w_gate, L2_ffn_w_expert, L2_ffn_b_expert)
    x = x + jnp.tanh(g_xattn[3]) * _L3_xattn_ref(_layernorm(x, axis=-1), ctx_1024, L3_xattn_ln_l_w, L3_xattn_ln_l_b, L3_xattn_ln_c_w, L3_xattn_ln_c_b, L3_xattn_Wq, L3_xattn_Wkv, L3_xattn_Wo, L3_xattn_bo)
    x = x + jnp.tanh(g_ffn[3]) * _L3_ffn_ref(_layernorm(x, axis=-1), L3_ffn_router_w, L3_ffn_w1, L3_ffn_w2, L3_ffn_shared_gate_up, L3_ffn_shared_down, L3_ffn_shared_gate_w)
    return x

_drawn_inputs = setup_inputs


def setup_inputs(seed=0):
    import zlib

    import numpy as np

    out = dict(_drawn_inputs(seed))
    spreads = {'L0_xattn_bo': (0.0, 0.1),
     'L1_xattn_bq': (0.0, 0.418),
     'L1_xattn_bk': (0.0, 0.8),
     'L1_xattn_bv': (0.0, 0.1),
     'L1_ffn_lb_bias': (0.0, 0.617),
     'L2_ffn_b_expert': (0.0, 0.8),
     'L3_xattn_ln_l_w': (1.0, 0.541),
     'L3_xattn_ln_l_b': (0.0, 0.603),
     'L3_xattn_ln_c_w': (1.0, 0.2),
     'L3_xattn_ln_c_b': (0.0, 0.1),
     'L3_xattn_bo': (0.0, 0.1)}
    factors = {'g_ffn': 8.0,
     'L0_xattn_Wq': 8.0,
     'L0_xattn_Wk': 8.0,
     'L0_ffn_w_gate': 2.783,
     'L1_ffn_gate_w': 3.136,
     'L1_ffn_w1': 2.874,
     'L2_xattn_Wq': 4.155,
     'L2_xattn_bq': 8.0,
     'L2_xattn_Wk': 4.021,
     'L2_xattn_bk': 8.0,
     'L2_xattn_bv': 4.065,
     'L2_ffn_w_gate': 4.07,
     'L3_ffn_router_w': 7.023,
     'L3_ffn_w1': 6.087,
     'L3_ffn_w2': 5.977,
     'L3_ffn_shared_gate_up': 8.0,
     'L3_ffn_shared_down': 8.0,
     'L3_ffn_shared_gate_w': 8.0}
    for name, (base, spread) in spreads.items():
        noise = np.random.default_rng([zlib.crc32(name.encode()), seed]).standard_normal(out[name].shape)
        drawn = base * np.exp(spread * noise) if base else spread * noise
        out[name] = jnp.asarray(drawn.astype(out[name].dtype))
    for name, factor in factors.items():
        out[name] = (out[name] * factor).astype(out[name].dtype)
    return out
```

```python
from contextlib import ExitStack

import numpy as np
import concourse.bass as bass
from concourse import mybir

ALU = mybir.AluOpType
ACT = mybir.ActivationFunctionType
AX = mybir.AxisListType
F32 = mybir.dt.float32
BF16 = mybir.dt.bfloat16
U32 = mybir.dt.uint32
I32 = mybir.dt.int32
U8 = mybir.dt.uint8
RMAX = bass.bass_isa.ReduceOp.max

P = 128
D = 256
KD = D // P
NB, S = 4, 512
TB = S // P
NT = NB * TB
C = 64
NC_ = NB * C
H, DH = 16, 64
INNER = H * DH
MI = INNER // P
FQ = 704
NFQ = (FQ + P - 1) // P
RFQ = FQ - (NFQ - 1) * P
NE = 8
CAP = 100
EPS = 1e-5
QMAX = 127.0
MAGIC = 1.5 * 2.0 ** 23
FMAX = float(np.finfo(np.float32).max)

PRE = {"pt": [2 + 2 + 4, 13 - 2, 1, 18, 3, 0, 4, 0], "sh": [28, 0, 3, 0, 3, 0, 28, 0],
       "o": [0] * 8, "ln": [1, 0, 0, 0, 0, 0, 0, 0]}
PER = {"pt": [10, 0, 3, 4, 3, 5, 10, 4], "sh": [4, 6, 1, 9, 1, 0, 4, 10],
       "o": [4, 2, 2, 18, 2, 2, 4, 18], "ln": [1, 0, 1, 1, 1, 1, 1, 1]}


def start_of(pipe, stage):
    return sum(PRE[pipe][s] + NB * PER[pipe][s] for s in range(stage))


class Block:

    def __init__(self, u, i=None):
        self.u, self.i = u, i

    def scaled(self, k, plus=0):
        return self.u * k + plus if self.i is None else self.i * (2 * k) + (self.u * k + plus)

    def fill(self, pipe, stage, k=0):
        first = start_of(pipe, stage) + PRE[pipe][stage] + k
        return self.scaled(PER[pipe][stage], first), (first + self.u * PER[pipe][stage]) % 2


def layers_kernel(nc, I, out, stages=8):
    ctx = ExitStack()
    with ctx:
        def sb(name, shape, dt=F32):
            return ctx.enter_context(nc.sbuf_tensor(name, shape, dt))

        def sem(name):
            return ctx.enter_context(nc.semaphore(name))

        x = sb("x", [P, NT * D])
        xn = sb("xn", [P, TB * D])
        xnT = sb("xnT", [P, 2, KD, S])
        ctxT = sb("ctxT", [P, KD, NC_])
        ctxnT = sb("ctxnT", [P, KD, NC_])
        mask = sb("mask", [P, NT, C], U8)
        work = sb("work", [P, 4096])
        area1 = sb("area1", [P, 16384])
        area2 = sb("area2", [P, 12288])
        area3 = sb("area3", [P, 9216])
        ident = sb("ident", [P, P])
        identb = sb("identb", [P, P], BF16)
        ones = sb("ones", [P, P])
        triu = sb("triu", [P, P], BF16)
        onesb = sb("onesb", [P, P], BF16)
        iota8 = sb("iota8", [P, NE])
        bo0 = sb("bo0", [P, D])
        bv1 = sb("bv1", [P, D])
        bfc2 = sb("bfc2", [P, D])
        be2 = sb("be2", [P, D])
        bo3 = sb("bo3", [P, D])
        lb1 = sb("lb1", [P, NE])
        gates = sb("gates", [P, 8])
        clips = sb("clips", [P, 2])
        cols = sb("cols", [P, 16])
        cols2 = sb("cols2", [P, 8])
        rowm = sb("rowm", [P, NT], I32)
        rowf = sb("rowf", [P, NT])
        gw = sb("gw", [P, 3, KD, NE + 1])
        stats = sb("stats", [P, TB, 6])
        mv = sb("mv", [P, NT, 2])
        mvb = sb("mvb", [P, TB, 2])
        var = sb("var", [P, NT])
        rstd = sb("rstd", [P, NT])
        minush = sb("minush", [P, NT])
        lat = sb("lat", [P, NT])
        mx = sb("mx", [P, 2, H])
        sm = sb("sm", [P, 2, H])
        rsm = sb("rsm", [P, 2, H])
        nmx = sb("nmx", [P, TB])
        lg = sb("lg", [P, TB, NE + 1])
        lb = sb("lb", [P, TB, NE])
        v8 = sb("v8", [P, TB, NE])
        i8 = sb("i8", [P, TB, NE], U32)
        i8f = sb("i8f", [P, TB, 2])
        oh = sb("oh", [P, TB, NE])
        oh2 = sb("oh2", [P, TB, NE])
        ohb = sb("ohb", [P, TB, NE], BF16)
        th = sb("th", [P, TB, NE + 1])
        ws = sb("ws", [P, TB, NE])
        sr = sb("sr", [P, 4, TB])
        wE = sb("wE", [P, TB, NE + 1])
        cnt = sb("cnt", [P, 2 * TB * NE])
        base = sb("base", [P, TB + 1, NE])
        qs = sb("qs", [P, 16])
        qw = sb("qw", [P, 4, NFQ])
        qd = sb("qd", [P, 4, KD])

        pt = [ctx.enter_context(nc.psum_tensor(f"pt{i}", [P, 512], F32)) for i in range(2)]
        sh = [ctx.enter_context(nc.psum_tensor(f"sh{i}", [P, 1024], F32)) for i in range(2)]
        ob = [ctx.enter_context(nc.psum_tensor(f"ob{i}", [P, 512], F32)) for i in range(2)]

        xin = work[:, 0:2 * D]
        prob = [work[:, i * 1024:(i + 1) * 1024] for i in range(2)]
        probT = work[:, 2048:3072]
        act_r = [work[:, i * 1024:(i + 1) * 1024] for i in range(2)]
        hid = [work[:, 2048 + i * 1024:3072 + i * 1024] for i in range(2)]
        hq = [work[:, i * 2048:i * 2048 + NFQ * S // 2].bitcast(BF16) for i in range(2)]
        keysA = area1[:, 0:8192]
        valsO = area1[:, 8192:16384]
        wq16, wk16, wv16, wo16 = (area2[:, i * 2048:(i + 1) * 2048] for i in range(4))
        kT16, vT16 = (area2[:, 8192 + i * 2048:10240 + i * 2048] for i in range(2))
        wqT16 = work[:, 2048:4096]
        xn_all = area1[:, 0:4096]
        hall = area1[:, 4096:16384].rearrange("p (f t) -> p f t", f=NFQ)
        qnat = area3[:, 0:NFQ * D * 2 + KD * FQ]
        qint = area3[:, 4608:6912].bitcast(BF16)
        wgT = area3[:, 0:NFQ * P].bitcast(BF16).rearrange("p (k f) -> p k f", k=KD)
        wuT = area3[:, NFQ * P:2 * NFQ * P].bitcast(BF16).rearrange("p (k f) -> p k f", k=KD)
        wdT = area3[:, 2 * NFQ * P:3 * NFQ * P].bitcast(BF16).rearrange("p (f d) -> p f d", f=NFQ)
        sdb = area3[:, 2304:2560]
        xqT = area3[:, 6912:8960].bitcast(BF16).rearrange("p (k t) -> p k t", k=KD)
        xqi = work[:, 0:2048].bitcast(BF16)
        w1h = [area2[:, 8192 + i * 512:8704 + i * 512] for i in range(7)]
        small = area1[:, 0:8192]
        nat1, nat2 = area2[:, 0:4096], area2[:, 4096:8192]
        natc = area1[:, 8192:9216]
        w1T, w2T, cT = area3[:, 0:4096], area3[:, 4096:8192], area3[:, 8192:9216]
        lgT = area1[0:NE + 1, 9216:9216 + S]
        wexp = area1[:, 10240:10752]
        gup, down = area2[:, 0:1024], area2[:, 1024:1536]

        in_ctx, in_x, in_small, in_w0, in_wq, in_n, in_c, in_wexp, in_w6, in_w7, in_s7 = map(
            sem, "in_ctx in_x in_small in_w0 in_wq in_n in_c in_wexp in_w6 in_w7 in_s7".split())
        const_made = sem("const_made")
        pool_step = sem("pool_step")
        gates_ready = sem("gates_ready")
        pt_full, pt_moved = sem("pt_full"), sem("pt_moved")
        sh_full, sh_taken, sh_half = sem("sh_full"), sem("sh_taken"), sem("sh_half")
        o_full, o_added = sem("o_full"), sem("o_added")
        ln_var, ln_rstd, ln_done = sem("ln_var"), sem("ln_rstd"), sem("ln_done")
        c_var, c_rstd, c_done = sem("c_var"), sem("c_rstd"), sem("c_done")
        shifted = [sem(f"shifted{s}") for s in range(8)]
        exped = [sem(f"exped{s}") for s in range(8)]
        prob_ready = [sem(f"prob_ready{s}") for s in range(8)]
        act_done = [sem(f"act_done{s}") for s in range(8)]
        router_in, router_act = sem("router_in"), sem("router_act")
        hot_ready = sem("hot_ready")
        stored = sem("stored")
        q_inv, q_int, x_int, q_diag, q_amax, q_top, q_clip, hq_ready = map(
            sem, "q_inv q_int x_int q_diag q_amax q_top q_clip hq_ready".split())
        w16_used = sem("w16_used")

        def xt(b, j):
            return x[:, bass.ds(b.scaled(TB * D, j * D), D)]

        block = ctx.enter_context(nc.Block())
        straight = [Block(u) for u in range(NB)]

        def blocks_of(eng, body):
            with eng.Fori(0, NB // 2) as i:
                for u in range(2):
                    body(Block(u, i))

        @block.sync
        def _(sp):
            def load(dst, src, s):
                sp.dma_start(dst, src).then_inc(s, 16)

            def load_columns(dst, src, s):
                sp.dma_start(dst, src, allow_slow_non_contiguous=True).then_inc(s, 16)

            def rows(w, k=KD):
                return w.rearrange("(k p) n -> p k n", p=P)

            def as3(a, k=KD):
                return a.rearrange("p (k n) -> p k n", k=k)

            load(as3(xin), I["ctx_1024"].rearrange("b c d -> (b c) d").rearrange("(t p) d -> p t d", p=P), in_ctx)
            load_columns(cols2[:, 0:2], I["L3_xattn_ln_c_w"].rearrange("(k p) -> p k", p=P), in_ctx)
            load_columns(cols2[:, 2:4], I["L3_xattn_ln_c_b"].rearrange("(k p) -> p k", p=P), in_ctx)
            load(as3(wk16), rows(I["L0_xattn_Wk"]), in_w0)
            load(as3(wq16), rows(I["L0_xattn_Wq"]), in_wq)
            load(as3(wv16), rows(I["L0_xattn_Wv"]), in_w0)
            load(as3(wo16, MI), rows(I["L0_xattn_Wo"]), in_w0)
            load(x[:, :].rearrange("p (t d) -> p t d", t=NT),
                 I["x"].rearrange("b (t p) d -> p (b t) d", p=P), in_x)
            for j, n in enumerate(["L1_xattn_bq", "L1_xattn_bk", "L2_xattn_bq", "L2_xattn_bk", "L2_xattn_bv",
                                   "L3_xattn_ln_l_w", "L3_xattn_ln_l_b"]):
                load_columns(cols[:, 2 * j:2 * j + 2], I[n].rearrange("(k p) -> p k", p=P), in_small)
            for t, n in ((bo0, "L0_xattn_bo"), (bv1, "L1_xattn_bv"), (bfc2, "L2_xattn_bfc"), (be2, "L2_ffn_b_expert"),
                         (bo3, "L3_xattn_bo"), (lb1, "L1_ffn_lb_bias")):
                load(t[:, :], I[n].partition_broadcast(P), in_small)
            load(gates[:, 0:4], I["g_xattn"].partition_broadcast(P), in_small)
            load(gates[:, 4:8], I["g_ffn"].partition_broadcast(P), in_small)
            load(clips[:, 0:1], I["L0_ffn_clip_x"].partition_broadcast(P), in_small)
            load(clips[:, 1:2], I["L0_ffn_clip_down"].partition_broadcast(P), in_small)
            load(mask[:, :, :], I["mask_BxSxS2_bk1"].rearrange("b (t p) c -> p (b t) c", p=P), in_small)
            load_columns(rowm[:, :], I["mask_BxS_ik1"].rearrange("b (t p) -> p (b t)", p=P), in_small)
            for k in range(KD):
                load_columns(gw[:, 0, k, 0:NE], I["L1_ffn_gate_w"][:, k * P:(k + 1) * P].rearrange("e p -> p e"), in_small)
            load(gw[:, 1, :, 0:NE], rows(I["L2_ffn_w_gate"]), in_small)
            load(gw[:, 2, :, 0:NE], rows(I["L3_ffn_router_w"]), in_small)
            load_columns(gw[:, 2, :, NE:NE + 1], rows(I["L3_ffn_shared_gate_w"]), in_small)
            for w, n in ((0, "L0_ffn_w_gate"), (1, "L0_ffn_w_up")):
                a = qnat[:, w * NFQ * D:(w + 1) * NFQ * D].rearrange("p (c n) -> p c n", c=NFQ)
                load(a[:, 0:NFQ - 1, :], rows(I[n][0:(NFQ - 1) * P, :]), in_n)
                load(a[0:RFQ, NFQ - 1, :], I[n][(NFQ - 1) * P:FQ, :], in_n)
            load(as3(qnat[:, 2 * NFQ * D:2 * NFQ * D + KD * FQ]), rows(I["L0_ffn_w_down"]), in_n)
            if stages > 1:
                sp.wait_ge(sh_taken, start_of("sh", 0) + PRE["sh"][0])
                for a, n in zip(w1h, ("L1_xattn_Wq", "L1_xattn_Wk", "L1_xattn_Wv", "L2_xattn_Wq", "L2_xattn_Wk",
                                      "L2_xattn_Wv", "L2_xattn_Wfc")):
                    load(as3(a), rows(I[n]), in_c)
                load(nat1.rearrange("p (e n) -> p e n", e=2 * NE), rows(I["L1_ffn_w1"].rearrange("e h d -> (e h) d")), in_c)
                load(nat2.rearrange("p (e n) -> p e n", e=2 * NE), rows(I["L1_ffn_w2"].rearrange("e h d -> (e h) d")), in_c)
            if stages > 2:
                sp.wait_ge(o_added, start_of("o", 2))
                load(as3(natc[:, 0:512]), rows(I["L1_ffn_cfc"]), in_wexp)
                load(as3(natc[:, 512:1024]), rows(I["L1_ffn_cproj"]), in_wexp)
                load(as3(wexp), rows(I["L2_ffn_w_expert"]), in_wexp)
            if stages > 4:
                sp.wait_ge(pt_moved, start_of("pt", 3) + PRE["pt"][3])
                for a, n in ((wq16, I["L3_xattn_Wq"]), (wk16, I["L3_xattn_Wkv"][:, 0:INNER]),
                             (wv16, I["L3_xattn_Wkv"][:, INNER:2 * INNER])):
                    load(as3(a), rows(n), in_w6)
                load(as3(wo16, MI), rows(I["L3_xattn_Wo"]), in_w6)
            if stages > 5:
                sp.wait_ge(o_added, start_of("o", 4))
                load(w1T.rearrange("p (e n) -> p e n", e=2 * NE), rows(I["L3_ffn_w1"].rearrange("e d f -> (e d) f")), in_w7)
                load(w2T.rearrange("p (e n) -> p e n", e=2 * NE), rows(I["L3_ffn_w2"].rearrange("e f d -> (e f) d")), in_w7)
            if stages > 7:
                sp.wait_ge(sh_taken, start_of("sh", 6) + PRE["sh"][6])
                load(as3(gup), rows(I["L3_ffn_shared_gate_up"]), in_s7)
                load(as3(down), rows(I["L3_ffn_shared_down"]), in_s7)
            for b in range(NB):
                sp.wait_ge(o_added, start_of("o", stages - 1) + (b + 1) * PER["o"][stages - 1])
                sp.dma_start(out[b].rearrange("(t p) d -> p t d", p=P),
                             x[:, b * TB * D:(b + 1) * TB * D].rearrange("p (t d) -> p t d", t=TB)).then_inc(stored, 16)
            sp.wait_ge(stored, 16 * NB)

        @block.gpsimd
        def _(pool):
            def ones_where(t, compare, pattern, mult, fill, start):
                pool.memset(t, start).then_inc(pool_step, 1)
                ones_where.n += 1
                pool.wait_ge(pool_step, ones_where.n)
                pool.affine_select(out=t, in_=t, compare_op=compare, fill=fill, base=0,
                                   pattern=pattern, channel_multiplier=mult).then_inc(const_made, 1)
            ones_where.n = 0
            ones_where(ident[:, :], ALU.not_equal, [[-1, P]], 1, 1.0, 0.0)
            pool.memset(minush[:, :], -0.5).then_inc(const_made, 1)
            ones_where(identb[:, :], ALU.not_equal, [[-1, P]], 1, 1.0, 0.0)
            ones_where(triu[:, :], ALU.is_ge, [[1, P]], -1, 0.0, 1.0)
            pool.memset(ones[:, :], 1.0).then_inc(const_made, 1)
            pool.memset(onesb[:, :], 1.0).then_inc(const_made, 1)
            pool.iota(iota8[:, :], pattern=[[1, NE]], base=0, channel_multiplier=0,
                      allow_small_or_imprecise_dtypes=True).then_inc(const_made, 1)

            def rsqrt(n, given):
                pool.tensor_tensor(rstd[:, n], var[:, n], minush[:, n], ALU.pow).then_inc(given, 1)

            pool.wait_ge(const_made, 7)
            pool.wait_ge(c_var, 1)
            rsqrt(slice(0, 2), c_rstd)

            def block_rstd(t, b):
                pool.wait_ge(ln_var, t + 1)
                rsqrt(slice(b * TB, (b + 1) * TB), ln_rstd)

            for b in range(NB):
                block_rstd(b, b)
            pool.wait_ge(q_inv, 1)
            pool.wait_ge(in_n, 16 * 5)

            def to_int(a, o, inv):
                pool.tensor_scalar(a, a, inv, QMAX, ALU.mult, ALU.min)
                pool.drain()
                pool.tensor_scalar(a, a, -QMAX - 1.0, MAGIC, ALU.max, ALU.add)
                pool.drain()
                pool.tensor_scalar(o, a, MAGIC, None, ALU.subtract).then_inc(q_int, 1)
            after = {0: range(0, 8), 1: range(8, 10), 2: range(10, 12), 3: range(12, 14)}
            for b in range(NB):
                for c in after[b]:
                    if c < 2 * NFQ:
                        r = RFQ if c % NFQ == NFQ - 1 else P
                        to_int(qnat[0:r, c * D:(c + 1) * D], qint[0:r, c * D:(c + 1) * D],
                               qw[0:r, 1 + 2 * (c // NFQ), c % NFQ:c % NFQ + 1])
                    else:
                        k, o = c - 2 * NFQ, 2 * NFQ * D + (c - 2 * NFQ) * FQ
                        to_int(qnat[:, o:o + FQ], qint[:, o:o + FQ], qd[:, 1, k:k + 1])
                block_rstd(NB + b, b)
            if stages > 1:
                for k in range(2):
                    pool.wait_ge(q_amax, k + 1)
                    pool.partition_all_reduce(qs[:, k + 2:k + 3], qs[:, k:k + 1], P, RMAX).then_inc(q_top, 1)
                with pool.Fori(2, min(6, stages + 1)) as s:
                    for b in range(NB):
                        block_rstd(s * NB + b, b)
            if stages > 5:
                for b in range(NB):
                    n = slice(b * TB, (b + 1) * TB)
                    pool.wait_ge(ln_var, 6 * NB + b + 1)
                    pool.tensor_tensor(rstd[:, n], var[:, n], minush[:, n], ALU.pow)
                    pool.drain()
                    pool.tensor_tensor(lat[:, n], rstd[:, n], rstd[:, n], ALU.mult)
                    pool.drain()
                    pool.tensor_tensor(lat[:, n], lat[:, n], mv[:, n, 1], ALU.mult)
                    pool.drain()
                    pool.tensor_scalar(lat[:, n], lat[:, n], EPS, None, ALU.add)
                    pool.drain()
                    pool.tensor_tensor(lat[:, n], lat[:, n], minush[:, n], ALU.pow)
                    pool.drain()
                    pool.tensor_tensor(rstd[:, n], rstd[:, n], lat[:, n], ALU.mult).then_inc(ln_rstd, 1)
            if stages > 6:
                with pool.Fori(7, stages + 1) as s:
                    for b in range(NB):
                        block_rstd(s * NB + b, b)

        @block.tensor
        def _(pe):
            def pt_slot(n):
                if not isinstance(n, int) or n >= 2:
                    pe.wait_ge(pt_moved, n - 1)

            def sh_slot(n):
                if not isinstance(n, int) or n >= 2:
                    pe.wait_ge(sh_taken, n - 1)

            def o_slot(n):
                if not isinstance(n, int) or n >= 2:
                    pe.wait_ge(o_added, n - 1)

            def transposes(n, slot, pieces, idn=None, cast=None, waited=False):
                if not waited:
                    pt_slot(n)
                for (r, c0, c1), src in pieces:
                    dst = pt[slot][:, :] if cast is None else pt[slot][:, :].bitcast(cast)
                    mm = pe.transpose(dst[0:r, c0:c1], src, (idn or ident)[0:src.shape[0], 0:src.shape[0]])
                mm.then_inc(pt_full, 1)

            def norm_T(stage, b, k0):
                pe.wait_ge(ln_done, b.fill("ln", stage)[0] + 1)
                for k in range(KD):
                    n, slot = b.fill("pt", stage, k0 + k)
                    transposes(n, slot, [((P, j * P, (j + 1) * P), xn[:, j * D + k * P:j * D + (k + 1) * P])
                                         for j in range(TB)])

            def first_norm_T(n0, count):
                pe.wait_ge(ln_done, count)
                for k in range(KD):
                    transposes(n0 + k, (n0 + k) % 2,
                               [((P, j * P, (j + 1) * P), xn[:, j * D + k * P:j * D + (k + 1) * P]) for j in range(TB)])

            def T(stage, b):
                return xnT[:, (b.fill("ln", stage)[1] + 1) % 2]

            def wait_T(stage, u, k):
                if u == 0:
                    return
                pe.wait_ge(pt_moved, Block(u - 1).fill("pt", stage, k)[0] + 1)

            def product(o, lhs, rhs):
                for k, (a, b) in enumerate(zip(lhs, rhs)):
                    mm = pe.matmul(o, a, b, start=(k == 0), stop=(k == len(lhs) - 1))
                return mm

            def fold16(stage, cT_, in_kv, in_q, n_kv, n_q):
                n0 = start_of("sh", stage)
                n = n0
                pe.wait_ge(in_kv, n_kv)
                for w in (wk16, wv16):
                    for half in range(2):
                        sh_slot(n)
                        for q in range(4):
                            m = 4 * half + q
                            mm = product(sh[n % 2][:, q * NC_:(q + 1) * NC_],
                                         [w[:, k * INNER + m * P:k * INNER + (m + 1) * P] for k in range(KD)],
                                         [cT_[:, k, :] for k in range(KD)])
                        mm.then_inc(sh_full, 1)
                        n += 1
                pe.wait_ge(in_q, n_q)
                p0 = start_of("pt", stage) + PRE["pt"][stage] - 4
                for f in range(4):
                    transposes(p0 + f, (p0 + f) % 2,
                               [((P, q * P, (q + 1) * P),
                                 wq16[:, (q % 2) * INNER + (2 * f + q // 2) * P:(q % 2) * INNER + (2 * f + q // 2 + 1) * P])
                                for q in range(4)])
                pe.wait_ge(pt_moved, p0 + 4)
                pe.wait_ge(sh_taken, n0 + 4)
                for m in range(MI):
                    sh_slot(n)
                    for k in range(KD):
                        for j in range(2):
                            r = slice(64 * j, 64 * j + 64)
                            mm = pe.matmul(sh[n % 2][:, j * 512 + k * NC_:j * 512 + (k + 1) * NC_],
                                           wqT16[r, m * D + k * P:m * D + (k + 1) * P],
                                           kT16[r, m * NC_:(m + 1) * NC_], start=True, stop=True)
                    mm.then_inc(sh_full, 1)
                    n += 1
                for m in range(MI):
                    for bp in range(2):
                        sh_slot(n)
                        for q in range(2):
                            b = 2 * bp + q
                            for j in range(2):
                                r = slice(64 * j, 64 * j + 64)
                                mm = pe.matmul(sh[n % 2][r, j * 512 + q * D:j * 512 + (q + 1) * D],
                                               vT16[r, m * NC_ + b * C:m * NC_ + (b + 1) * C],
                                               wo16[r, m * D:(m + 1) * D], start=True, stop=True)
                        mm.then_inc(sh_full, 1)
                        n += 1

            def attend16(stage):
                def scores(u, j):
                    n, slot = Block(u).fill("sh", stage, j)
                    sh_slot(n)
                    for c in range(2):
                        mm = product(sh[slot][:, c * 512:(c + 1) * 512],
                                     [T(stage, Block(u))[:, k, j * P:(j + 1) * P] for k in range(KD)],
                                     [keysA[:, (k * NB + u) * H * C + c * 512:(k * NB + u) * H * C + (c + 1) * 512]
                                      for k in range(KD)])
                    mm.then_inc(sh_full, 1)

                pe.wait_ge(sh_taken, start_of("sh", stage) + PRE["sh"][stage])
                scores(0, 0)
                scores(0, 1)
                for b in straight:
                    for j in range(TB):
                        next_norm = stage == 6 or b.u + 1 < NB
                        k0 = 2 * j if j < 2 or not next_norm else 2 * j + 2
                        pe.wait_ge(prob_ready[stage], b.u * TB + j + 1)
                        for half in range(2):
                            n, slot = b.fill("pt", stage, k0 + half)
                            transposes(n, slot, [((P, q * P, (q + 1) * P),
                                                  prob[j % 2][:, (4 * half + q) * P:(4 * half + q + 1) * P]) for q in range(4)])
                        if j == 1 and next_norm:
                            norm_T(stage, b, 4)
                        if j < 2:
                            scores(b.u, j + 2)
                        elif b.u + 1 < NB:
                            wait_T(stage, b.u + 1, 5)
                            scores(b.u + 1, j - 2)
                        n, slot = b.fill("o", stage, j)
                        o_slot(n)
                        pe.wait_ge(pt_moved, b.fill("pt", stage, k0 + 1)[0] + 1)
                        product(ob[slot][:, 0:D], [probT[:, m * P:(m + 1) * P] for m in range(MI)],
                                [valsO[:, (m * NB + b.u) * D:(m * NB + b.u + 1) * D] for m in range(MI)]
                                ).then_inc(o_full, 1)

            def attend1(stage):
                A, Vf = small[:, 1024:1536], small[:, 2048:3072]

                def scores(b):
                    n, slot = b.fill("sh", stage)
                    sh_slot(n)
                    for j in range(TB):
                        mm = product(sh[slot][:, j * C:(j + 1) * C],
                                     [T(stage, b)[:, k, j * P:(j + 1) * P] for k in range(KD)],
                                     [A[:, k * NC_ + b.u * C:k * NC_ + (b.u + 1) * C] for k in range(KD)])
                    mm.then_inc(sh_full, 1)

                pe.wait_ge(sh_taken, start_of("sh", stage) + PRE["sh"][stage])
                pe.wait_ge(pt_moved, start_of("pt", stage))
                scores(straight[0])
                for b in straight:
                    norm_T(stage, b, 0)
                    pe.wait_ge(prob_ready[stage], b.u + 1)
                    n, slot = b.fill("pt", stage, 2)
                    transposes(n, slot, [((C, j * P, (j + 1) * P), prob[b.u % 2][:, j * C:(j + 1) * C]) for j in range(TB)])
                    if b.u + 1 < NB:
                        wait_T(stage, b.u + 1, 1)
                        scores(straight[b.u + 1])
                    pe.wait_ge(pt_moved, n + 1)
                    for pair in range(2):
                        m, oslot = b.fill("o", stage, pair)
                        o_slot(m)
                        for q in range(2):
                            j = 2 * pair + q
                            mm = pe.matmul(ob[oslot][:, q * D:(q + 1) * D],
                                           probT[0:C, (b.u % 2) * S + j * P:(b.u % 2) * S + (j + 1) * P],
                                           Vf[0:C, b.u * D:(b.u + 1) * D], start=True, stop=True)
                        mm.then_inc(o_full, 1)

            def weight_T(n, src):
                transposes(n, n % 2, [((P, k * D + e * P, k * D + (e + 1) * P), src[:, e * D + k * P:e * D + (k + 1) * P])
                                      for k in range(KD) for e in range(KD)])

            def chunks(w, m=None):
                return [w[:, k * D:(k + 1) * D] if m is None else w[:, k * D + m * P:k * D + (m + 1) * P] for k in range(KD)]

            def fold1(stage, wq, wk, wv, fc=None):
                n = start_of("sh", stage)
                cc = [ctxT[:, k, :] for k in range(KD)]
                kT, A, Vt = small[:, 0:512], small[:, 1024:1536], small[:, 3072:3584]
                sh_slot(n)
                for m in range(KD):
                    mm = product(sh[n % 2][:, m * NC_:(m + 1) * NC_], chunks(wk, m), cc)
                if fc is not None:
                    for m in range(KD):
                        mm = product(sh[n % 2][:, 512 + m * NC_:512 + (m + 1) * NC_], chunks(wv, m), cc)
                mm.then_inc(sh_full, 1)
                sh_slot(n + 1)
                if fc is not None:
                    pe.wait_ge(sh_taken, n + 1)
                for b in range(NB):
                    lhs = ([ctxT[:, k, b * C:(b + 1) * C] for k in range(KD)] if fc is None else
                           [Vt[:, k * NC_ + b * C:k * NC_ + (b + 1) * C] for k in range(KD)])
                    mm = product(sh[(n + 1) % 2][0:C, b * D:(b + 1) * D], lhs, chunks(wv if fc is None else fc))
                mm.then_inc(sh_full, 1)
                pe.wait_ge(sh_taken, n + 1)
                sh_slot(n + 2)
                for m in range(KD):
                    mm = product(sh[n % 2][:, m * NC_:(m + 1) * NC_], chunks(wq, m),
                                 [kT[:, k * NC_:(k + 1) * NC_] for k in range(KD)])
                mm = product(sh[n % 2][:, 512:512 + NC_], [small[:, 7168 + k * P:7168 + (k + 1) * P] for k in range(KD)],
                             [kT[:, k * NC_:(k + 1) * NC_] for k in range(KD)])
                mm.then_inc(sh_full, 1)

            def logits(stage, b, r, k0, width):
                n, slot = b.fill("pt", stage, k0)
                pt_slot(n)
                product(pt[slot][0:width, :], [gw[:, r, k, 0:width] for k in range(KD)],
                        [T(stage, b)[:, k, :] for k in range(KD)]).then_inc(pt_full, 1)

            def logits_moved(stage, b, k0):
                pe.wait_ge(pt_moved, b.fill("pt", stage, k0)[0] + 1)

            def logits_T(stage, b, k0, width):
                n, slot = b.fill("pt", stage, k0)
                transposes(n, slot, [((P, j * width, (j + 1) * width), lgT[0:width, j * P:(j + 1) * P]) for j in range(TB)], waited=True)

            def experts(stage, r, width, pieces):
                def up(b, e, between=None):
                    n, slot = b.fill("sh", stage, e)
                    sh_slot(n)
                    for f in range(2):
                        if f == 1 and between:
                            between()
                        if e < NE:
                            lhs = [w1T[:, (2 * e + k) * D + f * P:(2 * e + k) * D + (f + 1) * P] for k in range(KD)] \
                                if stage == 7 else [w1T[:, k * NE * D + e * D + f * P:k * NE * D + e * D + (f + 1) * P] for k in range(KD)]
                        elif stage == 3:
                            lhs = [cT[:, k * D + f * P:k * D + (f + 1) * P] for k in range(KD)]
                        else:
                            lhs = [gup[:, k * 2 * D + f * D + (e - NE) * P:k * 2 * D + f * D + (e - NE + 1) * P] for k in range(KD)]
                        mm = product(sh[slot][:, f * S:(f + 1) * S], lhs, [T(stage, b)[:, k, :] for k in range(KD)])
                    mm.then_inc(sh_full, 1)

                def back(b, e, last_piece):
                    pe.wait_ge(sh_taken, b.fill("sh", stage, last_piece)[0] + 1)
                    for pair in range(2):
                        n, slot = b.fill("o", stage, 2 * e + pair)
                        o_slot(n)
                        for q in range(2):
                            j = 2 * pair + q
                            if e < NE:
                                rhs = [w2T[:, (2 * e + f) * D:(2 * e + f + 1) * D] for f in range(2)]
                            elif stage == 3:
                                rhs = [cT[:, 512 + f * D:512 + (f + 1) * D] for f in range(2)]
                            else:
                                rhs = [down[:, f * D:(f + 1) * D] for f in range(2)]
                            mm = product(ob[slot][:, q * D:(q + 1) * D],
                                         [hid[e % 2][:, f * S + j * P:f * S + (j + 1) * P] for f in range(2)], rhs)
                        mm.then_inc(o_full, 1)

                def body(b):
                    pe.wait_ge(pt_moved, b.fill("pt", stage, 0)[0])
                    up(b, 0)
                    logits(stage, b, r, 0, width)
                    up(b, 1, lambda: logits_moved(stage, b, 0))
                    logits_T(stage, b, 1, width)
                    for e in range(NE + 1):
                        if e == 4:
                            norm_T(stage, b, 2)
                        back(b, e, e if e < NE else pieces - 1)
                        if e + 2 < pieces:
                            up(b, e + 2)
                blocks_of(pe, body)

            pe.wait_ge(const_made, 7)
            pe.wait_ge(in_ctx, 48)
            transposes(0, 0, [((P, k * NC_ + t * P, k * NC_ + (t + 1) * P), xin[:, t * D + k * P:t * D + (k + 1) * P])
                              for k in range(KD) for t in range(2)])
            pe.wait_ge(c_done, 1)
            transposes(1, 1, [((P, k * NC_ + t * P, k * NC_ + (t + 1) * P), xn[:, t * D + k * P:t * D + (k + 1) * P])
                              for k in range(KD) for t in range(2)])
            pe.wait_ge(pt_moved, 1)
            first_norm_T(2, 1)
            fold16(0, ctxT, in_w0, in_wq, 48, 16)
            attend16(0)

            if stages > 1:
                n = start_of("pt", 1) - 2
                pe.wait_ge(q_int, 14)
                for w in range(2):
                    for k in range(KD):
                        transposes(n, n % 2,
                                   [((P, c * P, c * P + (RFQ if c == NFQ - 1 else P)),
                                     qint[0:(RFQ if c == NFQ - 1 else P), (w * NFQ + c) * D + k * P:(w * NFQ + c) * D + (k + 1) * P])
                                    for c in range(NFQ)], identb, BF16)
                        n += 1
                o = 2 * NFQ * D
                for cs in (range(0, 4), range(4, NFQ)):
                    transposes(n, n % 2,
                               [((RFQ if c == NFQ - 1 else P, (c - cs[0]) * D + h * P, (c - cs[0]) * D + (h + 1) * P),
                                 qint[:, o + h * FQ + c * P:o + h * FQ + min((c + 1) * P, FQ)])
                                for c in cs for h in range(KD)], identb, BF16)
                    n += 1
                pt_slot(n)
                pe.wait_ge(q_diag, 1)
                for h in range(KD):
                    mm = pe.matmul(pt[n % 2][:, h * P:(h + 1) * P], ones[:, :], xn[:, h * P:(h + 1) * P], start=True, stop=True)
                mm.then_inc(pt_full, 1)
                n += 1
                for b in range(NB):
                    pe.wait_ge(x_int, b + 1)
                    transposes(n, n % 2, [((P, k * S + j * P, k * S + (j + 1) * P),
                                           xqi[:, (b % 2) * 1024 + j * D + k * P:(b % 2) * 1024 + j * D + (k + 1) * P])
                                          for k in range(KD) for j in range(TB)], identb, BF16)
                    n += 1
                pe.wait_ge(pt_moved, n)

                def gate_up(b):
                    for f in range(NFQ):
                        n, slot = b.fill("sh", 1, f)
                        sh_slot(n)
                        for w, wT in ((0, wgT), (1, wuT)):
                            mm = product(sh[slot][:, w * S:(w + 1) * S], [wT[:, k, f * P:(f + 1) * P] for k in range(KD)],
                                         [xqT[:, k, bass.ds(b.scaled(S), S)] for k in range(KD)])
                        mm.then_inc(sh_full, 1)
                blocks_of(pe, gate_up)
                for b in straight:
                    pe.wait_ge(hq_ready, b.u + 1)
                    for pair in range(2):
                        n, slot = b.fill("o", 1, pair)
                        o_slot(n)
                        for q in range(2):
                            j = 2 * pair + q
                            for f in range(NFQ):
                                r = RFQ if f == NFQ - 1 else P
                                mm = pe.matmul(ob[slot][:, q * D:(q + 1) * D],
                                               hq[b.u % 2][0:r, f * S + j * P:f * S + (j + 1) * P],
                                               wdT[0:r, f, :], start=(f == 0), stop=(f == NFQ - 1))
                        mm.then_inc(o_full, 1)
                first_norm_T(start_of("pt", 2) - 2, start_of("ln", 2))
            if stages > 2:
                pe.wait_ge(in_c, 16 * 9)
                weight_T(start_of("pt", 2), w1h[0])
                pe.wait_ge(pt_moved, start_of("pt", 2) + 1)
                fold1(2, small[:, 4096:4608], w1h[1], w1h[2])
                attend1(2)
            if stages > 3:
                n = start_of("pt", 3)
                pe.wait_ge(in_wexp, 48)
                for nat, wide in ((nat1, 2 * NE), (nat2, 2 * NE), (natc, 4)):
                    for g in range(wide // 2):
                        weight_T(n, nat[:, g * 512:(g + 1) * 512])
                        n += 1
                pe.wait_ge(pt_moved, n)
                experts(3, 0, NE, NE + 1)
            if stages > 4:
                n = start_of("pt", 4)
                for q, w in enumerate((w1h[4], w1h[5], w1h[6])):
                    weight_T(n + q, w)
                pe.wait_ge(pt_moved, n + 3)
                fold1(4, w1h[3], small[:, 4096:4608], small[:, 4608:5120], small[:, 5120:5632])
                attend1(4)
            if stages > 5:
                def expert5(b):
                    pe.wait_ge(pt_moved, b.fill("pt", 5, 0)[0])
                    logits(5, b, 1, 0, NE)
                    for pair in range(2):
                        n, slot = b.fill("o", 5, pair)
                        o_slot(n)
                        for q in range(2):
                            j = 2 * pair + q
                            if j == 1:
                                logits_moved(5, b, 0)
                            mm = product(ob[slot][:, q * D:(q + 1) * D],
                                         [T(5, b)[:, k, j * P:(j + 1) * P] for k in range(KD)],
                                         [wexp[:, k * D:(k + 1) * D] for k in range(KD)])
                        mm.then_inc(o_full, 1)
                        if pair == 0:
                            logits_T(5, b, 1, NE)
                            norm_T(5, b, 2)
                    n, slot = b.fill("pt", 5, 4)
                    pe.wait_ge(hot_ready, b.scaled(1, 1))
                    pt_slot(n)
                    pe.matmul(pt[slot][:, 0:TB * NE], triu[:, :], ohb[:, :, :].rearrange("p j e -> p (j e)"), start=True, stop=True)
                    pe.matmul(pt[slot][:, TB * NE:2 * TB * NE], onesb[:, :], ohb[:, :, :].rearrange("p j e -> p (j e)"),
                              start=True, stop=True).then_inc(pt_full, 1)
                blocks_of(pe, expert5)
            if stages > 6:
                fold16(6, ctxnT, in_w6, in_w6, 64, 64)
                attend16(6)
            if stages > 7:
                pe.wait_ge(in_w7, 32)
                pe.wait_ge(in_s7, 32)
                experts(7, 2, NE + 1, NE + 2)

        @block.scalar
        def _(act):
            def full(n):
                act.wait_ge(pt_full, n + 1)

            def move(n, slot, dst, r=P, cols_=512, cast=None):
                full(n)
                src = pt[slot][:, :] if cast is None else pt[slot][:, :].bitcast(cast)
                act.copy(dst, src[0:r, 0:cols_]).then_inc(pt_moved, 1)

            def norm_move(stage, b, k0, to_stage=None):
                par = b.fill("ln", stage)[1]
                for k in range(KD):
                    n, slot = b.fill("pt", stage, k0 + k)
                    full(n)
                    if (to_stage or stage) == 6:
                        act.activation(xnT[:, par, k, :], pt[slot][:, :], ACT.Identity, bias=cols[:, 12 + k:13 + k],
                                       scale=cols[:, 10 + k:11 + k]).then_inc(pt_moved, 1)
                    else:
                        act.copy(xnT[:, par, k, :], pt[slot][:, :]).then_inc(pt_moved, 1)

            def first_norm_move(n0, par):
                for k in range(KD):
                    move(n0 + k, (n0 + k) % 2, xnT[:, par, k, :])

            def fold16(stage):
                n0 = start_of("sh", stage)
                for e in range(4):
                    act.wait_ge(sh_full, n0 + e + 1)
                    dst = (kT16 if e < 2 else vT16)[:, (e % 2) * 1024:(e % 2) * 1024 + 512]
                    act.activation(dst, sh[(n0 + e) % 2][:, 0:512], ACT.Copy,
                                   scale=DH ** -0.5 if e < 2 else 1.0).then_inc(sh_half, 1)
                p0 = start_of("pt", stage) + PRE["pt"][stage] - 4
                for f in range(4):
                    move(p0 + f, (p0 + f) % 2, wqT16[:, f * 512:(f + 1) * 512])
                for m in range(MI):
                    n = n0 + 4 + m
                    act.wait_ge(sh_full, n + 1)
                    act.copy(keysA.rearrange("p (kb h c) -> p kb h c", kb=KD * NB, h=H)[:, :, 2 * m, :],
                             sh[n % 2][:, 0:512].rearrange("p (kb c) -> p kb c", c=C)).then_inc(sh_half, 1)
                for q in range(2 * MI):
                    n = n0 + 12 + q
                    m, bp = q // 2, q % 2
                    act.wait_ge(sh_full, n + 1)
                    dst = valsO[0:64, (m * NB + 2 * bp) * D:(m * NB + 2 * bp + 2) * D]
                    if m == 0:
                        act.copy(dst, sh[n % 2][0:64, 0:512]).then_inc(sh_half, 1)
                    else:
                        act.activation(dst, sh[n % 2][0:64, 0:512], ACT.Identity, bias=0.0,
                                       scale=gates[0:64, stage // 2:stage // 2 + 1]).then_inc(sh_half, 1)

            def attend16(stage):
                def exps(i):
                    if stage == 0:
                        act.wait_ge(shifted[stage], i + 1)
                    else:
                        act.wait_ge(sh_taken, Block(i // TB).fill("sh", stage, i % TB)[0] + 1)
                    act.activation(prob[i % 2], prob[i % 2], ACT.Exp).then_inc(exped[stage], 1)
                exps(0)
                for b in straight:
                    for j in range(TB):
                        i = b.u * TB + j
                        if i + 1 < NT:
                            exps(i + 1)
                        next_norm = stage == 6 or b.u + 1 < NB
                        k0 = 2 * j if j < 2 or not next_norm else 2 * j + 2
                        for half in range(2):
                            n, slot = b.fill("pt", stage, k0 + half)
                            move(n, slot, probT[:, half * 512:(half + 1) * 512])
                        if j == 1 and next_norm:
                            norm_move(stage, b, 4, stage if b.u + 1 < NB else 7)

            def attend1(stage):
                for b in straight:
                    act.wait_ge(shifted[stage], b.u + 1)
                    act.activation(prob[b.u % 2][:, 0:TB * C], prob[b.u % 2][:, 0:TB * C], ACT.Exp).then_inc(exped[stage], 1)
                    norm_move(stage, b, 0)
                    n, slot = b.fill("pt", stage, 2)
                    move(n, slot, probT[0:C, (b.u % 2) * S:(b.u % 2) * S + S], r=C)

            def experts(stage, width, pieces):
                def lead(b, e):
                    n, slot = b.fill("sh", stage, e)
                    act.wait_ge(sh_full, n + 1)
                    for f in range(1 if e >= NE and stage == 7 else 2):
                        a = act.activation(act_r[e % 2][:, f * S:(f + 1) * S], sh[slot][:, f * S:(f + 1) * S],
                                           ACT.Relu if stage == 3 else ACT.Tanh, scale=1.0 if stage == 3 else 0.5)
                        a.then_inc(act_done[stage], 1)

                def body(b):
                    lead(b, 0)
                    n, slot = b.fill("pt", stage, 0)
                    move(n, slot, lgT[0:width, :], r=width)
                    lead(b, 1)
                    n, slot = b.fill("pt", stage, 1)
                    full(n)
                    act.copy(lg[:, :, 0:width], pt[slot][:, 0:TB * width].rearrange("p (j e) -> p j e", j=TB)).then_inc(pt_moved, 1)
                    if stage == 3:
                        act.drain()
                        act.activation(th[:, :, 0:NE], lg[:, :, 0:NE], ACT.Tanh, scale=0.5).then_inc(router_act, 1)
                    else:
                        act.wait_ge(router_in, b.scaled(1, 4 + 1))
                        act.activation(ws[:, :, :], ws[:, :, :], ACT.Exp).then_inc(router_act, 1)
                        act.activation(th[:, :, NE:NE + 1], lg[:, :, NE:NE + 1], ACT.Tanh, scale=0.5).then_inc(router_act, 1)
                    for e in range(2, pieces):
                        lead(b, e)
                        if e == 5:
                            norm_move(stage, b, 2)
                blocks_of(act, body)

            full(0)
            act.copy(ctxT[:, :, :].rearrange("p k c -> p (k c)"), pt[0][:, :]).then_inc(pt_moved, 1)
            act.wait_ge(in_ctx, 48)
            full(1)
            for k in range(KD):
                a = act.activation(ctxnT[:, k, :], pt[1][:, k * NC_:(k + 1) * NC_], ACT.Identity,
                                   bias=cols2[:, 2 + k:3 + k], scale=cols2[:, k:k + 1])
            a.then_inc(pt_moved, 1)
            first_norm_move(2, 0)
            act.wait_ge(in_small, 16 * 24)
            act.activation(gates[:, :], gates[:, :], ACT.Tanh)
            act.activation(clips[:, :], clips[:, :], ACT.Tanh, scale=0.5)
            act.drain()
            act.copy(qs[:, 14:16], clips[:, :]).then_inc(gates_ready, 1)
            fold16(0)
            attend16(0)
            if stages > 1:
                n = start_of("pt", 1) - 2
                for w, wT in ((0, wgT), (1, wuT)):
                    for k in range(KD):
                        move(n, n % 2, wT[:, k, 0:FQ], cols_=FQ, cast=BF16)
                        n += 1
                move(n, n % 2, wdT[:, 0:4, :].rearrange("p f d -> p (f d)"), cols_=4 * D, cast=BF16)
                n += 1
                full(n)
                act.copy(wdT[:, 4, :], pt[n % 2][:, :].bitcast(BF16)[:, 0:D])
                act.copy(wdT[0:RFQ, 5, :], pt[n % 2][:, :].bitcast(BF16)[0:RFQ, D:2 * D]).then_inc(pt_moved, 1)
                n += 1
                move(n, n % 2, sdb, cols_=D)
                n += 1
                for b in range(NB):
                    full(n)
                    act.copy(xqT[:, :, b * S:(b + 1) * S],
                             pt[n % 2][:, :].bitcast(BF16).rearrange("p (k t) -> p k t", k=KD)).then_inc(pt_moved, 1)
                    n += 1
                act.wait_ge(q_clip, 1)

                def gate_tanh(b):
                    for f in range(NFQ):
                        n, slot = b.fill("sh", 1, f)
                        r = RFQ if f == NFQ - 1 else P
                        act.wait_ge(sh_full, n + 1)
                        act.activation(act_r[f % 2][0:r, 0:S], sh[slot][0:r, 0:S], ACT.Tanh,
                                       scale=qw[0:r, 0, f:f + 1]).then_inc(act_done[1], 1)
                blocks_of(act, gate_tanh)
                first_norm_move(start_of("pt", 2) - 2, (start_of("ln", 2) - 1) % 2)
            if stages > 2:
                move(start_of("pt", 2), start_of("pt", 2) % 2, small[:, 4096:4608])
                attend1(2)
            if stages > 3:
                n = start_of("pt", 3)
                for g in range(NE):
                    full(n)
                    act.copy(w1T.rearrange("p (k n) -> p k n", k=KD)[:, :, g * D:(g + 1) * D],
                             pt[n % 2][:, :].rearrange("p (k n) -> p k n", k=KD)).then_inc(pt_moved, 1)
                    n += 1
                for g in range(NE):
                    move(n, n % 2, w2T[:, g * 512:(g + 1) * 512])
                    n += 1
                for g in range(2):
                    move(n, n % 2, cT[:, g * 512:(g + 1) * 512])
                    n += 1
                experts(3, NE, NE + 1)
            if stages > 4:
                for q in range(3):
                    n = start_of("pt", 4) + q
                    move(n, n % 2, small[:, 4096 + q * 512:4608 + q * 512])
                attend1(4)
            if stages > 5:
                for b in straight:
                    n, slot = b.fill("pt", 5, 0)
                    move(n, slot, lgT[0:NE, :], r=NE)
                    n, slot = b.fill("pt", 5, 1)
                    full(n)
                    act.copy(lg[:, :, 0:NE], pt[slot][:, 0:TB * NE].rearrange("p (j e) -> p j e", j=TB)).then_inc(pt_moved, 1)
                    act.wait_ge(router_in, b.u + 1)
                    act.activation(ws[:, :, :], ws[:, :, :], ACT.Exp).then_inc(router_act, 1)
                    norm_move(5, b, 2, 6 if b.u == NB - 1 else 5)
                    n, slot = b.fill("pt", 5, 4)
                    move(n, slot, cnt[:, :], cols_=2 * TB * NE)
            if stages > 6:
                fold16(6)
                attend16(6)
            if stages > 7:
                experts(7, NE + 1, NE + 2)

        @block.vector
        def _(dve):
            def tiles_of(b, t, k):
                return bass.ds(b.scaled(TB * k, t * k), k)

            def norm_stats(b, tile=None, tiles=TB, signal=None):
                dve.drain()
                for j in range(tiles):
                    dve.bn_stats(stats[:, j, :], tile(j) if tile else xt(b, j))
                dve.drain()
                for j in range(tiles):
                    dve.bn_aggr(mvb[:, j, :], stats[:, j, :])
                dve.drain()
                n = bass.ds(b.scaled(TB), tiles)
                dve.tensor_copy(mv[:, n, :], mvb[:, 0:tiles, :])
                dve.tensor_scalar(var[:, n], mvb[:, 0:tiles, 1], EPS, None, ALU.add).then_inc(signal or ln_var, 1)

            def apply_norm(dst, src, b, tiles):
                for j in range(tiles):
                    n = tiles_of(b, j, 1)
                    ins = dve.tensor_scalar(dst(j), src(j), mv[:, n, 0], rstd[:, n], ALU.subtract, ALU.mult)
                return ins

            def xn_tile(j):
                return xn[:, j * D:(j + 1) * D]

            class Wrapped:

                def __init__(self, b):
                    self.b = b

                def scaled(self, k, plus=0):
                    if self.b.i is None or self.b.u == 0:
                        return Block((self.b.u + 1) % NB, self.b.i).scaled(k, plus)
                    return self.b.i * (-2 * k) + (2 * k + plus)

            def norm_next(stage, b, free):
                nxt = Wrapped(b)
                dve.wait_ge(ln_rstd, b.scaled(1, stage * NB + 2))
                dve.wait_ge(pt_full, free)
                apply_norm(xn_tile, lambda j: x[:, tiles_of(nxt, j, D)], nxt, TB).then_inc(ln_done, 1)

            def xn_free(stage, b, k):
                per = PER["pt"][stage]
                if b.i is None and b.u == 0:
                    return start_of("pt", stage)
                return b.scaled(per, start_of("pt", stage) + PRE["pt"][stage] - per + k + 1)

            def add(b, stage, k, tiles, weight=None):
                n, slot = b.fill("o", stage, k)
                dve.wait_ge(o_full, n + 1)
                for q, j in enumerate(tiles):
                    o = ob[slot][:, q * D:(q + 1) * D]
                    if weight is None:
                        ins = dve.tensor_tensor(xt(b, j), o, xt(b, j), ALU.add)
                    else:
                        ins = dve.scalar_tensor_tensor(xt(b, j), o, weight(j), xt(b, j), ALU.mult, ALU.add)
                ins.then_inc(o_added, 1)

            def fold16(stage, bias):
                n0 = start_of("sh", stage)
                g = gates[:, stage // 2:stage // 2 + 1]
                half0 = 28 * (stage // 6)
                for e in range(4):
                    dve.wait_ge(sh_full, n0 + e + 1)
                    dve.wait_ge(sh_half, half0 + e + 1)
                    dst = (kT16 if e < 2 else vT16)[:, (e % 2) * 1024 + 512:(e % 2) * 1024 + 1024]
                    dve.tensor_scalar(dst, sh[(n0 + e) % 2][:, 512:1024], DH ** -0.5 if e < 2 else 1.0, None,
                                      ALU.mult).then_inc(sh_taken, 1)
                for m in range(MI):
                    n = n0 + 4 + m
                    dve.wait_ge(sh_full, n + 1)
                    dve.wait_ge(sh_half, half0 + 4 + m + 1)
                    dve.tensor_copy(keysA.rearrange("p (kb h c) -> p kb h c", kb=KD * NB, h=H)[:, :, 2 * m + 1, :],
                                    sh[n % 2][:, 512:1024].rearrange("p (kb c) -> p kb c", c=C)).then_inc(sh_taken, 1)
                for q in range(2 * MI):
                    n = n0 + 12 + q
                    m, bp = q // 2, q % 2
                    dve.wait_ge(sh_full, n + 1)
                    dve.wait_ge(sh_half, half0 + 12 + q + 1)
                    cols_ = slice((m * NB + 2 * bp) * D, (m * NB + 2 * bp + 2) * D)
                    if m == 0:
                        v = valsO[0:64, cols_].rearrange("p (b d) -> p b d", b=2)
                        dve.tensor_tensor(v, v, bias[0:64, :].unsqueeze(1).broadcast_to([64, 2, D]), ALU.add)
                        dve.drain()
                        dve.tensor_scalar(valsO[0:64, cols_], valsO[0:64, cols_], g[0:64, :], None, ALU.mult)
                    dve.tensor_scalar(valsO[64:128, cols_], sh[n % 2][64:128, 512:1024], g[64:128, :], None,
                                      ALU.mult).then_inc(sh_taken, 1)

            def heads(a):
                return a.rearrange("p (h c) -> p h c", h=H)

            def over_keys(a, n=H):
                return a.unsqueeze(2).broadcast_to([P, n, C])

            def attend16(stage):
                def shift(i):
                    b, j = Block(i // TB), i % TB
                    n, slot = b.fill("sh", stage, j)
                    dve.wait_ge(sh_full, n + 1)
                    p = prob[i % 2]
                    if stage == 0:
                        dve.scalar_tensor_tensor(heads(p), mask[:, i, :].unsqueeze(1).broadcast_to([P, H, C]), -FMAX,
                                                 heads(sh[slot][:, :]), ALU.mult, ALU.add).then_inc(sh_taken, 1)
                        dve.drain()
                        dve.tensor_reduce(mx[:, i % 2, :], heads(p), AX.X, ALU.max)
                        dve.drain()
                        dve.tensor_tensor(heads(p), heads(p), over_keys(mx[:, i % 2, :]), ALU.subtract).then_inc(shifted[stage], 1)
                    else:
                        dve.tensor_scalar(p, sh[slot][:, :], -11.0, 11.0, ALU.max, ALU.min).then_inc(sh_taken, 1)

                def normalise(i):
                    p = prob[i % 2]
                    dve.wait_ge(exped[stage], i + 1)
                    dve.tensor_reduce(sm[:, i % 2, :], heads(p), AX.X, ALU.add)
                    dve.drain()
                    dve.reciprocal(rsm[:, i % 2, :], sm[:, i % 2, :])
                    dve.drain()
                    dve.tensor_tensor(heads(p), heads(p), over_keys(rsm[:, i % 2, :]), ALU.mult).then_inc(prob_ready[stage], 1)

                shift(0)
                normalise(0)
                for b in straight:
                    for j in range(TB):
                        i = b.u * TB + j
                        if i + 1 < NT:
                            shift(i + 1)
                        if i >= 1:
                            pb, pj = Block((i - 1) // TB), (i - 1) % TB
                            add(pb, stage, pj, [pj])
                            if pj == TB - 1:
                                norm_stats(pb)
                        if i + 1 < NT:
                            normalise(i + 1)
                        if j == 0 and (stage == 6 or b.u + 1 < NB):
                            norm_next(stage, b, xn_free(stage, b, 5))
                add(straight[-1], stage, TB - 1, [TB - 1])
                norm_stats(straight[-1])

            def attend1(stage):
                def shift(b):
                    n, slot = b.fill("sh", stage)
                    dve.wait_ge(sh_full, n + 1)
                    p = prob[b.u % 2][:, 0:TB * C].rearrange("p (j c) -> p j c", j=TB)
                    m = mx[:, b.u % 2, 0:TB]
                    cb = small[:, 1536 + b.u * C:1536 + (b.u + 1) * C]
                    dve.tensor_tensor(p, sh[slot][:, 0:TB * C].rearrange("p (j c) -> p j c", j=TB),
                                      cb.unsqueeze(1).broadcast_to([P, TB, C]), ALU.add).then_inc(sh_taken, 1)
                    if stage == 4:
                        dve.drain()
                        r = rowf[:, b.u * TB:(b.u + 1) * TB]
                        dve.tensor_tensor(p, p, over_keys(r, TB), ALU.mult)
                        dve.drain()
                        dve.tensor_scalar(nmx[:, :], r, 1.0e10, -1.0e10, ALU.mult, ALU.add)
                        dve.drain()
                        dve.tensor_tensor(p, p, over_keys(nmx[:, :], TB), ALU.add)
                    dve.drain()
                    dve.tensor_reduce(m, p, AX.X, ALU.max)
                    dve.drain()
                    dve.tensor_tensor(p, p, over_keys(m, TB), ALU.subtract).then_inc(shifted[stage], 1)

                def finish(b):
                    for pair in range(2):
                        add(b, stage, pair, [2 * pair, 2 * pair + 1])
                    norm_stats(b)

                shift(straight[0])
                for b in straight:
                    norm_next(stage, b, xn_free(stage, b, 1))
                    p = prob[b.u % 2][:, 0:TB * C].rearrange("p (j c) -> p j c", j=TB)
                    s, r = sm[:, b.u % 2, 0:TB], rsm[:, b.u % 2, 0:TB]
                    dve.wait_ge(exped[stage], b.u + 1)
                    dve.tensor_reduce(s, p, AX.X, ALU.add)
                    dve.drain()
                    dve.reciprocal(r, s)
                    dve.drain()
                    dve.tensor_tensor(p, p, over_keys(r, TB), ALU.mult).then_inc(prob_ready[stage], 1)
                    if b.u >= 1:
                        finish(straight[b.u - 1])
                    if b.u + 1 < NB:
                        shift(straight[b.u + 1])
                finish(straight[-1])

            def fold1(stage, bq, bk):
                n = start_of("sh", stage)
                g = gates[:, stage // 2:stage // 2 + 1]
                kT, A, cb, Vf, Vt = (small[:, 0:512], small[:, 1024:1536], small[:, 1536:1792], small[:, 2048:3072],
                                     small[:, 3072:3584])
                for k in range(KD):
                    dve.tensor_scalar(small[:, 7168 + k * P:7168 + (k + 1) * P], ones[:, :], bq[:, k:k + 1], None, ALU.mult)
                dve.wait_ge(sh_full, n + 1)
                for k in range(KD):
                    ins = dve.tensor_scalar(kT[:, k * NC_:(k + 1) * NC_], sh[n % 2][:, k * NC_:(k + 1) * NC_],
                                            bk[:, k:k + 1], None, ALU.add)
                if stage == 4:
                    for k in range(KD):
                        ins = dve.tensor_scalar(Vt[:, k * NC_:(k + 1) * NC_], sh[n % 2][:, 512 + k * NC_:512 + (k + 1) * NC_],
                                                cols[:, 8 + k:9 + k], None, ALU.add)
                ins.then_inc(sh_taken, 1)
                dve.wait_ge(sh_full, n + 2)
                bias = (bv1 if stage == 2 else bfc2)[0:C, :].unsqueeze(1).broadcast_to([C, 2, D])
                for h in range(2):
                    dve.tensor_tensor(Vf[0:C, h * 512:(h + 1) * 512].rearrange("p (b d) -> p b d", b=2),
                                      sh[(n + 1) % 2][0:C, h * 512:(h + 1) * 512].rearrange("p (b d) -> p b d", b=2),
                                      bias, ALU.add)
                dve.drain()
                dve.tensor_scalar(Vf[0:C, :], Vf[0:C, :], g[0:C, :], None, ALU.mult).then_inc(sh_taken, 1)
                dve.wait_ge(sh_full, n + 3)
                dve.tensor_scalar(A, sh[n % 2][:, 0:512], D ** -0.5, None, ALU.mult)
                dve.tensor_scalar(cb, sh[n % 2][:, 512:512 + NC_], D ** -0.5, None, ALU.mult).then_inc(sh_taken, 1)

            def top(src):
                for j in range(TB):
                    dve.max(v8[:, j, :], src[:, j, 0:NE])
                dve.drain()

            def onehot(dst, which):
                dve.tensor_tensor(dst, iota8[:, :].unsqueeze(1).broadcast_to([P, TB, NE]),
                                  i8f[:, :, which].unsqueeze(2).broadcast_to([P, TB, NE]), ALU.is_equal)

            def places(src, n):
                for j in range(TB):
                    dve.max_index(i8[:, j, :], v8[:, j, :], src[:, j, 0:NE])
                dve.drain()
                dve.tensor_copy(i8f[:, :, 0:n], i8[:, :, 0:n])
                dve.drain()
                onehot(oh[:, :, :], 0)
                if n == 2:
                    onehot(oh2[:, :, :], 1)
                    dve.drain()
                    dve.tensor_tensor(oh[:, :, :], oh[:, :, :], oh2[:, :, :], ALU.add)
                dve.drain()

            def per_tile(a, n=NE):
                return a.unsqueeze(2).broadcast_to([P, TB, n])

            def softmax_shift(src):
                top(src)
                dve.tensor_tensor(ws[:, :, :], src[:, :, 0:NE], per_tile(v8[:, :, 0]), ALU.subtract).then_inc(router_in, 1)

            def softmax_probs(acts):
                dve.wait_ge(router_act, acts)
                dve.tensor_reduce(sr[:, 0, :], ws[:, :, :], AX.X, ALU.add)
                dve.drain()
                dve.reciprocal(sr[:, 1, :], sr[:, 0, :])
                dve.drain()
                dve.tensor_tensor(ws[:, :, :], ws[:, :, :], per_tile(sr[:, 1, :]), ALU.mult)
                dve.drain()

            def experts(stage, pieces):
                def hidden(b, e):
                    n, slot = b.fill("sh", stage, e)
                    g, r = sh[slot], act_r[e % 2]
                    done = b.scaled(2 * NE + 2, 2 * e if e <= NE else 2 * NE + 1)
                    if stage == 3 or e < NE:
                        for f in range(2):
                            dve.wait_ge(act_done[stage], done + f + 1)
                            sl = slice(f * S, (f + 1) * S)
                            if stage == 3:
                                ins = dve.scalar_tensor_tensor(hid[e % 2][:, sl], g[:, sl], 0.0, r[:, sl], ALU.max, ALU.mult)
                            else:
                                ins = dve.scalar_tensor_tensor(hid[e % 2][:, sl], r[:, sl], 1.0, g[:, sl], ALU.add, ALU.mult)
                    else:
                        dve.wait_ge(act_done[stage], done + 1)
                        dve.scalar_tensor_tensor(r[:, 0:S], r[:, 0:S], 1.0, g[:, 0:S], ALU.add, ALU.mult)
                        dve.drain()
                        f = e - NE
                        ins = dve.tensor_tensor(hid[0][:, f * S:(f + 1) * S], g[:, S:2 * S], r[:, 0:S], ALU.mult)
                    ins.then_inc(sh_taken, 1)

                def route(b, part):
                    if stage == 3 and part == 0:
                        dve.wait_ge(pt_moved, b.fill("pt", stage, 1)[0] + 1)
                        dve.tensor_tensor(lb[:, :, :], lg[:, :, 0:NE], lb1[:, :].unsqueeze(1).broadcast_to([P, TB, NE]), ALU.add)
                        dve.drain()
                        top(lb)
                        places(lb, 2)
                    if stage == 3 and part == 1:
                        dve.wait_ge(router_act, b.scaled(1, 1))
                        dve.tensor_scalar(ws[:, :, :], th[:, :, 0:NE], 0.5, 0.5, ALU.mult, ALU.add)
                        dve.drain()
                        dve.tensor_tensor(ws[:, :, :], ws[:, :, :], oh[:, :, :], ALU.mult)
                        dve.drain()
                        dve.tensor_reduce(sr[:, 0, :], ws[:, :, :], AX.X, ALU.add)
                        dve.drain()
                        dve.tensor_scalar(sr[:, 0, :], sr[:, 0, :], 1e-6, None, ALU.add)
                        dve.drain()
                        dve.reciprocal(sr[:, 1, :], sr[:, 0, :])
                        dve.drain()
                        dve.tensor_scalar(sr[:, 2, :], sr[:, 1, :], gates[:, 5:6], None, ALU.mult)
                        dve.drain()
                        dve.tensor_tensor(wE[:, :, 0:NE], ws[:, :, :], per_tile(sr[:, 2, :]), ALU.mult)
                        dve.tensor_scalar(wE[:, :, NE:NE + 1], ones[:, 0:TB].unsqueeze(2), gates[:, 5:6], None, ALU.mult)
                        dve.drain()
                    if stage == 7 and part == 0:
                        dve.wait_ge(pt_moved, b.fill("pt", stage, 1)[0] + 1)
                        dve.tensor_copy(lb[:, :, :], lg[:, :, 0:NE])
                        dve.drain()
                        softmax_shift(lb)
                    if stage == 7 and part == 1:
                        softmax_probs(b.scaled(2, 8 + 2))
                        top(ws)
                        places(ws, 2)
                        dve.tensor_tensor(ws[:, :, :], ws[:, :, :], oh[:, :, :], ALU.mult)
                        dve.drain()
                        dve.tensor_scalar(wE[:, :, 0:NE], ws[:, :, :], gates[:, 7:8], 0.5, ALU.mult, ALU.mult)
                        dve.tensor_scalar(wE[:, :, NE:NE + 1], th[:, :, NE:NE + 1], 1.0, 0.25, ALU.add, ALU.mult)
                        dve.drain()
                        dve.tensor_scalar(wE[:, :, NE:NE + 1], wE[:, :, NE:NE + 1], gates[:, 7:8], None, ALU.mult)
                        dve.drain()

                def sums(b, e):
                    for pair in range(2):
                        add(b, stage, 2 * e + pair, [2 * pair, 2 * pair + 1], lambda j: wE[:, j, e:e + 1])

                def body(b):
                    hidden(b, 0)
                    hidden(b, 1)
                    route(b, 0)
                    route(b, 1)
                    for e in range(NE + 1):
                        sums(b, e)
                        if e + 2 < pieces:
                            hidden(b, e + 2)
                        if e == 1:
                            norm_next(stage, b, xn_free(stage, b, 3))
                    norm_stats(b)
                blocks_of(dve, body)

            dve.wait_ge(in_ctx, 48)
            norm_stats(Block(0), lambda j: xin[:, j * D:(j + 1) * D], 2, c_var)
            dve.wait_ge(c_rstd, 1)
            apply_norm(xn_tile, lambda j: xin[:, j * D:(j + 1) * D], Block(0), 2).then_inc(c_done, 1)
            dve.wait_ge(in_x, 16)
            for b in straight:
                norm_stats(b)
            dve.wait_ge(ln_rstd, 1)
            dve.wait_ge(pt_full, 2)
            apply_norm(xn_tile, lambda j: xt(straight[0], j), straight[0], TB).then_inc(ln_done, 1)
            dve.wait_ge(in_n, 16 * 5)
            dve.memset(qw[:, :, :], 1.0)
            dve.drain()
            for w in range(2):
                a = qnat[:, w * NFQ * D:(w + 1) * NFQ * D].rearrange("p (c n) -> p c n", c=NFQ)
                dve.tensor_reduce(qw[:, 2 * w, 0:NFQ - 1], a[:, 0:NFQ - 1, :], AX.X, ALU.max, apply_absolute_value=True)
                dve.tensor_reduce(qw[0:RFQ, 2 * w, NFQ - 1:NFQ], a[0:RFQ, NFQ - 1, :], AX.X, ALU.max, apply_absolute_value=True)
            dve.tensor_reduce(qd[:, 0, :], qnat[:, 2 * NFQ * D:2 * NFQ * D + KD * FQ].rearrange("p (k n) -> p k n", k=KD),
                              AX.X, ALU.max, apply_absolute_value=True)
            dve.drain()
            for a in (qw[:, 0, :], qw[:, 2, :], qd[:, 0, :]):
                dve.tensor_scalar(a, a, 1.0 / QMAX, None, ALU.mult)
            dve.drain()
            for w in range(2):
                dve.reciprocal(qw[:, 2 * w + 1, :], qw[:, 2 * w, :])
            dve.reciprocal(qd[:, 1, :], qd[:, 0, :]).then_inc(q_inv, 1)
            dve.wait_ge(in_small, 16 * 24)
            dve.tensor_copy(rowf[:, :], rowm[:, :])
            dve.drain()
            dve.tensor_scalar(rowf[:, :], rowf[:, :], 0.0, None, ALU.not_equal)
            dve.wait_ge(gates_ready, 1)
            fold16(0, bo0)
            attend16(0)
            if stages > 1:
                def xna(j):
                    return xn_all[:, j * D:(j + 1) * D]
                dve.wait_ge(pt_full, start_of("pt", 1) - 2)
                for h in range(KD):
                    ins = dve.tensor_scalar(xn[:, h * P:(h + 1) * P], ident[:, :], qd[:, 0, h:h + 1], None, ALU.mult)
                ins.then_inc(q_diag, 1)
                dve.wait_ge(ln_rstd, 2 * NB)
                apply_norm(xna, lambda j: x[:, j * D:(j + 1) * D], straight[0], NT)
                dve.drain()

                def scale_of(k):
                    dve.wait_ge(q_top, k + 1)
                    dve.tensor_scalar(qs[:, 8 + k:9 + k], qs[:, 14 + k:15 + k], 0.5, 0.5, ALU.mult, ALU.add)
                    dve.drain()
                    dve.tensor_tensor(qs[:, 8 + k:9 + k], qs[:, 8 + k:9 + k], qs[:, 2 + k:3 + k], ALU.mult)
                    dve.drain()
                    dve.tensor_scalar(qs[:, 4 + k:5 + k], qs[:, 8 + k:9 + k], 1.0 / QMAX, None, ALU.mult)
                    dve.drain()
                    dve.reciprocal(qs[:, 6 + k:7 + k], qs[:, 4 + k:5 + k])
                    dve.drain()

                def to_int(a, o, inv):
                    dve.tensor_scalar(a, a, inv, QMAX, ALU.mult, ALU.min)
                    dve.drain()
                    dve.tensor_scalar(a, a, -QMAX - 1.0, MAGIC, ALU.max, ALU.add)
                    dve.drain()
                    return dve.tensor_scalar(o, a, MAGIC, None, ALU.subtract)

                dve.tensor_reduce(qs[:, 0:1], xn_all, AX.X, ALU.max, apply_absolute_value=True).then_inc(q_amax, 1)
                scale_of(0)
                dve.tensor_scalar(qw[:, 0, :], qw[:, 0, :], qs[:, 4:5], 0.5, ALU.mult, ALU.mult)
                dve.tensor_scalar(qw[:, 2, :], qw[:, 2, :], qs[:, 4:5], None, ALU.mult)
                dve.drain()
                dve.tensor_tensor(qw[:, 2, :], qw[:, 0, :], qw[:, 2, :], ALU.mult).then_inc(q_clip, 1)
                dve.wait_ge(q_int, 14)
                for wT in (wgT, wuT):
                    dve.memset(wT[:, :, FQ:NFQ * P], 0.0)
                dve.drain()
                n0 = start_of("pt", 1) + 5
                for b in range(NB):
                    if b >= 2:
                        dve.wait_ge(pt_full, n0 + b - 1)
                    to_int(xn_all[:, b * TB * D:(b + 1) * TB * D], xqi[:, (b % 2) * 1024:(b % 2) * 1024 + 1024],
                           qs[:, 6:7]).then_inc(x_int, 1)
                dve.memset(hall[:, NFQ - 1, :], 0.0)
                dve.drain()

                def gate_up(b):
                    for f in range(NFQ):
                        n, slot = b.fill("sh", 1, f)
                        r = RFQ if f == NFQ - 1 else P
                        dve.wait_ge(act_done[1], b.scaled(NFQ, f + 1))
                        t = act_r[f % 2][0:r, 0:S]
                        dve.scalar_tensor_tensor(t, t, 1.0, sh[slot][0:r, 0:S], ALU.add, ALU.mult)
                        dve.drain()
                        dve.scalar_tensor_tensor(hall[0:r, f, bass.ds(b.scaled(S), S)], t, qw[0:r, 2, f:f + 1],
                                                 sh[slot][0:r, S:2 * S], ALU.mult, ALU.mult).then_inc(sh_taken, 1)
                with dve.Fori(0, NB // 2) as i:
                    for u in range(2):
                        gate_up(Block(u, i))
                dve.drain()
                dve.tensor_reduce(qs[:, 1:2], area1[:, 4096:16384], AX.X, ALU.max, apply_absolute_value=True).then_inc(q_amax, 1)
                scale_of(1)
                dve.wait_ge(pt_moved, start_of("pt", 1) + 5)
                dve.tensor_scalar(sdb, sdb, qs[:, 5:6], gates[:, 4:5], ALU.mult, ALU.mult)
                dve.drain()

                def quantise(b):
                    a = hall[:, :, b * S:(b + 1) * S]
                    to_int(a, hq[b % 2].rearrange("p (f t) -> p f t", f=NFQ), qs[:, 7:8]).then_inc(hq_ready, 1)

                def back(b):
                    for pair in range(2):
                        n, slot = b.fill("o", 1, pair)
                        dve.wait_ge(o_full, n + 1)
                        y = xn[:, pair * 512:(pair + 1) * 512]
                        dve.tensor_tensor(y.rearrange("p (q d) -> p q d", q=2),
                                          ob[slot][:, :].rearrange("p (q d) -> p q d", q=2),
                                          sdb.unsqueeze(1).broadcast_to([P, 2, D]), ALU.mult)
                        dve.drain()
                        xx = x[:, (b.u * TB + 2 * pair) * D:(b.u * TB + 2 * pair + 2) * D]
                        dve.tensor_tensor(xx, xx, y, ALU.add).then_inc(o_added, 1)
                        dve.drain()
                quantise(0)
                quantise(1)
                for b in straight:
                    back(b)
                    if b.u + 2 < NB:
                        quantise(b.u + 2)
                    norm_stats(b)
                norm_next(1, straight[-1], start_of("pt", 2) - 2)
            if stages > 2:
                fold1(2, cols[:, 0:2], cols[:, 2:4])
                attend1(2)
            if stages > 3:
                experts(3, NE + 1)
            if stages > 4:
                fold1(4, cols[:, 4:6], cols[:, 6:8])
                attend1(4)
            if stages > 5:
                dve.memset(base[:, :, :], 0.0)

                def route5(b):
                    norm_next(5, b, xn_free(5, b, 3))
                    dve.wait_ge(pt_moved, b.fill("pt", 5, 1)[0] + 1)
                    softmax_shift(lg)
                    places(lg, 1)
                    dve.tensor_copy(ohb[:, :, :], oh[:, :, :]).then_inc(hot_ready, 1)
                    softmax_probs(b.scaled(1, 4 + 1))
                    dve.tensor_reduce(sr[:, 3, :], ws[:, :, :], AX.X, ALU.max)
                    dve.wait_ge(pt_moved, b.fill("pt", 5, 4)[0] + 1)
                    tot = cnt[:, TB * NE:2 * TB * NE].rearrange("p (j e) -> p j e", j=TB)
                    for j in range(TB):
                        dve.tensor_tensor(base[:, j + 1, :], base[:, j, :], tot[:, j, :], ALU.add)
                        dve.drain()
                    c3 = cnt[:, 0:TB * NE].rearrange("p (j e) -> p j e", j=TB)
                    dve.tensor_tensor(c3, c3, base[:, 0:TB, :], ALU.add)
                    dve.drain()
                    dve.tensor_tensor(c3, c3, oh[:, :, :], ALU.mult)
                    dve.tensor_copy(base[:, 0, :], base[:, TB, :])
                    dve.drain()
                    dve.tensor_reduce(sr[:, 0, :], c3, AX.X, ALU.add)
                    dve.drain()
                    dve.tensor_scalar(sr[:, 1, :], sr[:, 0, :], float(CAP), gates[:, 6:7], ALU.is_le, ALU.mult)
                    dve.drain()
                    dve.tensor_tensor(sr[:, 2, :], sr[:, 1, :], sr[:, 3, :], ALU.mult)
                    dve.drain()
                    for pair in range(2):
                        n, slot = b.fill("o", 5, pair)
                        dve.wait_ge(o_full, n + 1)
                        y = work[:, pair * 512:(pair + 1) * 512]
                        dve.tensor_tensor(y.rearrange("p (q d) -> p q d", q=2),
                                          ob[slot][:, :].rearrange("p (q d) -> p q d", q=2),
                                          be2[:, :].unsqueeze(1).broadcast_to([P, 2, D]), ALU.add)
                        dve.drain()
                        for q in range(2):
                            j = 2 * pair + q
                            ins = dve.scalar_tensor_tensor(xt(b, j), y[:, q * D:(q + 1) * D], sr[:, 2, j:j + 1], xt(b, j),
                                                           ALU.mult, ALU.add)
                        ins.then_inc(o_added, 1)
                for b in straight:
                    route5(b)
                    norm_stats(b)
            if stages > 6:
                fold16(6, bo3)
                attend16(6)
            if stages > 7:
                experts(7, NE + 2)


_INS = ['x', 'ctx_1024', 'mask_BxSxS2_bk1', 'mask_BxS_ik1', 'g_xattn', 'g_ffn', 'L0_xattn_Wq', 'L0_xattn_Wk', 'L0_xattn_Wv', 'L0_xattn_Wo', 'L0_xattn_bo', 'L0_ffn_clip_x', 'L0_ffn_clip_down', 'L0_ffn_w_gate', 'L0_ffn_w_up', 'L0_ffn_w_down', 'L1_xattn_Wq', 'L1_xattn_bq', 'L1_xattn_Wk', 'L1_xattn_bk', 'L1_xattn_Wv', 'L1_xattn_bv', 'L1_ffn_gate_w', 'L1_ffn_lb_bias', 'L1_ffn_w1', 'L1_ffn_w2', 'L1_ffn_cfc', 'L1_ffn_cproj', 'L2_xattn_Wq', 'L2_xattn_bq', 'L2_xattn_Wk', 'L2_xattn_bk', 'L2_xattn_Wv', 'L2_xattn_bv', 'L2_xattn_Wfc', 'L2_xattn_bfc', 'L2_ffn_w_gate', 'L2_ffn_w_expert', 'L2_ffn_b_expert', 'L3_xattn_ln_l_w', 'L3_xattn_ln_l_b', 'L3_xattn_ln_c_w', 'L3_xattn_ln_c_b', 'L3_xattn_Wq', 'L3_xattn_Wkv', 'L3_xattn_Wo', 'L3_xattn_bo', 'L3_ffn_router_w', 'L3_ffn_w1', 'L3_ffn_w2', 'L3_ffn_shared_gate_up', 'L3_ffn_shared_down', 'L3_ffn_shared_gate_w']


def kernel(**inputs):
    import numpy as _np
    import concourse.bacc as _bacc
    from concourse import mybir as _mybir
    from concourse.bass_utils import run_bass_kernel_spmd as _run

    nc = _bacc.Bacc("TRN2", target_bir_lowering=False, num_devices=1)
    arrays, args = {}, {}
    for name in _INS:
        a = _np.ascontiguousarray(inputs[name])
        arrays[f"in_{name}"] = a
        args[name] = nc.dram_tensor(f"in_{name}", a.shape, _mybir.dt.from_np(a.dtype), kind="ExternalInput").ap()
    out = nc.dram_tensor("out_0", (NB, S, D), F32, kind="ExternalOutput").ap()
    layers_kernel(nc, args, out)
    r = _run(nc, [arrays], core_ids=[0])
    return r.results[0]["out_0"]
```

```python
from contextlib import ExitStack

import numpy as np
import concourse.bass as bass
from concourse import mybir

ALU = mybir.AluOpType
ACT = mybir.ActivationFunctionType
AX = mybir.AxisListType
F32 = mybir.dt.float32
F32R = mybir.dt.float32r
BF16 = mybir.dt.bfloat16
U32 = mybir.dt.uint32
I32 = mybir.dt.int32
U8 = mybir.dt.uint8
RMAX = bass.bass_isa.ReduceOp.max

P = 128
D = 256
KD = D // P
NB, S = 4, 512
TB = S // P
NT = NB * TB
C = 64
NC_ = NB * C
H, DH = 16, 64
INNER = H * DH
MI = INNER // P
FQ = 704
NFQ = (FQ + P - 1) // P
RFQ = FQ - (NFQ - 1) * P
NE = 8
CAP = 100
EPS = 1e-5
QMAX = 127.0
MAGIC = 1.5 * 2.0 ** 23
FMAX = float(np.finfo(np.float32).max)

PRE = {"pt": [2 + 2 + 4, 17 - 2, 0, 2, 0, 0, 4, 0], "sh": [20, 6, 0, 0, 0, 0, 20, 0],
       "o": [0] * 8, "ln": [1, 0, 0, 0, 0, 0, 0, 0]}
PER = {"pt": [10, 0, 3 + 4, 4, 3, 5, 10, 4], "sh": [4, 0, 1, 9, 1, 0, 4, 10],
       "o": [4, 2, 2, 18, 2, 2, 4, 18], "ln": [1, 0, 1, 1, 1, 1, 1, 1]}


def start_of(pipe, stage):
    return sum(PRE[pipe][s] + NB * PER[pipe][s] for s in range(stage))


def wq_fills(stage):
    return start_of("pt", stage) + (2 if stage == 0 else 0)


def halvings(stage, b, e):
    per = NE + 1 if stage == 3 else NE + 2
    if e < 0:
        within = 0 if e == -1 else e + NE + 2 - per
    else:
        within = per if e == NE else e + 1
    return b.scaled(per, 3 + (NB * (NE + 1) if stage == 7 else 0) + within)


class Block:

    def __init__(self, u, i=None):
        self.u, self.i = u, i

    def scaled(self, k, plus=0):
        return self.u * k + plus if self.i is None else self.i * (2 * k) + (self.u * k + plus)

    def fill(self, pipe, stage, k=0):
        first = start_of(pipe, stage) + PRE[pipe][stage] + k
        return self.scaled(PER[pipe][stage], first), (first + self.u * PER[pipe][stage]) % 2


def layers_kernel(nc, I, out):
    ctx = ExitStack()
    with ctx:
        def sb(name, shape, dt=F32):
            return ctx.enter_context(nc.sbuf_tensor(name, shape, dt))

        def sem(name):
            return ctx.enter_context(nc.semaphore(name))

        x = sb("x", [P, NT * D])
        xn = sb("xn", [P, TB * D])
        xnT = sb("xnT", [P, 2, KD, S])
        ctxT = sb("ctxT", [P, KD, NC_])
        ctxnT = sb("ctxnT", [P, KD, NC_])
        mask = sb("mask", [P, NT, C], U8)
        work = sb("work", [P, 4096])
        with nc.sbuf_tensor("area1", [P, 16384], F32) as area1, nc.sbuf_tensor("area2", [P, 12288], F32) as area2, \
                nc.sbuf_tensor("area3", [P, 9216], F32) as area3:
            pass
        wA = sb("wA", [P, 2, 4096], F32R)
        sA = sb("sA", [P, 2, 512], F32R)
        sb("pad1", [P, 1536])
        xnTR = sb("xnTR", [P, 2, 2, KD * S], F32R)
        sB = sb("sB", [P, 2, 512], F32R)
        sb("pad2", [P, 512 + 4096])
        hidR = sb("hidR", [P, 2, 2, 2 * S], F32R)
        sb("pad3", [P, 4096])
        wB = sb("wB", [P, 2, 4096], F32R)
        sC = sb("sC", [P, 2, 512], F32R)
        ident = sb("ident", [P, P])
        identb = sb("identb", [P, P], BF16)
        ones = sb("ones", [P, P])
        triu = sb("triu", [P, P], BF16)
        onesb = sb("onesb", [P, P], BF16)
        iota8 = sb("iota8", [P, NE])
        bo0 = sb("bo0", [P, D])
        bv1 = sb("bv1", [P, D])
        bfc2 = sb("bfc2", [P, D])
        be2 = sb("be2", [P, D])
        bo3 = sb("bo3", [P, D])
        lb1 = sb("lb1", [P, NE])
        gates = sb("gates", [P, 8])
        clips = sb("clips", [P, 2])
        cols = sb("cols", [P, 16])
        cols2 = sb("cols2", [P, 4])
        rowm = sb("rowm", [P, NT], I32)
        rowf = sb("rowf", [P, NT])
        gw = sb("gw", [P, 3, KD, NE + 1])
        stats = sb("stats", [P, TB, 6])
        mv = sb("mv", [P, NT, 2])
        mvb = sb("mvb", [P, TB, 2])
        var = sb("var", [P, NT])
        rstd = sb("rstd", [P, NT])
        minush = sb("minush", [P, NT])
        lat = sb("lat", [P, NT])
        mx = sb("mx", [P, 2, H])
        sm = sb("sm", [P, 2, H])
        rsm = sb("rsm", [P, 2, H])
        nmx = sb("nmx", [P, TB])
        lg = sb("lg", [P, TB, NE + 1])
        lb = sb("lb", [P, TB, NE])
        v8 = sb("v8", [P, TB, NE])
        i8 = sb("i8", [P, TB, NE], U32)
        i8f = sb("i8f", [P, TB, 2])
        oh = sb("oh", [P, TB, NE])
        oh2 = sb("oh2", [P, TB, NE])
        ohb = sb("ohb", [P, TB, NE], BF16)
        th = sb("th", [P, TB, NE + 1])
        ws = sb("ws", [P, TB, NE])
        sr = sb("sr", [P, 4, TB])
        wE = sb("wE", [P, TB, NE + 1])
        cnt = sb("cnt", [P, (TB + 1) * NE])
        base = sb("base", [P, NE])
        qs = sb("qs", [P, 16])
        qw = sb("qw", [P, 4, NFQ])
        qd = sb("qd", [P, 4, KD])
        xmm = sb("xmm", [P, 2, NT])
        hmax = sb("hmax", [P, NB * NFQ])

        pt = [ctx.enter_context(nc.psum_tensor(f"pt{i}", [P, 512], F32)) for i in range(2)]
        sh = [ctx.enter_context(nc.psum_tensor(f"sh{i}", [P, 1024], F32)) for i in range(2)]
        ob = [ctx.enter_context(nc.psum_tensor(f"ob{i}", [P, 512], F32)) for i in range(2)]

        gu = [(sh[0][:, 0:512], sh[0][:, 512:1024]), (sh[1][:, 0:512], sh[1][:, 512:1024]),
              (ob[0][:, :], ob[1][:, :]), (pt[0][:, :], pt[1][:, :])]

        xin = work[:, 0:2 * D]
        prob = [work[:, i * 1024:(i + 1) * 1024] for i in range(2)]
        probT = work[:, 2048:3072]
        hid = [work[:, i * 1024:(i + 1) * 1024] for i in range(3)]
        gate_t = [work[:, i * S:(i + 1) * S] for i in range(4)]
        up_s = [work[:, 2048 + i * S:2048 + (i + 1) * S] for i in range(4)]
        hq = [work[:, i * 2048:i * 2048 + NFQ * S // 2].bitcast(BF16) for i in range(2)]
        keysA = area1[:, 0:8192]
        valsO = area1[:, 8192:16384]
        wq16, wk16, wv16, wo16 = (area2[:, i * 2048:(i + 1) * 2048] for i in range(4))
        kT16 = work[:, 0:2048]
        vD16 = area2[:, 8192:12288].rearrange("p (m b j c) -> p m b j c", m=MI, b=NB, j=2)
        wqT16 = work[:, 2048:4096]
        xn_all = area1[:, 0:4096]
        hall = area1[:, 4096:16384].rearrange("p (f t) -> p f t", f=NFQ)
        qnat = area3[:, 0:NFQ * D * 2 + KD * FQ]
        qint = area3[:, 4608:6912].bitcast(BF16)
        wgT = area3[:, 0:NFQ * P].bitcast(BF16).rearrange("p (k f) -> p k f", k=KD)
        wuT = area3[:, NFQ * P:2 * NFQ * P].bitcast(BF16).rearrange("p (k f) -> p k f", k=KD)
        wdT = area3[:, 2 * NFQ * P:3 * NFQ * P].bitcast(BF16).rearrange("p (f d) -> p f d", f=NFQ)
        sdb = area3[:, 2304:2560]
        xqT = area3[:, 6912:8960].bitcast(BF16).rearrange("p (k t) -> p k t", k=KD)
        xqi = work[:, 0:2048].bitcast(BF16)
        w1h = [area2[:, 8192 + i * 512:8704 + i * 512] for i in range(7)]
        class Fold:

            def __init__(self, kT, wT, bq, A, cb, V, Vt=None):
                self.kT, self.wT, self.bq, self.A, self.cb, self.V, self.Vt = kT, wT, bq, A, cb, V, Vt
        xn_done = area1[:, 0:4096]
        fold2 = Fold(kT=xn_done[:, 0:512], wT=[xn_done[:, 512:1024]], bq=xn_done[:, 1024:1280],
                     A=area3[:, 8192:8704], cb=area3[:, 8704:8960], V=area2[:, 8192:9216])
        fold4 = Fold(wT=[xn_done[:, 1280 + i * 512:1792 + i * 512] for i in range(3)], kT=xn_done[:, 2816:3328],
                     Vt=xn_done[:, 3328:3840], bq=xn_done[:, 3840:4096],
                     A=area2[:, 9216:9728], cb=area2[:, 11776:12032], V=area2[:, 10240:11264])
        folds = {2: fold2, 4: fold4}
        nat1, nat2 = area2[:, 0:4096], area2[:, 4096:8192]
        natc = area1[:, 8192:9216]
        lgT = area1[0:NE + 1, 9216:9216 + S]
        wexp = area1[:, 10240:10752]
        raw1, raw2 = area2[:, 0:4096], area2[:, 8192:12288]
        gup, down = area2[:, 0:1024], area2[:, 1024:1536]

        def half_pair(w, g=0):
            return w[:, 0, g * 512:(g + 1) * 512], w[:, 1, g * 512:(g + 1) * 512]
        split2 = [half_pair(w, g) for w in (wA, wB) for g in range(NE)]
        nat12 = [nat[:, g * 512:(g + 1) * 512] for nat in (nat1, nat2) for g in range(NE)]
        moved_T = [area1[:, 9216 + i * 512:9728 + i * 512] for i in range(2)]
        split3 = [half_pair(sB), half_pair(sC)]
        split7 = [(half_pair(wA, g), raw2[:, g * 512:(g + 1) * 512]) for g in range(NE)] + [
            (tuple(h.rearrange("p (k n) -> p k n", k=KD) for h in half_pair(s)),
             gup.rearrange("p (k n) -> p k n", k=KD)[:, :, i * D:(i + 1) * D]) for i, s in enumerate((sC, sB))] + [
            (half_pair(sA), down)]

        in_ctx, in_x, in_small, in_wk, in_wv, in_wq, in_wo, in_n, in_c, in_wexp, in_w6, in_w7, in_s7 = map(
            sem, "in_ctx in_x in_small in_wk in_wv in_wq in_wo in_n in_c in_wexp in_w6 in_w7 in_s7".split())
        const_made = sem("const_made")
        pool_step = sem("pool_step")
        gates_ready = sem("gates_ready")
        pt_full, pt_moved = sem("pt_full"), sem("pt_moved")
        sh_full, sh_taken = sem("sh_full"), sem("sh_taken")
        sh_half = sem("sh_half")
        o_full, o_added = sem("o_full"), sem("o_added")
        ln_var, ln_rstd, ln_done = sem("ln_var"), sem("ln_rstd"), sem("ln_done")
        c_var, c_rstd, c_done = sem("c_var"), sem("c_rstd"), sem("c_done")
        shifted = [sem(f"shifted{s}") for s in range(8)]
        exped = [sem(f"exped{s}") for s in range(8)]
        prob_ready = [sem(f"prob_ready{s}") for s in range(8)]
        act_done = [sem(f"act_done{s}") for s in range(8)]
        router_in, router_act = sem("router_in"), sem("router_act")
        hot_ready = sem("hot_ready")
        stored = sem("stored")
        wt_lo = sem("wt_lo")
        w_hi, w_lo = sem("w_hi"), sem("w_lo")
        raw_split = sem("raw_split")
        x_hi, x_lo = sem("x_hi"), sem("x_lo")
        h_hi, h_lo = sem("h_hi"), sem("h_lo")
        q_inv, q_int, q_diag = map(sem, "q_inv q_int q_diag".split())
        q_amax, q_top, q_scaled = map(sem, "q_amax q_top q_scaled".split())
        x_clip, h_clip, x_int, hq_ready = map(sem, "x_clip h_clip x_int hq_ready".split())
        gu_full, gu_half, gu_taken = map(sem, "gu_full gu_half gu_taken".split())

        def xt(b, j):
            return x[:, bass.ds(b.scaled(TB * D, j * D), D)]

        block = ctx.enter_context(nc.Block())
        straight = [Block(u) for u in range(NB)]

        def blocks_of(eng, body):
            with eng.Fori(0, NB // 2) as i:
                for u in range(2):
                    body(Block(u, i))

        @block.sync
        def _(sp):
            def load(dst, src, s):
                sp.dma_start(dst, src).then_inc(s, 16)

            def load_columns(dst, src, s):
                sp.dma_start(dst, src, allow_slow_non_contiguous=True).then_inc(s, 16)

            def rows(w, k=KD):
                return w.rearrange("(k p) n -> p k n", p=P)

            def as3(a, k=KD):
                return a.rearrange("p (k n) -> p k n", k=k)

            load(as3(xin), I["ctx_1024"].rearrange("b c d -> (b c) d").rearrange("(t p) d -> p t d", p=P), in_ctx)
            load_columns(cols2[:, 0:2], I["L3_xattn_ln_c_w"].rearrange("(k p) -> p k", p=P), in_ctx)
            load_columns(cols2[:, 2:4], I["L3_xattn_ln_c_b"].rearrange("(k p) -> p k", p=P), in_ctx)
            load(as3(wk16), rows(I["L0_xattn_Wk"]), in_wk)
            load(as3(wv16), rows(I["L0_xattn_Wv"]), in_wv)
            load(as3(wq16), rows(I["L0_xattn_Wq"]), in_wq)
            load(x[:, :].rearrange("p (t d) -> p t d", t=NT),
                 I["x"].rearrange("b (t p) d -> p (b t) d", p=P), in_x)
            load(as3(wo16, MI), rows(I["L0_xattn_Wo"]), in_wo)
            for j, n in enumerate(["L1_xattn_bq", "L1_xattn_bk", "L2_xattn_bq", "L2_xattn_bk", "L2_xattn_bv",
                                   "L3_xattn_ln_l_w", "L3_xattn_ln_l_b"]):
                load_columns(cols[:, 2 * j:2 * j + 2], I[n].rearrange("(k p) -> p k", p=P), in_small)
            for t, n in ((bo0, "L0_xattn_bo"), (bv1, "L1_xattn_bv"), (bfc2, "L2_xattn_bfc"), (be2, "L2_ffn_b_expert"),
                         (bo3, "L3_xattn_bo"), (lb1, "L1_ffn_lb_bias")):
                load(t[:, :], I[n].partition_broadcast(P), in_small)
            load(gates[:, 0:4], I["g_xattn"].partition_broadcast(P), in_small)
            load(gates[:, 4:8], I["g_ffn"].partition_broadcast(P), in_small)
            load(clips[:, 0:1], I["L0_ffn_clip_x"].partition_broadcast(P), in_small)
            load(clips[:, 1:2], I["L0_ffn_clip_down"].partition_broadcast(P), in_small)
            load(mask[:, :, :], I["mask_BxSxS2_bk1"].rearrange("b (t p) c -> p (b t) c", p=P), in_small)
            load_columns(rowm[:, :], I["mask_BxS_ik1"].rearrange("b (t p) -> p (b t)", p=P), in_small)
            for k in range(KD):
                load_columns(gw[:, 0, k, 0:NE], I["L1_ffn_gate_w"][:, k * P:(k + 1) * P].rearrange("e p -> p e"), in_small)
            load(gw[:, 1, :, 0:NE], rows(I["L2_ffn_w_gate"]), in_small)
            load(gw[:, 2, :, 0:NE], rows(I["L3_ffn_router_w"]), in_small)
            load_columns(gw[:, 2, :, NE:NE + 1], rows(I["L3_ffn_shared_gate_w"]), in_small)
            for w, n in ((0, "L0_ffn_w_gate"), (1, "L0_ffn_w_up")):
                a = qnat[:, w * NFQ * D:(w + 1) * NFQ * D].rearrange("p (c n) -> p c n", c=NFQ)
                load(a[:, 0:NFQ - 1, :], rows(I[n][0:(NFQ - 1) * P, :]), in_n)
                load(a[0:RFQ, NFQ - 1, :], I[n][(NFQ - 1) * P:FQ, :], in_n)
            load(as3(qnat[:, 2 * NFQ * D:2 * NFQ * D + KD * FQ]), rows(I["L0_ffn_w_down"]), in_n)
            sp.wait_ge(sh_taken, start_of("sh", 0) + PRE["sh"][0])
            for a, n in zip(w1h, ("L1_xattn_Wq", "L1_xattn_Wk", "L1_xattn_Wv", "L2_xattn_Wq", "L2_xattn_Wk",
                                  "L2_xattn_Wv", "L2_xattn_Wfc")):
                load(as3(a), rows(I[n]), in_c)
            load(nat1.rearrange("p (e n) -> p e n", e=2 * NE), rows(I["L1_ffn_w1"].rearrange("e h d -> (e h) d")), in_c)
            load(nat2.rearrange("p (e n) -> p e n", e=2 * NE), rows(I["L1_ffn_w2"].rearrange("e h d -> (e h) d")), in_c)
            sp.wait_ge(o_added, start_of("o", 2))
            load(as3(natc[:, 0:512]), rows(I["L1_ffn_cfc"]), in_wexp)
            load(as3(natc[:, 512:1024]), rows(I["L1_ffn_cproj"]), in_wexp)
            load(as3(wexp), rows(I["L2_ffn_w_expert"]), in_wexp)
            sp.wait_ge(o_added, start_of("o", 4))
            for a, n in ((wq16, I["L3_xattn_Wq"]), (wk16, I["L3_xattn_Wkv"][:, 0:INNER]),
                         (wv16, I["L3_xattn_Wkv"][:, INNER:2 * INNER])):
                load(as3(a), rows(n), in_w6)
            load(as3(wo16, MI), rows(I["L3_xattn_Wo"]), in_w6)
            sp.wait_ge(sh_taken, start_of("sh", 6) + PRE["sh"][6])
            load(raw1.rearrange("p (e n) -> p e n", e=2 * NE), rows(I["L3_ffn_w1"].rearrange("e d f -> (e d) f")), in_w7)
            load(raw2.rearrange("p (e n) -> p e n", e=2 * NE), rows(I["L3_ffn_w2"].rearrange("e f d -> (e f) d")), in_w7)
            sp.wait_ge(raw_split, 2)
            load(as3(gup), rows(I["L3_ffn_shared_gate_up"]), in_s7)
            load(as3(down), rows(I["L3_ffn_shared_down"]), in_s7)
            for b in range(NB):
                sp.wait_ge(o_added, start_of("o", 7) + (b + 1) * PER["o"][7])
                sp.dma_start(out[b].rearrange("(t p) d -> p t d", p=P),
                             x[:, b * TB * D:(b + 1) * TB * D].rearrange("p (t d) -> p t d", t=TB)).then_inc(stored, 16)
            sp.wait_ge(stored, 16 * NB)

        @block.gpsimd
        def _(pool):
            def ones_where(t, compare, pattern, mult, fill, start):
                pool.memset(t, start).then_inc(pool_step, 1)
                ones_where.n += 1
                pool.wait_ge(pool_step, ones_where.n)
                pool.affine_select(out=t, in_=t, compare_op=compare, fill=fill, base=0,
                                   pattern=pattern, channel_multiplier=mult).then_inc(const_made, 1)
            ones_where.n = 0
            ones_where(ident[:, :], ALU.not_equal, [[-1, P]], 1, 1.0, 0.0)
            pool.memset(minush[:, :], -0.5).then_inc(const_made, 1)
            ones_where(identb[:, :], ALU.not_equal, [[-1, P]], 1, 1.0, 0.0)
            ones_where(triu[:, :], ALU.is_ge, [[1, P]], -1, 0.0, 1.0)
            pool.memset(ones[:, :], 1.0).then_inc(const_made, 1)
            pool.memset(onesb[:, :], 1.0).then_inc(const_made, 1)
            pool.iota(iota8[:, :], pattern=[[1, NE]], base=0, channel_multiplier=0,
                      allow_small_or_imprecise_dtypes=True).then_inc(const_made, 1)

            def rsqrt(n, given):
                pool.tensor_tensor(rstd[:, n], var[:, n], minush[:, n], ALU.pow).then_inc(given, 1)

            pool.wait_ge(const_made, 7)
            pool.wait_ge(c_var, 1)
            rsqrt(slice(0, 2), c_rstd)

            def block_rstd(t, b):
                pool.wait_ge(ln_var, t + 1)
                rsqrt(slice(b * TB, (b + 1) * TB), ln_rstd)

            for b in range(NB):
                block_rstd(b, b)
            pool.wait_ge(q_inv, 1)
            pool.wait_ge(in_n, 16 * 5)

            def to_int(a, o, inv):
                pool.tensor_scalar(a, a, inv, QMAX, ALU.mult, ALU.min)
                pool.drain()
                pool.tensor_scalar(a, a, -QMAX - 1.0, MAGIC, ALU.max, ALU.add)
                pool.drain()
                pool.tensor_scalar(o, a, MAGIC, None, ALU.subtract).then_inc(q_int, 1)
            after = {0: range(0, 8), 1: range(8, 10), 2: range(10, 12), 3: range(12, 14)}
            for b in range(NB):
                for c in after[b]:
                    if c < 2 * NFQ:
                        r = RFQ if c % NFQ == NFQ - 1 else P
                        to_int(qnat[0:r, c * D:(c + 1) * D], qint[0:r, c * D:(c + 1) * D],
                               qw[0:r, 1 + 2 * (c // NFQ), c % NFQ:c % NFQ + 1])
                    else:
                        k, o = c - 2 * NFQ, 2 * NFQ * D + (c - 2 * NFQ) * FQ
                        to_int(qnat[:, o:o + FQ], qint[:, o:o + FQ], qd[:, 1, k:k + 1])
                block_rstd(NB + b, b)
            def largest(k):
                pool.wait_ge(q_amax, k + 1)
                pool.partition_all_reduce(qs[:, k + 2:k + 3], qs[:, k:k + 1], P, RMAX).then_inc(q_top, 1)

            largest(0)
            pool.memset(hmax[:, :], 0.0).then_inc(gu_taken, 4)

            def gate_up(b):
                for f in range(NFQ):
                    slot = (b.u * NFQ + f) % 4
                    r = RFQ if f == NFQ - 1 else P
                    pool.wait_ge(gu_half, b.scaled(NFQ, 4 + f + 1))
                    pool.tensor_tensor(hall[0:r, f, bass.ds(b.scaled(S), S)], gate_t[slot][0:r, :],
                                       up_s[slot][0:r, :], ALU.mult).then_inc(gu_taken, 1)
            blocks_of(pool, gate_up)
            largest(1)
            for b in range(NB):
                block_rstd(2 * NB + b, b)

            def rest(o, a, hi, given):
                pool.tensor_tensor(o, a, hi.bitcast(F32), ALU.subtract).then_inc(given, 1)

            def expert_halves(stage):
                k = stage // 4
                if stage == 3:
                    pool.memset(qs[:, 0:1], 0.0).then_inc(h_lo, 3)

                def body(b):
                    for e in range(NE + 1):
                        slot = (b.u * (NE + 1) + e) % 2
                        parts = 2 if e == NE and stage == 7 else 1
                        for q in range(parts):
                            part = slice(q * 2 * S // parts, (q + 1) * 2 * S // parts)
                            pool.wait_ge(h_hi, b.scaled(NE + 1 + k, NB * (NE + 1) * k + e + q + 1))
                            rest(hidR[:, slot, 1, part], hid[e % 3][:, part], hidR[:, slot, 0, part], h_lo)
                    pool.wait_ge(ln_var, b.scaled(1, (stage + 1) * NB + 1))
                    n = bass.ds(b.scaled(TB), TB)
                    pool.tensor_tensor(rstd[:, n], var[:, n], minush[:, n], ALU.pow).then_inc(ln_rstd, 1)
                blocks_of(pool, body)
            for b in range(NB):
                for g in range(4 * b, 4 * b + 4):
                    pool.wait_ge(pt_moved, straight[b].fill("pt", 2, 3 + g % 4)[0] + 1)
                    rest(split2[g][1], moved_T[g % 2], split2[g][0], wt_lo)
                block_rstd(3 * NB + b, b)
            expert_halves(3)
            for b in range(NB):
                block_rstd(5 * NB + b, b)
            for b in range(NB):
                n = slice(b * TB, (b + 1) * TB)
                pool.wait_ge(ln_var, 6 * NB + b + 1)
                pool.tensor_tensor(rstd[:, n], var[:, n], minush[:, n], ALU.pow)
                pool.drain()
                pool.tensor_tensor(lat[:, n], rstd[:, n], rstd[:, n], ALU.mult)
                pool.drain()
                pool.tensor_tensor(lat[:, n], lat[:, n], mv[:, n, 1], ALU.mult)
                pool.drain()
                pool.tensor_scalar(lat[:, n], lat[:, n], EPS, None, ALU.add)
                pool.drain()
                pool.tensor_tensor(lat[:, n], lat[:, n], minush[:, n], ALU.pow)
                pool.drain()
                pool.tensor_tensor(rstd[:, n], rstd[:, n], lat[:, n], ALU.mult).then_inc(ln_rstd, 1)
            for b in range(NB):
                if b == 0:
                    pool.wait_ge(in_w7, 32)
                q = slice(b * 1024, (b + 1) * 1024)
                pool.tensor_copy(wB[:, 0, q], raw1[:, q])
                pool.drain()
                rest(wB[:, 1, q], raw1[:, q], wB[:, 0, q], raw_split)
                block_rstd(7 * NB + b, b)
            expert_halves(7)

        @block.tensor
        def _(pe):
            def pt_slot(n):
                if not isinstance(n, int) or n >= 2:
                    pe.wait_ge(pt_moved, n - 1)

            def sh_slot(n):
                if not isinstance(n, int) or n >= 2:
                    pe.wait_ge(sh_taken, n - 1)

            def o_slot(n):
                if not isinstance(n, int) or n >= 2:
                    pe.wait_ge(o_added, n - 1)

            def transposes(n, slot, pieces, idn=None, cast=None, waited=False):
                if not waited:
                    pt_slot(n)
                for (r, c0, c1), src in pieces:
                    dst = pt[slot][:, :] if cast is None else pt[slot][:, :].bitcast(cast)
                    mm = pe.transpose(dst[0:r, c0:c1], src, (idn or ident)[0:src.shape[0], 0:src.shape[0]])
                mm.then_inc(pt_full, 1)

            def norm_T(stage, b, k0):
                pe.wait_ge(ln_done, b.fill("ln", stage)[0] + 1)
                for k in range(KD):
                    n, slot = b.fill("pt", stage, k0 + k)
                    transposes(n, slot, [((P, j * P, (j + 1) * P), xn[:, j * D + k * P:j * D + (k + 1) * P])
                                         for j in range(TB)])

            def first_norm_T(n0, count):
                pe.wait_ge(ln_done, count)
                for k in range(KD):
                    transposes(n0 + k, (n0 + k) % 2,
                               [((P, j * P, (j + 1) * P), xn[:, j * D + k * P:j * D + (k + 1) * P]) for j in range(TB)])

            def T(stage, b):
                return xnT[:, (b.fill("ln", stage)[1] + 1) % 2]

            def halves(lhs, rhs):
                out_l, out_r = [], []
                for (lh, ll), (rh, rl) in zip(lhs, rhs):
                    out_l += [lh, lh, ll]
                    out_r += [rh, rl, rh]
                return out_l, out_r

            def wait_T(stage, u, k):
                if u == 0:
                    return
                pe.wait_ge(pt_moved, Block(u - 1).fill("pt", stage, k)[0] + 1)

            def product(o, lhs, rhs):
                for k, (a, b) in enumerate(zip(lhs, rhs)):
                    mm = pe.matmul(o, a, b, start=(k == 0), stop=(k == len(lhs) - 1))
                return mm

            def fold16(stage, cT_, in_k, in_v, in_q, in_o, loads):
                n0 = start_of("sh", stage)
                n = n0
                for w, given in ((wk16, in_k), (wv16, in_v)):
                    pe.wait_ge(given, loads)
                    for half in range(2):
                        sh_slot(n)
                        for q in range(4):
                            m = 4 * half + q
                            mm = product(sh[n % 2][:, q * NC_:(q + 1) * NC_],
                                         [w[:, k * INNER + m * P:k * INNER + (m + 1) * P] for k in range(KD)],
                                         [cT_[:, k, :] for k in range(KD)])
                        mm.then_inc(sh_full, 1)
                        n += 1
                pe.wait_ge(in_q, loads)
                p0 = wq_fills(stage)
                for f in range(4):
                    transposes(p0 + f, (p0 + f) % 2,
                               [((P, q * P, (q + 1) * P),
                                 wq16[:, (q % 2) * INNER + (2 * f + q // 2) * P:(q % 2) * INNER + (2 * f + q // 2 + 1) * P])
                                for q in range(4)])
                pe.wait_ge(pt_moved, p0 + 4)
                pe.wait_ge(sh_taken, n0 + 4)
                for m in range(MI):
                    sh_slot(n)
                    for k in range(KD):
                        for j in range(2):
                            r = slice(64 * j, 64 * j + 64)
                            mm = pe.matmul(sh[n % 2][:, j * 512 + k * NC_:j * 512 + (k + 1) * NC_],
                                           wqT16[r, m * D + k * P:m * D + (k + 1) * P],
                                           kT16[r, m * NC_:(m + 1) * NC_], start=True, stop=True)
                    mm.then_inc(sh_full, 1)
                    n += 1
                pe.wait_ge(in_o, loads)
                for m in range(MI):
                    sh_slot(n)
                    for b in range(NB):
                        mm = pe.matmul(sh[n % 2][:, b * D:(b + 1) * D], vD16[:, m, b, :, :].rearrange("p j c -> p (j c)"),
                                       wo16[:, m * D:(m + 1) * D], start=True, stop=True)
                    mm.then_inc(sh_full, 1)
                    n += 1

            def attend16(stage):
                def scores(u, j):
                    n, slot = Block(u).fill("sh", stage, j)
                    sh_slot(n)
                    for c in range(2):
                        mm = product(sh[slot][:, c * 512:(c + 1) * 512],
                                     [T(stage, Block(u))[:, k, j * P:(j + 1) * P] for k in range(KD)],
                                     [keysA[:, (k * NB + u) * H * C + c * 512:(k * NB + u) * H * C + (c + 1) * 512]
                                      for k in range(KD)])
                    mm.then_inc(sh_full, 1)

                pe.wait_ge(sh_taken, start_of("sh", stage) + PRE["sh"][stage])
                scores(0, 0)
                scores(0, 1)
                for b in straight:
                    for j in range(TB):
                        next_norm = stage == 6 or b.u + 1 < NB
                        k0 = 2 * j if j < 2 or not next_norm else 2 * j + 2
                        if j == 2 and next_norm:
                            norm_T(stage, b, 4)
                        pe.wait_ge(prob_ready[stage], b.u * TB + j + 1)
                        for half in range(2):
                            n, slot = b.fill("pt", stage, k0 + half)
                            transposes(n, slot, [((P, q * P, (q + 1) * P),
                                                  prob[j % 2][:, (4 * half + q) * P:(4 * half + q + 1) * P]) for q in range(4)])
                        if j < 2:
                            scores(b.u, j + 2)
                        elif b.u + 1 < NB:
                            wait_T(stage, b.u + 1, 5)
                            scores(b.u + 1, j - 2)
                        n, slot = b.fill("o", stage, j)
                        o_slot(n)
                        pe.wait_ge(pt_moved, b.fill("pt", stage, k0 + 1)[0] + 1)
                        product(ob[slot][:, 0:D], [probT[:, m * P:(m + 1) * P] for m in range(MI)],
                                [valsO[:, (m * NB + b.u) * D:(m * NB + b.u + 1) * D] for m in range(MI)]
                                ).then_inc(o_full, 1)

            def weight_T(n, src):
                transposes(n, n % 2, [((P, k * D + e * P, k * D + (e + 1) * P), src[:, e * D + k * P:e * D + (k + 1) * P])
                                      for k in range(KD) for e in range(KD)])

            def attend1(stage):
                A, Vf = folds[stage].A, folds[stage].V

                def weights(b, which):
                    for q in which if stage == 2 else ():
                        weight_T(b.fill("pt", 2, 3 + q)[0], nat12[4 * b.u + q])

                def scores(b):
                    n, slot = b.fill("sh", stage)
                    sh_slot(n)
                    for j in range(TB):
                        at = b.u // 2 * 2 * C
                        mm = product(sh[slot][:, j * 2 * C:(j + 1) * 2 * C],
                                     [T(stage, b)[:, k, j * P:(j + 1) * P] for k in range(KD)],
                                     [A[:, k * NC_ + at:k * NC_ + at + 2 * C] for k in range(KD)])
                    mm.then_inc(sh_full, 1)

                pe.wait_ge(sh_taken, start_of("sh", stage) + PRE["sh"][stage])
                pe.wait_ge(pt_moved, start_of("pt", stage))
                scores(straight[0])
                for b in straight:
                    norm_T(stage, b, 0)
                    pe.wait_ge(prob_ready[stage], b.u + 1)
                    n, slot = b.fill("pt", stage, 2)
                    transposes(n, slot, [((C, j * P, (j + 1) * P), prob[b.u % 2][:, j * C:(j + 1) * C]) for j in range(TB)])
                    if b.u + 1 < NB:
                        wait_T(stage, b.u + 1, 1)
                        scores(straight[b.u + 1])
                    weights(b, (0, 1))
                    pe.wait_ge(pt_moved, n + 1)
                    for pair in range(2):
                        m, oslot = b.fill("o", stage, pair)
                        o_slot(m)
                        for q in range(2):
                            j = 2 * pair + q
                            mm = pe.matmul(ob[oslot][:, q * D:(q + 1) * D],
                                           probT[0:C, (b.u % 2) * S + j * P:(b.u % 2) * S + (j + 1) * P],
                                           Vf[0:C, b.u * D:(b.u + 1) * D], start=True, stop=True)
                        mm.then_inc(o_full, 1)
                    weights(b, (2, 3))

            def chunks(w, m=None):
                return [w[:, k * D:(k + 1) * D] if m is None else w[:, k * D + m * P:k * D + (m + 1) * P] for k in range(KD)]

            def fold1(stage, part, wq, wk, wv, fc=None):
                n = start_of("sh", 1) + PRE["sh"][1] - 6 + (0 if stage == 2 else 3)
                kT, Vt = folds[stage].kT, folds[stage].Vt
                sh_slot(n + part)
                if part == 0:
                    cc = [ctxT[:, k, :] for k in range(KD)]
                    for m in range(KD):
                        mm = product(sh[n % 2][:, m * NC_:(m + 1) * NC_], chunks(wk, m), cc)
                    if fc is not None:
                        for m in range(KD):
                            mm = product(sh[n % 2][:, 512 + m * NC_:512 + (m + 1) * NC_], chunks(wv, m), cc)
                if part == 1:
                    if fc is not None:
                        pe.wait_ge(sh_taken, n + 1)
                    for b in range(NB):
                        lhs = ([ctxT[:, k, b * C:(b + 1) * C] for k in range(KD)] if fc is None else
                               [Vt[:, k * NC_ + b * C:k * NC_ + (b + 1) * C] for k in range(KD)])
                        mm = product(sh[(n + 1) % 2][0:C, b * D:(b + 1) * D], lhs, chunks(wv if fc is None else fc))
                if part == 2:
                    pe.wait_ge(sh_taken, n + 1)
                    for m in range(KD):
                        mm = product(sh[n % 2][:, m * NC_:(m + 1) * NC_], chunks(wq, m),
                                     [kT[:, k * NC_:(k + 1) * NC_] for k in range(KD)])
                    mm = product(sh[n % 2][:, 512:512 + NC_], [folds[stage].bq[:, k * P:(k + 1) * P] for k in range(KD)],
                                 [kT[:, k * NC_:(k + 1) * NC_] for k in range(KD)])
                mm.then_inc(sh_full, 1)

            def logits(stage, b, r, k0, width):
                n, slot = b.fill("pt", stage, k0)
                pt_slot(n)
                product(pt[slot][0:width, :], [gw[:, r, k, 0:width] for k in range(KD)],
                        [T(stage, b)[:, k, :] for k in range(KD)]).then_inc(pt_full, 1)

            def logits_moved(stage, b, k0):
                pe.wait_ge(pt_moved, b.fill("pt", stage, k0)[0] + 1)

            def logits_T(stage, b, k0, width):
                n, slot = b.fill("pt", stage, k0)
                transposes(n, slot, [((P, j * width, (j + 1) * width), lgT[0:width, j * P:(j + 1) * P]) for j in range(TB)], waited=True)

            def experts(stage, r, width, pieces):
                nth = stage // 4
                w_up, w_back = (wA, wB) if stage == 3 else (wB, wA)
                s_up = (sB,) if stage == 3 else (sC, sB)
                s_back = sC if stage == 3 else sA

                def both(w, at, n):
                    return w[:, 0, at:at + n], w[:, 1, at:at + n]

                def up(b, e, between=None):
                    n, slot = b.fill("sh", stage, e)
                    par = (b.fill("ln", stage)[1] + 1) % 2
                    sh_slot(n)
                    for f in range(2):
                        if f == 1 and between:
                            between()
                        if e < NE:
                            lhs = [both(w_up, (2 * e + k) * D + f * P, P) for k in range(KD)]
                        elif stage == 3:
                            lhs = [both(sB, k * D + f * P, P) for k in range(KD)]
                        else:
                            lhs = [both(s_up[f], k * D + (e - NE) * P, P) for k in range(KD)]
                        mm = product(sh[slot][:, f * S:(f + 1) * S],
                                     *halves(lhs, [both(xnTR[:, par], k * S, S) for k in range(KD)]))
                    mm.then_inc(sh_full, 1)

                def back(b, e):
                    pe.wait_ge(h_lo, halvings(stage, b, e))
                    h = hidR[:, (b.u * (NE + 1) + e) % 2]
                    for pair in range(2):
                        n, slot = b.fill("o", stage, 2 * e + pair)
                        o_slot(n)
                        for q in range(2):
                            j = 2 * pair + q
                            rhs = [both(w_back, (2 * e + f) * D, D) if e < NE else both(s_back, f * D, D) for f in range(2)]
                            mm = product(ob[slot][:, q * D:(q + 1) * D],
                                         *halves([both(h, f * S + j * P, P) for f in range(2)], rhs))
                        mm.then_inc(o_full, 1)

                def body(b):
                    pe.wait_ge(x_lo, b.scaled(1, 5 * nth + 1))
                    up(b, 0)
                    logits(stage, b, r, 0, width)
                    up(b, 1, lambda: logits_moved(stage, b, 0))
                    logits_T(stage, b, 1, width)
                    if stage == 7:
                        pe.wait_ge(w_lo, NE + 3)
                    for e in range(NE + 1):
                        if e + 2 < pieces:
                            up(b, e + 2)
                        if e == 2:
                            norm_T(stage, b, 2)
                        back(b, e)
                blocks_of(pe, body)

            pe.wait_ge(const_made, 7)
            pe.wait_ge(in_ctx, 48)
            transposes(0, 0, [((P, k * NC_ + t * P, k * NC_ + (t + 1) * P), xin[:, t * D + k * P:t * D + (k + 1) * P])
                              for k in range(KD) for t in range(2)])
            pe.wait_ge(c_done, 1)
            transposes(1, 1, [((P, k * NC_ + t * P, k * NC_ + (t + 1) * P), xn[:, t * D + k * P:t * D + (k + 1) * P])
                              for k in range(KD) for t in range(2)])
            pe.wait_ge(pt_moved, 1)
            fold16(0, ctxT, in_wk, in_wv, in_wq, in_wo, 16)
            first_norm_T(6, 1)
            pe.wait_ge(pt_moved, 8)
            attend16(0)

            n = start_of("pt", 1) - 2
            pe.wait_ge(q_int, 14)
            for w in range(2):
                for k in range(KD):
                    transposes(n, n % 2,
                               [((P, c * P, c * P + (RFQ if c == NFQ - 1 else P)),
                                 qint[0:(RFQ if c == NFQ - 1 else P), (w * NFQ + c) * D + k * P:(w * NFQ + c) * D + (k + 1) * P])
                                for c in range(NFQ)], identb, BF16)
                    n += 1
            o = 2 * NFQ * D
            for cs in (range(0, 4), range(4, NFQ)):
                transposes(n, n % 2,
                           [((RFQ if c == NFQ - 1 else P, (c - cs[0]) * D + h * P, (c - cs[0]) * D + (h + 1) * P),
                             qint[:, o + h * FQ + c * P:o + h * FQ + min((c + 1) * P, FQ)])
                            for c in cs for h in range(KD)], identb, BF16)
                n += 1
            pt_slot(n)
            pe.wait_ge(q_diag, 1)
            for h in range(KD):
                mm = pe.matmul(pt[n % 2][:, h * P:(h + 1) * P], ones[:, :], xn[:, h * P:(h + 1) * P], start=True, stop=True)
            mm.then_inc(pt_full, 1)
            n += 1
            for b in range(NB):
                pe.wait_ge(x_int, b + 1)
                transposes(n, n % 2, [((P, k * S + j * P, k * S + (j + 1) * P),
                                       xqi[:, (b % 2) * 1024 + j * D + k * P:(b % 2) * 1024 + j * D + (k + 1) * P])
                                      for k in range(KD) for j in range(TB)], identb, BF16)
                n += 1
            pe.wait_ge(pt_moved, n)

            def gate_up(b):
                for f in range(NFQ):
                    pe.wait_ge(gu_half, b.scaled(NFQ, f + 1))
                    for w, wT in ((0, wgT), (1, wuT)):
                        mm = product(gu[(b.u * NFQ + f) % 4][w], [wT[:, k, f * P:(f + 1) * P] for k in range(KD)],
                                     [xqT[:, k, bass.ds(b.scaled(S), S)] for k in range(KD)])
                    mm.then_inc(gu_full, 1)
            pe.wait_ge(o_added, start_of("o", 1))
            blocks_of(pe, gate_up)
            pe.wait_ge(in_c, 16 * 9)
            pe.wait_ge(gu_half, 4 + NB * NFQ)
            n = start_of("pt", 2) - 6
            weight_T(n, w1h[0])
            w2 = (fold2.wT[0], w1h[1], w1h[2])
            fold1(2, 0, *w2)
            fold1(2, 1, *w2)
            pe.wait_ge(pt_moved, n + 1)
            fold1(2, 2, *w2)
            w4 = (w1h[3], *fold4.wT)
            for b in straight:
                pe.wait_ge(hq_ready, b.u + 1)
                for pair in range(2):
                    n, slot = b.fill("o", 1, pair)
                    o_slot(n)
                    for q in range(2):
                        j = 2 * pair + q
                        for f in range(NFQ):
                            r = RFQ if f == NFQ - 1 else P
                            mm = pe.matmul(ob[slot][:, q * D:(q + 1) * D],
                                           hq[b.u % 2][0:r, f * S + j * P:f * S + (j + 1) * P],
                                           wdT[0:r, f, :], start=(f == 0), stop=(f == NFQ - 1))
                    mm.then_inc(o_full, 1)
                if b.u == 0:
                    for q in range(3):
                        weight_T(start_of("pt", 2) - 5 + q, w1h[4 + q])
                if b.u == 1:
                    pe.wait_ge(pt_moved, start_of("pt", 2) - 2)
                if b.u == 1 or b.u == 2:
                    fold1(4, b.u - 1, *w4)
            first_norm_T(start_of("pt", 2) - 2, start_of("ln", 2))
            fold1(4, 2, *w4)
            attend1(2)
            n = start_of("pt", 3)
            pe.wait_ge(in_wexp, 48)
            for g in range(2):
                weight_T(n, natc[:, g * 512:(g + 1) * 512])
                n += 1
            pe.wait_ge(pt_moved, n)
            pe.wait_ge(wt_lo, 2 * NE)
            experts(3, 0, NE, NE + 1)
            attend1(4)
            def expert5(b):
                pe.wait_ge(pt_moved, b.fill("pt", 5, 0)[0])
                logits(5, b, 1, 0, NE)
                for pair in range(2):
                    n, slot = b.fill("o", 5, pair)
                    o_slot(n)
                    for q in range(2):
                        j = 2 * pair + q
                        if j == 1:
                            logits_moved(5, b, 0)
                        mm = product(ob[slot][:, q * D:(q + 1) * D],
                                     [T(5, b)[:, k, j * P:(j + 1) * P] for k in range(KD)] + [ones[0:1, :]],
                                     [wexp[:, k * D:(k + 1) * D] for k in range(KD)] + [be2[0:1, :]])
                    mm.then_inc(o_full, 1)
                    if pair == 0:
                        logits_T(5, b, 1, NE)
                        norm_T(5, b, 2)
                        n, slot = b.fill("pt", 5, 4)
                        pe.wait_ge(hot_ready, b.scaled(1, 1))
                        pt_slot(n)
                        hot = ohb[:, :, :].rearrange("p j e -> p (j e)")
                        pe.matmul(pt[slot][:, 0:TB * NE], triu[:, :], hot, start=True, stop=False)
                        for k in range(1, TB):
                            pe.matmul(pt[slot][:, k * NE:TB * NE], onesb[:, :], hot[:, 0:(TB - k) * NE], start=False,
                                      stop=(k == TB - 1))
                        for k in range(TB):
                            mm = pe.matmul(pt[slot][:, TB * NE:(TB + 1) * NE], onesb[:, :], hot[:, k * NE:(k + 1) * NE],
                                           start=(k == 0), stop=(k == TB - 1))
                        mm.then_inc(pt_full, 1)
            blocks_of(pe, expert5)
            fold16(6, ctxnT, in_w6, in_w6, in_w6, in_w6, 64)
            attend16(6)
            pe.wait_ge(raw_split, 4)
            experts(7, 2, NE + 1, NE + 2)

        @block.scalar
        def _(act):
            def full(n):
                act.wait_ge(pt_full, n + 1)

            def move(n, slot, dst, r=P, cols_=512, cast=None):
                full(n)
                src = pt[slot][:, :] if cast is None else pt[slot][:, :].bitcast(cast)
                act.copy(dst, src[0:r, 0:cols_]).then_inc(pt_moved, 1)

            def norm_move(stage, b, k0, to_stage=None):
                par = b.fill("ln", stage)[1]
                for k in range(KD):
                    n, slot = b.fill("pt", stage, k0 + k)
                    full(n)
                    if (to_stage or stage) == 6:
                        act.activation(xnT[:, par, k, :], pt[slot][:, :], ACT.Identity, bias=cols[:, 12 + k:13 + k],
                                       scale=cols[:, 10 + k:11 + k]).then_inc(pt_moved, 1)
                    else:
                        act.copy(xnT[:, par, k, :], pt[slot][:, :]).then_inc(pt_moved, 1)

            def first_norm_move(n0, par):
                for k in range(KD):
                    move(n0 + k, (n0 + k) % 2, xnT[:, par, k, :])

            def fold16(stage):
                n0 = start_of("sh", stage)
                for e in range(4):
                    act.wait_ge(sh_full, n0 + e + 1)
                    src = sh[(n0 + e) % 2][:, 0:512]
                    if e < 2:
                        act.activation(kT16[:, e * 1024:e * 1024 + 512], src, ACT.Copy, scale=DH ** -0.5).then_inc(sh_half, 1)
                    else:
                        for j in range(2):
                            a = act.copy(vD16[64 * j:64 * j + 64, 4 * e - 8:4 * e - 6, :, j, :],
                                         src[64 * j:64 * j + 64, :].rearrange("p (m b c) -> p m b c", m=2, b=NB))
                        a.then_inc(sh_half, 1)
                p0 = wq_fills(stage)
                for f in range(4):
                    move(p0 + f, (p0 + f) % 2, wqT16[:, f * 512:(f + 1) * 512])
                for m in range(MI):
                    n = n0 + 4 + m
                    act.wait_ge(sh_full, n + 1)
                    act.copy(keysA.rearrange("p (kb h c) -> p kb h c", kb=KD * NB, h=H)[:, :, 2 * m, :],
                             sh[n % 2][:, 0:512].rearrange("p (kb c) -> p kb c", c=C)).then_inc(sh_half, 1)
                if stage == 0:
                    act.wait_ge(in_small, 16 * 24)
                    act.activation(gates[:, :], gates[:, :], ACT.Tanh)
                    act.activation(clips[:, :], clips[:, :], ACT.Tanh, scale=0.5)
                    act.drain()
                    act.copy(qs[:, 14:16], clips[:, :]).then_inc(gates_ready, 1)
                for m in range(MI):
                    n = n0 + 12 + m
                    act.wait_ge(sh_full, n + 1)
                    dst = valsO[:, m * NB * D:(m * NB + 2) * D]
                    if m == 0:
                        act.copy(dst, sh[n % 2][:, 0:512]).then_inc(sh_half, 1)
                    else:
                        act.activation(dst, sh[n % 2][:, 0:512], ACT.Identity, bias=0.0,
                                       scale=gates[:, stage // 2:stage // 2 + 1]).then_inc(sh_half, 1)

            def attend16(stage):
                def exps(i):
                    if stage == 0:
                        act.wait_ge(shifted[stage], i + 1)
                    else:
                        act.wait_ge(sh_taken, Block(i // TB).fill("sh", stage, i % TB)[0] + 1)
                    act.activation(prob[i % 2], prob[i % 2], ACT.Exp).then_inc(exped[stage], 1)
                exps(0)
                for b in straight:
                    for j in range(TB):
                        i = b.u * TB + j
                        if i + 1 < NT:
                            exps(i + 1)
                        next_norm = stage == 6 or b.u + 1 < NB
                        k0 = 2 * j if j < 2 or not next_norm else 2 * j + 2
                        for half in range(2):
                            n, slot = b.fill("pt", stage, k0 + half)
                            move(n, slot, probT[:, half * 512:(half + 1) * 512])
                        if j == 1 and next_norm:
                            norm_move(stage, b, 4, stage if b.u + 1 < NB else 7)

            def attend1(stage):
                def exps(u):
                    act.wait_ge(shifted[stage], u + 1)
                    act.activation(prob[u % 2][:, 0:TB * C], prob[u % 2][:, 0:TB * C], ACT.Exp).then_inc(exped[stage], 1)

                def weights(b, which):
                    for q in which if stage == 2 else ():
                        g = 4 * b.u + q
                        if g >= 2:
                            act.wait_ge(wt_lo, g - 1)
                        n, slot = b.fill("pt", 2, 3 + q)
                        full(n)
                        act.copy(split2[g][0], pt[slot][:, :])
                        act.copy(moved_T[g % 2], pt[slot][:, :]).then_inc(pt_moved, 1)

                exps(0)
                for b in straight:
                    norm_move(stage, b, 0)
                    n, slot = b.fill("pt", stage, 2)
                    move(n, slot, probT[0:C, (b.u % 2) * S:(b.u % 2) * S + S], r=C)
                    weights(b, (0, 1))
                    if b.u + 1 < NB:
                        exps(b.u + 1)
                    weights(b, (2, 3))

            def experts(stage, width, pieces):
                nth = stage // 4

                def x_high(par):
                    act.copy(xnTR[:, par, 0, :], xnT[:, par, :, :].rearrange("p k t -> p (k t)")).then_inc(x_hi, 1)

                def lead(b, e):
                    n, slot = b.fill("sh", stage, e)
                    if e <= NE:
                        act.wait_ge(h_lo, halvings(stage, b, e - 3))
                    act.wait_ge(sh_full, n + 1)
                    wide = 2 * S if e < NE or stage == 3 else S
                    act.activation(hid[e % 3][:, 0:wide], sh[slot][:, 0:wide],
                                   ACT.Relu if stage == 3 else ACT.Tanh, scale=1.0 if stage == 3 else 0.5
                                   ).then_inc(act_done[stage], 1)

                def high(b, e, part=slice(0, 2 * S)):
                    piece = NE + 1 if e == NE and stage == 7 and part.start > 0 else e
                    act.wait_ge(sh_taken, b.fill("sh", stage, piece)[0] + 1)
                    act.wait_ge(o_full, b.scaled(2 * (NE + 1), start_of("o", stage) + 2 * (e - 1)))
                    act.copy(hidR[:, (b.u * (NE + 1) + e) % 2, 0, part], hid[e % 3][:, part]).then_inc(h_hi, 1)

                act.wait_ge(o_full, start_of("o", stage))
                x_high((start_of("ln", stage) + 1) % 2)
                if stage == 7:
                    act.wait_ge(in_s7, 32)
                    for dst, src in split7:
                        act.copy(dst[0], src).then_inc(w_hi, 1)

                def body(b):
                    lead(b, 0)
                    n, slot = b.fill("pt", stage, 0)
                    move(n, slot, lgT[0:width, :], r=width)
                    high(b, 0)
                    lead(b, 1)
                    n, slot = b.fill("pt", stage, 1)
                    full(n)
                    act.copy(lg[:, :, 0:width], pt[slot][:, 0:TB * width].rearrange("p (j e) -> p j e", j=TB)).then_inc(pt_moved, 1)
                    if stage == 3:
                        act.drain()
                        act.activation(th[:, :, 0:NE], lg[:, :, 0:NE], ACT.Tanh, scale=0.5).then_inc(router_act, 1)
                    for e in range(NE + 1):
                        if e == NE and stage == 7:
                            high(b, e, slice(0, S))
                            high(b, e, slice(S, 2 * S))
                        elif e > 0:
                            high(b, e)
                        if e + 2 < pieces:
                            lead(b, e + 2)
                        if e == 0 and stage == 7:
                            act.wait_ge(router_in, b.scaled(1, 4 + 1))
                            act.activation(ws[:, :, :], ws[:, :, :], ACT.Exp).then_inc(router_act, 1)
                            act.activation(th[:, :, NE:NE + 1], lg[:, :, NE:NE + 1], ACT.Tanh, scale=0.5).then_inc(router_act, 1)
                        if e == 2:
                            norm_move(stage, b, 2)
                            act.drain()
                            x_high(b.fill("ln", stage)[1])
                blocks_of(act, body)

            full(0)
            act.copy(ctxT[:, :, :].rearrange("p k c -> p (k c)"), pt[0][:, :]).then_inc(pt_moved, 1)
            act.wait_ge(in_ctx, 48)
            full(1)
            for k in range(KD):
                a = act.activation(ctxnT[:, k, :], pt[1][:, k * NC_:(k + 1) * NC_], ACT.Identity,
                                   bias=cols2[:, 2 + k:3 + k], scale=cols2[:, k:k + 1])
            a.then_inc(pt_moved, 1)
            fold16(0)
            first_norm_move(6, 0)
            attend16(0)
            n = start_of("pt", 1) - 2
            for w, wT in ((0, wgT), (1, wuT)):
                for k in range(KD):
                    move(n, n % 2, wT[:, k, 0:FQ], cols_=FQ, cast=BF16)
                    n += 1
            move(n, n % 2, wdT[:, 0:4, :].rearrange("p f d -> p (f d)"), cols_=4 * D, cast=BF16)
            n += 1
            full(n)
            act.copy(wdT[:, 4, :], pt[n % 2][:, :].bitcast(BF16)[:, 0:D])
            act.copy(wdT[0:RFQ, 5, :], pt[n % 2][:, :].bitcast(BF16)[0:RFQ, D:2 * D]).then_inc(pt_moved, 1)
            n += 1
            move(n, n % 2, sdb, cols_=D)
            n += 1
            def x_integers(b):
                act.wait_ge(x_clip, b + 1)
                if b >= 2:
                    act.wait_ge(pt_full, n + b - 1)
                act.activation(xqi[:, (b % 2) * 1024:(b % 2) * 1024 + 1024], xn_all[:, b * TB * D:(b + 1) * TB * D],
                               ACT.Copy, bias=-MAGIC).then_inc(x_int, 1)
            x_integers(0)
            x_integers(1)
            for b in range(NB):
                full(n + b)
                act.copy(xqT[:, :, b * S:(b + 1) * S],
                         pt[(n + b) % 2][:, :].bitcast(BF16).rearrange("p (k t) -> p k t", k=KD)).then_inc(pt_moved, 1)
                if b + 2 < NB:
                    x_integers(b + 2)
            act.wait_ge(q_scaled, 1)

            def gate_tanh(b):
                for f in range(NFQ):
                    slot = (b.u * NFQ + f) % 4
                    r = RFQ if f == NFQ - 1 else P
                    act.wait_ge(gu_full, b.scaled(NFQ, f + 1))
                    act.wait_ge(gu_taken, b.scaled(NFQ, f + 1))
                    act.activation(gate_t[slot][0:r, :], gu[slot][0][0:r, :], ACT.Tanh, scale=qw[0:r, 0, f:f + 1])
                    act.activation(up_s[slot][0:r, :], gu[slot][1][0:r, :], ACT.Identity, bias=0.0,
                                   scale=qw[0:r, 2, f:f + 1]).then_inc(act_done[1], 1)
            blocks_of(act, gate_tanh)
            n = start_of("pt", 2) - 6
            move(n, n % 2, fold2.wT[0])
            for b in range(NB):
                if b == 2:
                    for q in range(3):
                        move(n + 1 + q, (n + 1 + q) % 2, fold4.wT[q])
                act.wait_ge(h_clip, b + 1)
                if b >= 2:
                    act.wait_ge(o_full, straight[b - 2].fill("o", 1, 1)[0] + 1)
                act.activation(hq[b % 2].rearrange("p (f t) -> p f t", f=NFQ), hall[:, :, b * S:(b + 1) * S],
                               ACT.Copy, bias=-MAGIC).then_inc(hq_ready, 1)
            first_norm_move(start_of("pt", 2) - 2, (start_of("ln", 2) - 1) % 2)
            attend1(2)
            n = start_of("pt", 3)
            for dst in split3:
                full(n)
                act.copy(dst[0], pt[n % 2][:, :]).then_inc(w_hi, 1)
                n += 1
            experts(3, NE, NE + 1)
            attend1(4)
            for b in straight:
                n, slot = b.fill("pt", 5, 0)
                move(n, slot, lgT[0:NE, :], r=NE)
                n, slot = b.fill("pt", 5, 1)
                full(n)
                act.copy(lg[:, :, 0:NE], pt[slot][:, 0:TB * NE].rearrange("p (j e) -> p j e", j=TB)).then_inc(pt_moved, 1)
                act.wait_ge(router_in, b.u + 1)
                act.activation(ws[:, :, :], ws[:, :, :], ACT.Exp).then_inc(router_act, 1)
                norm_move(5, b, 2, 6 if b.u == NB - 1 else 5)
                n, slot = b.fill("pt", 5, 4)
                move(n, slot, cnt[:, :], cols_=(TB + 1) * NE)
            fold16(6)
            attend16(6)
            experts(7, NE + 1, NE + 2)

        @block.vector
        def _(dve):
            def tiles_of(b, t, k):
                return bass.ds(b.scaled(TB * k, t * k), k)

            def norm_stats(b, tile=None, tiles=TB, signal=None):
                dve.drain()
                for j in range(tiles):
                    dve.bn_stats(stats[:, j, :], tile(j) if tile else xt(b, j))
                dve.drain()
                for j in range(tiles):
                    dve.bn_aggr(mvb[:, j, :], stats[:, j, :])
                dve.drain()
                n = bass.ds(b.scaled(TB), tiles)
                dve.tensor_copy(mv[:, n, :], mvb[:, 0:tiles, :])
                dve.tensor_scalar(var[:, n], mvb[:, 0:tiles, 1], EPS, None, ALU.add).then_inc(signal or ln_var, 1)

            def apply_norm(dst, src, b, tiles):
                for j in range(tiles):
                    n = tiles_of(b, j, 1)
                    ins = dve.tensor_scalar(dst(j), src(j), mv[:, n, 0], rstd[:, n], ALU.subtract, ALU.mult)
                return ins

            def xn_tile(j):
                return xn[:, j * D:(j + 1) * D]

            class Wrapped:

                def __init__(self, b):
                    self.b = b

                def scaled(self, k, plus=0):
                    if self.b.i is None or self.b.u == 0:
                        return Block((self.b.u + 1) % NB, self.b.i).scaled(k, plus)
                    return self.b.i * (-2 * k) + (2 * k + plus)

            def norm_next(stage, b, free):
                nxt = Wrapped(b)
                dve.wait_ge(ln_rstd, b.scaled(1, stage * NB + 2))
                dve.wait_ge(pt_full, free)
                apply_norm(xn_tile, lambda j: x[:, tiles_of(nxt, j, D)], nxt, TB).then_inc(ln_done, 1)

            def xn_free(stage, b, k):
                per = PER["pt"][stage]
                if b.i is None and b.u == 0:
                    return start_of("pt", stage)
                return b.scaled(per, start_of("pt", stage) + PRE["pt"][stage] - per + k + 1)

            def add(b, stage, k, tiles, weight=None):
                n, slot = b.fill("o", stage, k)
                dve.wait_ge(o_full, n + 1)
                for q, j in enumerate(tiles):
                    o = ob[slot][:, q * D:(q + 1) * D]
                    if weight is None:
                        ins = dve.tensor_tensor(xt(b, j), o, xt(b, j), ALU.add)
                    else:
                        ins = dve.scalar_tensor_tensor(xt(b, j), o, weight(j), xt(b, j), ALU.mult, ALU.add)
                ins.then_inc(o_added, 1)

            def fold16(stage, bias, between={}):
                n0 = start_of("sh", stage)
                g = gates[:, stage // 2:stage // 2 + 1]
                half0 = PRE["sh"][0] * (stage // 6)

                def off_diagonal(j):
                    dve.memset(vD16[64 * j:64 * j + 64, :, :, 1 - j, :], 0.0)
                if stage == 0:
                    for j in range(2):
                        off_diagonal(j)
                for e in range(4):
                    dve.wait_ge(sh_full, n0 + e + 1)
                    dve.wait_ge(sh_half, half0 + e + 1)
                    src = sh[(n0 + e) % 2][:, 512:1024]
                    if e < 2:
                        dve.tensor_scalar(kT16[:, e * 1024 + 512:e * 1024 + 1024], src, DH ** -0.5, None,
                                          ALU.mult).then_inc(sh_taken, 1)
                    else:
                        for j in range(2):
                            ins = dve.tensor_copy(vD16[64 * j:64 * j + 64, 4 * e - 6:4 * e - 4, :, j, :],
                                                  src[64 * j:64 * j + 64, :].rearrange("p (m b c) -> p m b c", m=2, b=NB))
                        ins.then_inc(sh_taken, 1)
                    between.get(e, nothing)()
                for m in range(MI):
                    n = n0 + 4 + m
                    dve.wait_ge(sh_full, n + 1)
                    dve.wait_ge(sh_half, half0 + 4 + m + 1)
                    dve.tensor_copy(keysA.rearrange("p (kb h c) -> p kb h c", kb=KD * NB, h=H)[:, :, 2 * m + 1, :],
                                    sh[n % 2][:, 512:1024].rearrange("p (kb c) -> p kb c", c=C)).then_inc(sh_taken, 1)
                    if m < 2 and stage == 6:
                        off_diagonal(m)
                    between.get(4 + m, nothing)()
                for m in range(MI):
                    n = n0 + 12 + m
                    dve.wait_ge(sh_full, n + 1)
                    dve.wait_ge(sh_half, half0 + 12 + m + 1)
                    v = valsO[:, m * NB * D:(m + 1) * NB * D]
                    if m == 0:
                        dve.tensor_copy(v[:, 512:1024], sh[n % 2][:, 512:1024])
                        dve.drain()
                        v0 = v[0:64, :].rearrange("p (b d) -> p b d", b=NB)
                        dve.tensor_tensor(v0, v0, bias[0:64, :].unsqueeze(1).broadcast_to([64, NB, D]), ALU.add)
                        dve.drain()
                        dve.tensor_scalar(v, v, g, None, ALU.mult).then_inc(sh_taken, 1)
                    else:
                        dve.tensor_scalar(v[:, 512:1024], sh[n % 2][:, 512:1024], g, None, ALU.mult).then_inc(sh_taken, 1)
                    between.get(12 + m, nothing)()

            def nothing():
                pass

            def heads(a):
                return a.rearrange("p (h c) -> p h c", h=H)

            def over_keys(a, n=H):
                return a.unsqueeze(2).broadcast_to([P, n, C])

            def extremes(b):
                xb = x[:, b.u * TB * D:(b.u + 1) * TB * D].rearrange("p (t d) -> p t d", t=TB)
                for k, op in enumerate((ALU.max, ALU.min)):
                    dve.tensor_reduce(xmm[:, k, b.u * TB:(b.u + 1) * TB], xb, AX.X, op)

            def attend16(stage):
                def shift(i):
                    b, j = Block(i // TB), i % TB
                    n, slot = b.fill("sh", stage, j)
                    dve.wait_ge(sh_full, n + 1)
                    p = prob[i % 2]
                    if stage == 0:
                        dve.scalar_tensor_tensor(heads(p), mask[:, i, :].unsqueeze(1).broadcast_to([P, H, C]), -FMAX,
                                                 heads(sh[slot][:, :]), ALU.mult, ALU.add).then_inc(sh_taken, 1)
                        dve.drain()
                        dve.tensor_reduce(mx[:, i % 2, :], heads(p), AX.X, ALU.max)
                        dve.drain()
                        dve.tensor_tensor(heads(p), heads(p), over_keys(mx[:, i % 2, :]), ALU.subtract).then_inc(shifted[stage], 1)
                    else:
                        dve.tensor_scalar(p, sh[slot][:, :], -11.0, 11.0, ALU.max, ALU.min).then_inc(sh_taken, 1)

                def normalise(i):
                    p = prob[i % 2]
                    dve.wait_ge(exped[stage], i + 1)
                    dve.tensor_reduce(sm[:, i % 2, :], heads(p), AX.X, ALU.add)
                    dve.drain()
                    dve.reciprocal(rsm[:, i % 2, :], sm[:, i % 2, :])
                    dve.drain()
                    dve.tensor_tensor(heads(p), heads(p), over_keys(rsm[:, i % 2, :]), ALU.mult).then_inc(prob_ready[stage], 1)

                shift(0)
                normalise(0)
                for b in straight:
                    for j in range(TB):
                        i = b.u * TB + j
                        if i + 1 < NT:
                            shift(i + 1)
                        if i >= 1:
                            pb, pj = Block((i - 1) // TB), (i - 1) % TB
                            add(pb, stage, pj, [pj])
                            if pj == TB - 1:
                                norm_stats(pb)
                                if stage == 0:
                                    extremes(pb)
                        if i + 1 < NT:
                            normalise(i + 1)
                        if j == 1 and (stage == 6 or b.u + 1 < NB):
                            norm_next(stage, b, xn_free(stage, b, 5))
                add(straight[-1], stage, TB - 1, [TB - 1])
                norm_stats(straight[-1])
                if stage == 0:
                    extremes(straight[-1])

            def attend1(stage):
                def shift(b):
                    n, slot = b.fill("sh", stage)
                    dve.wait_ge(sh_full, n + 1)
                    p = prob[b.u % 2][:, 0:TB * C].rearrange("p (j c) -> p j c", j=TB)
                    m = mx[:, b.u % 2, 0:TB]
                    cb = folds[stage].cb[:, b.u * C:(b.u + 1) * C]
                    dve.tensor_tensor(p, sh[slot][:, 0:TB * 2 * C].rearrange("p (j b c) -> p j b c", j=TB, b=2)[:, :, b.u % 2, :],
                                      cb.unsqueeze(1).broadcast_to([P, TB, C]), ALU.add).then_inc(sh_taken, 1)
                    if stage == 4:
                        dve.drain()
                        r = rowf[:, b.u * TB:(b.u + 1) * TB]
                        dve.tensor_tensor(p, p, over_keys(r, TB), ALU.mult)
                        dve.drain()
                        dve.tensor_scalar(nmx[:, :], r, 1.0e10, -1.0e10, ALU.mult, ALU.add)
                        dve.drain()
                        dve.tensor_tensor(p, p, over_keys(nmx[:, :], TB), ALU.add)
                    dve.drain()
                    dve.tensor_reduce(m, p, AX.X, ALU.max)
                    dve.drain()
                    dve.tensor_tensor(p, p, over_keys(m, TB), ALU.subtract).then_inc(shifted[stage], 1)

                def finish(b):
                    for pair in range(2):
                        add(b, stage, pair, [2 * pair, 2 * pair + 1])
                    norm_stats(b)

                shift(straight[0])
                for b in straight:
                    norm_next(stage, b, xn_free(stage, b, 1))
                    p = prob[b.u % 2][:, 0:TB * C].rearrange("p (j c) -> p j c", j=TB)
                    s, r = sm[:, b.u % 2, 0:TB], rsm[:, b.u % 2, 0:TB]
                    dve.wait_ge(exped[stage], b.u + 1)
                    dve.tensor_reduce(s, p, AX.X, ALU.add)
                    dve.drain()
                    dve.reciprocal(r, s)
                    dve.drain()
                    dve.tensor_tensor(p, p, over_keys(r, TB), ALU.mult).then_inc(prob_ready[stage], 1)
                    if b.u >= 1:
                        finish(straight[b.u - 1])
                    if b.u + 1 < NB:
                        shift(straight[b.u + 1])
                finish(straight[-1])

            def fold1(stage, part):
                n = start_of("sh", 1) + PRE["sh"][1] - 6 + (0 if stage == 2 else 3)
                g = gates[:, stage // 2:stage // 2 + 1]
                F = folds[stage]
                bq, bk = (cols[:, 0:2], cols[:, 2:4]) if stage == 2 else (cols[:, 4:6], cols[:, 6:8])
                if part == 0:
                    for k in range(KD):
                        dve.tensor_scalar(F.bq[:, k * P:(k + 1) * P], ones[:, :], bq[:, k:k + 1], None, ALU.mult)
                    dve.wait_ge(sh_full, n + 1)
                    for k in range(KD):
                        ins = dve.tensor_scalar(F.kT[:, k * NC_:(k + 1) * NC_], sh[n % 2][:, k * NC_:(k + 1) * NC_],
                                                bk[:, k:k + 1], None, ALU.add)
                    if stage == 4:
                        for k in range(KD):
                            ins = dve.tensor_scalar(F.Vt[:, k * NC_:(k + 1) * NC_],
                                                    sh[n % 2][:, 512 + k * NC_:512 + (k + 1) * NC_],
                                                    cols[:, 8 + k:9 + k], None, ALU.add)
                    ins.then_inc(sh_taken, 1)
                if part == 1:
                    dve.wait_ge(sh_full, n + 2)
                    bias = (bv1 if stage == 2 else bfc2)[0:C, :].unsqueeze(1).broadcast_to([C, 2, D])
                    for h in range(2):
                        dve.tensor_tensor(F.V[0:C, h * 512:(h + 1) * 512].rearrange("p (b d) -> p b d", b=2),
                                          sh[(n + 1) % 2][0:C, h * 512:(h + 1) * 512].rearrange("p (b d) -> p b d", b=2),
                                          bias, ALU.add)
                    dve.drain()
                    dve.tensor_scalar(F.V[0:C, :], F.V[0:C, :], g[0:C, :], None, ALU.mult).then_inc(sh_taken, 1)
                if part == 2:
                    dve.wait_ge(sh_full, n + 3)
                    dve.tensor_scalar(F.A, sh[n % 2][:, 0:512], D ** -0.5, None, ALU.mult)
                    dve.tensor_scalar(F.cb, sh[n % 2][:, 512:512 + NC_], D ** -0.5, None, ALU.mult).then_inc(sh_taken, 1)

            def top(src):
                for j in range(TB):
                    dve.max(v8[:, j, :], src[:, j, 0:NE])
                dve.drain()

            def onehot(dst, which):
                dve.tensor_tensor(dst, iota8[:, :].unsqueeze(1).broadcast_to([P, TB, NE]),
                                  i8f[:, :, which].unsqueeze(2).broadcast_to([P, TB, NE]), ALU.is_equal)

            def places(src, n):
                for j in range(TB):
                    dve.max_index(i8[:, j, :], v8[:, j, :], src[:, j, 0:NE])
                dve.drain()
                dve.tensor_copy(i8f[:, :, 0:n], i8[:, :, 0:n])
                dve.drain()
                onehot(oh[:, :, :], 0)
                if n == 2:
                    onehot(oh2[:, :, :], 1)
                    dve.drain()
                    dve.tensor_tensor(oh[:, :, :], oh[:, :, :], oh2[:, :, :], ALU.add)
                dve.drain()

            def per_tile(a, n=NE):
                return a.unsqueeze(2).broadcast_to([P, TB, n])

            def softmax_shift(src):
                top(src)
                dve.tensor_tensor(ws[:, :, :], src[:, :, 0:NE], per_tile(v8[:, :, 0]), ALU.subtract).then_inc(router_in, 1)

            def softmax_probs(acts):
                dve.wait_ge(router_act, acts)
                dve.tensor_reduce(sr[:, 0, :], ws[:, :, :], AX.X, ALU.add)
                dve.drain()
                dve.reciprocal(sr[:, 1, :], sr[:, 0, :])
                dve.drain()
                dve.tensor_tensor(ws[:, :, :], ws[:, :, :], per_tile(sr[:, 1, :]), ALU.mult)
                dve.drain()

            def rest(dst, src, n, done):
                dve.wait_ge(w_hi, n)
                dve.tensor_tensor(dst[1], src, dst[0].bitcast(F32), ALU.subtract).then_inc(done, 1)

            def experts(stage, pieces):
                def hidden(b, e):
                    n, slot = b.fill("sh", stage, e)
                    g, r = sh[slot], hid[e % 3]
                    dve.wait_ge(act_done[stage], b.scaled(pieces, e + 1))
                    if stage == 3:
                        ins = dve.scalar_tensor_tensor(r, g[:, :], 0.0, r, ALU.max, ALU.mult)
                    elif e < NE:
                        ins = dve.scalar_tensor_tensor(r, r, 1.0, g[:, :], ALU.add, ALU.mult)
                    else:
                        f = e - NE
                        dve.scalar_tensor_tensor(r[:, 0:S], r[:, 0:S], 1.0, g[:, 0:S], ALU.add, ALU.mult)
                        dve.drain()
                        ins = dve.tensor_tensor(hid[NE % 3][:, f * S:(f + 1) * S], g[:, S:2 * S], r[:, 0:S], ALU.mult)
                    ins.then_inc(sh_taken, 1)

                def route(b, part):
                    if stage == 3 and part == 0:
                        dve.wait_ge(pt_moved, b.fill("pt", stage, 1)[0] + 1)
                        dve.tensor_tensor(lb[:, :, :], lg[:, :, 0:NE], lb1[:, :].unsqueeze(1).broadcast_to([P, TB, NE]), ALU.add)
                        dve.drain()
                        top(lb)
                        places(lb, 2)
                    if stage == 3 and part == 1:
                        dve.wait_ge(router_act, b.scaled(1, 1))
                        dve.tensor_scalar(ws[:, :, :], th[:, :, 0:NE], 0.5, 0.5, ALU.mult, ALU.add)
                        dve.drain()
                        dve.tensor_tensor(ws[:, :, :], ws[:, :, :], oh[:, :, :], ALU.mult)
                        dve.drain()
                        dve.tensor_reduce(sr[:, 0, :], ws[:, :, :], AX.X, ALU.add)
                        dve.drain()
                        dve.tensor_scalar(sr[:, 0, :], sr[:, 0, :], 1e-6, None, ALU.add)
                        dve.drain()
                        dve.reciprocal(sr[:, 1, :], sr[:, 0, :])
                        dve.drain()
                        dve.tensor_scalar(sr[:, 2, :], sr[:, 1, :], gates[:, 5:6], None, ALU.mult)
                        dve.drain()
                        dve.tensor_tensor(wE[:, :, 0:NE], ws[:, :, :], per_tile(sr[:, 2, :]), ALU.mult)
                        dve.tensor_scalar(wE[:, :, NE:NE + 1], ones[:, 0:TB].unsqueeze(2), gates[:, 5:6], None, ALU.mult)
                        dve.drain()
                    if stage == 7 and part == 0:
                        dve.wait_ge(pt_moved, b.fill("pt", stage, 1)[0] + 1)
                        dve.tensor_copy(lb[:, :, :], lg[:, :, 0:NE])
                        dve.drain()
                        softmax_shift(lb)
                    if stage == 7 and part == 1:
                        softmax_probs(b.scaled(2, 8 + 2))
                        top(ws)
                        places(ws, 2)
                        dve.tensor_tensor(ws[:, :, :], ws[:, :, :], oh[:, :, :], ALU.mult)
                        dve.drain()
                        dve.tensor_scalar(wE[:, :, 0:NE], ws[:, :, :], gates[:, 7:8], 0.5, ALU.mult, ALU.mult)
                        dve.tensor_scalar(wE[:, :, NE:NE + 1], th[:, :, NE:NE + 1], 1.0, 0.25, ALU.add, ALU.mult)
                        dve.drain()
                        dve.tensor_scalar(wE[:, :, NE:NE + 1], wE[:, :, NE:NE + 1], gates[:, 7:8], None, ALU.mult)
                        dve.drain()

                def sums(b, e):
                    for pair in range(2):
                        add(b, stage, 2 * e + pair, [2 * pair, 2 * pair + 1], lambda j: wE[:, j, e:e + 1])

                def x_rest(par, n):
                    dve.wait_ge(x_hi, n)
                    dve.tensor_tensor(xnTR[:, par, 1, :], xnT[:, par, :, :].rearrange("p k t -> p (k t)"),
                                      xnTR[:, par, 0, :].bitcast(F32), ALU.subtract).then_inc(x_lo, 1)
                x_rest((start_of("ln", stage) + 1) % 2, 5 * (stage // 4) + 1)
                if stage == 7:
                    for q, (dst, src) in enumerate(split7):
                        rest(dst, src, len(split3) + q + 1, w_lo)

                def body(b):
                    hidden(b, 0)
                    hidden(b, 1)
                    for e in range(NE + 1):
                        if e == 0:
                            route(b, 0)
                        if e + 2 < pieces:
                            hidden(b, e + 2)
                        if e == 0:
                            route(b, 1)
                        sums(b, e)
                        if e == 1:
                            norm_next(stage, b, xn_free(stage, b, 3))
                        if e == 4:
                            x_rest(b.fill("ln", stage)[1], b.scaled(1, 5 * (stage // 4) + 2))
                    norm_stats(b)
                blocks_of(dve, body)

            dve.wait_ge(in_ctx, 48)
            norm_stats(Block(0), lambda j: xin[:, j * D:(j + 1) * D], 2, c_var)
            dve.wait_ge(c_rstd, 1)
            apply_norm(xn_tile, lambda j: xin[:, j * D:(j + 1) * D], Block(0), 2).then_inc(c_done, 1)

            def first_stats(b):
                dve.wait_ge(in_x, 16)
                norm_stats(b)

            def first_norm():
                dve.wait_ge(ln_rstd, 1)
                dve.wait_ge(pt_full, 2)
                apply_norm(xn_tile, lambda j: xt(straight[0], j), straight[0], TB).then_inc(ln_done, 1)

            def row_max(w):
                if w == 0:
                    dve.wait_ge(in_n, 16 * 5)
                    dve.memset(qw[:, :, :], 1.0)
                    dve.drain()
                if w < 2:
                    a = qnat[:, w * NFQ * D:(w + 1) * NFQ * D].rearrange("p (c n) -> p c n", c=NFQ)
                    dve.tensor_reduce(qw[:, 2 * w, 0:NFQ - 1], a[:, 0:NFQ - 1, :], AX.X, ALU.max, apply_absolute_value=True)
                    dve.tensor_reduce(qw[0:RFQ, 2 * w, NFQ - 1:NFQ], a[0:RFQ, NFQ - 1, :], AX.X, ALU.max,
                                      apply_absolute_value=True)
                else:
                    dve.tensor_reduce(qd[:, 0, :], qnat[:, 2 * NFQ * D:2 * NFQ * D + KD * FQ].rearrange("p (k n) -> p k n", k=KD),
                                      AX.X, ALU.max, apply_absolute_value=True)

            def weight_scales():
                dve.drain()
                for a in (qw[:, 0, :], qw[:, 2, :], qd[:, 0, :]):
                    dve.tensor_scalar(a, a, 1.0 / QMAX, None, ALU.mult)
                dve.drain()
                for w in range(2):
                    dve.reciprocal(qw[:, 2 * w + 1, :], qw[:, 2 * w, :])
                dve.reciprocal(qd[:, 1, :], qd[:, 0, :]).then_inc(q_inv, 1)

            def row_masks():
                dve.wait_ge(in_small, 16 * 24)
                dve.tensor_copy(rowf[:, :], rowm[:, :])
                dve.drain()
                dve.tensor_scalar(rowf[:, :], rowf[:, :], 0.0, None, ALU.not_equal)
                dve.wait_ge(gates_ready, 1)
            fold16(0, bo0, {3: lambda: first_stats(straight[0]), 4: lambda: row_max(0), 5: lambda: row_max(1),
                            6: lambda: row_max(2), 7: weight_scales, 8: lambda: first_stats(straight[1]), 9: first_norm,
                            11: row_masks, 13: lambda: first_stats(straight[2]), 16: lambda: first_stats(straight[3])})
            attend16(0)
            def xna(j):
                return xn_all[:, j * D:(j + 1) * D]
            dve.wait_ge(pt_full, start_of("pt", 1) - 2)
            for h in range(KD):
                ins = dve.tensor_scalar(xn[:, h * P:(h + 1) * P], ident[:, :], qd[:, 0, h:h + 1], None, ALU.mult)
            ins.then_inc(q_diag, 1)
            dve.memset(hall[:, NFQ - 1, :], 0.0)
            dve.wait_ge(ln_rstd, 2 * NB)
            dve.drain()
            for k in range(2):
                dve.tensor_tensor(xmm[:, k, :], xmm[:, k, :], mv[:, :, 0], ALU.subtract)
            dve.drain()
            for k in range(2):
                dve.tensor_tensor(xmm[:, k, :], xmm[:, k, :], rstd[:, :], ALU.mult)
            dve.drain()
            dve.tensor_reduce(qs[:, 0:1], xmm[:, :, :].rearrange("p k t -> p (k t)"), AX.X, ALU.max,
                              apply_absolute_value=True).then_inc(q_amax, 1)
            apply_norm(xna, lambda j: x[:, j * D:(j + 1) * D], straight[0], NT)
            dve.drain()

            def scale_of(k):
                dve.wait_ge(q_top, k + 1)
                dve.tensor_scalar(qs[:, 8 + k:9 + k], qs[:, 14 + k:15 + k], 0.5, 0.5, ALU.mult, ALU.add)
                dve.drain()
                dve.tensor_tensor(qs[:, 8 + k:9 + k], qs[:, 8 + k:9 + k], qs[:, 2 + k:3 + k], ALU.mult)
                dve.drain()
                dve.tensor_scalar(qs[:, 4 + k:5 + k], qs[:, 8 + k:9 + k], 1.0 / QMAX, None, ALU.mult)
                dve.drain()
                dve.reciprocal(qs[:, 6 + k:7 + k], qs[:, 4 + k:5 + k])
                dve.drain()

            def clip(a, inverse):
                dve.tensor_scalar(a, a, inverse, MAGIC, ALU.mult, ALU.add)
                dve.drain()
                return dve.tensor_scalar(a, a, MAGIC - QMAX - 1.0, MAGIC + QMAX, ALU.max, ALU.min)

            scale_of(0)
            dve.tensor_scalar(qw[:, 0, :], qw[:, 0, :], qs[:, 4:5], 0.5, ALU.mult, ALU.mult)
            dve.tensor_scalar(qw[:, 2, :], qw[:, 2, :], qs[:, 4:5], None, ALU.mult)
            dve.drain()
            dve.tensor_tensor(qw[:, 2, :], qw[:, 0, :], qw[:, 2, :], ALU.mult).then_inc(q_scaled, 1)
            dve.drain()
            dve.memset(qs[:, 12:13], 0.0).then_inc(gu_half, 4)
            dve.wait_ge(q_int, 14)
            for wT in (wgT, wuT):
                dve.memset(wT[:, :, FQ:NFQ * P], 0.0)
            dve.drain()
            for b in range(NB):
                clip(xn_all[:, b * TB * D:(b + 1) * TB * D], qs[:, 6:7]).then_inc(x_clip, 1)

            with dve.Fori(0, NB // 2) as i:
                def magnitude(n):
                    b, f = Block(n // NFQ, i), n % NFQ
                    dve.wait_ge(gu_taken, b.scaled(NFQ, 4 + f + 1))
                    dve.tensor_reduce(hmax[:, bass.ds(b.scaled(NFQ, f), 1)], hall[:, f, bass.ds(b.scaled(S), S)], AX.X,
                                      ALU.max, apply_absolute_value=True)
                for n in range(2 * NFQ):
                    b, f = Block(n // NFQ, i), n % NFQ
                    r = RFQ if f == NFQ - 1 else P
                    dve.wait_ge(act_done[1], b.scaled(NFQ, f + 1))
                    t = gate_t[n % 4][0:r, :]
                    dve.scalar_tensor_tensor(t, t, 1.0, gu[n % 4][0][0:r, :], ALU.add, ALU.mult).then_inc(gu_half, 1)
                    if n >= 4:
                        magnitude(n - 4)
                for n in range(2 * NFQ - 4, 2 * NFQ):
                    magnitude(n)
            dve.drain()
            dve.tensor_reduce(qs[:, 1:2], hmax[:, :], AX.X, ALU.max).then_inc(q_amax, 1)
            fold1(2, 0)
            scale_of(1)
            dve.wait_ge(pt_moved, start_of("pt", 1) + 5)
            dve.tensor_scalar(sdb, sdb, qs[:, 5:6], gates[:, 4:5], ALU.mult, ALU.mult).then_inc(q_scaled, 1)
            dve.drain()

            def quantise(b):
                clip(hall[:, :, b * S:(b + 1) * S], qs[:, 7:8]).then_inc(h_clip, 1)

            def back(b):
                for pair in range(2):
                    n, slot = b.fill("o", 1, pair)
                    dve.wait_ge(o_full, n + 1)
                    y = xn[:, pair * 512:(pair + 1) * 512]
                    dve.tensor_tensor(y.rearrange("p (q d) -> p q d", q=2),
                                      ob[slot][:, :].rearrange("p (q d) -> p q d", q=2),
                                      sdb.unsqueeze(1).broadcast_to([P, 2, D]), ALU.mult)
                    dve.drain()
                    xx = x[:, (b.u * TB + 2 * pair) * D:(b.u * TB + 2 * pair + 2) * D]
                    dve.tensor_tensor(xx, xx, y, ALU.add).then_inc(o_added, 1)
                    dve.drain()
            quantise(0)
            fold1(2, 1)
            quantise(1)
            fold1(2, 2)
            for b in straight:
                back(b)
                if b.u + 2 < NB:
                    quantise(b.u + 2)
                norm_stats(b)
                if b.u == 1 or b.u == 2:
                    fold1(4, b.u - 1)
            norm_next(1, straight[-1], start_of("pt", 2) - 2)
            fold1(4, 2)
            attend1(2)
            for q, dst in enumerate(split3):
                rest(dst, pt[(start_of("pt", 3) + q) % 2][:, :], q + 1, pt_moved)
            experts(3, NE + 1)
            attend1(4)
            dve.memset(base[:, :], 0.0)

            def route5(b):
                norm_next(5, b, xn_free(5, b, 3))
                dve.wait_ge(pt_moved, b.fill("pt", 5, 1)[0] + 1)
                softmax_shift(lg)
                places(lg, 1)
                dve.tensor_copy(ohb[:, :, :], oh[:, :, :]).then_inc(hot_ready, 1)
                softmax_probs(b.scaled(1, 4 + 1))
                dve.tensor_reduce(sr[:, 3, :], ws[:, :, :], AX.X, ALU.max)
                dve.wait_ge(pt_moved, b.fill("pt", 5, 4)[0] + 1)
                c3 = cnt[:, 0:TB * NE].rearrange("p (j e) -> p j e", j=TB)
                dve.tensor_tensor(c3, c3, base[:, :].unsqueeze(1).broadcast_to([P, TB, NE]), ALU.add)
                dve.drain()
                dve.tensor_tensor(c3, c3, oh[:, :, :], ALU.mult)
                dve.tensor_tensor(base[:, :], base[:, :], cnt[:, TB * NE:(TB + 1) * NE], ALU.add)
                dve.drain()
                dve.tensor_reduce(sr[:, 0, :], c3, AX.X, ALU.add)
                dve.drain()
                dve.tensor_scalar(sr[:, 1, :], sr[:, 0, :], float(CAP), gates[:, 6:7], ALU.is_le, ALU.mult)
                dve.drain()
                dve.tensor_tensor(sr[:, 2, :], sr[:, 1, :], sr[:, 3, :], ALU.mult)
                dve.drain()
                for pair in range(2):
                    n, slot = b.fill("o", 5, pair)
                    dve.wait_ge(o_full, n + 1)
                    for q in range(2):
                        j = 2 * pair + q
                        ins = dve.scalar_tensor_tensor(xt(b, j), ob[slot][:, q * D:(q + 1) * D], sr[:, 2, j:j + 1],
                                                       xt(b, j), ALU.mult, ALU.add)
                    ins.then_inc(o_added, 1)
            for b in straight:
                route5(b)
                norm_stats(b)
            fold16(6, bo3)
            attend16(6)
            experts(7, NE + 2)


_INS = ['x', 'ctx_1024', 'mask_BxSxS2_bk1', 'mask_BxS_ik1', 'g_xattn', 'g_ffn', 'L0_xattn_Wq', 'L0_xattn_Wk', 'L0_xattn_Wv', 'L0_xattn_Wo', 'L0_xattn_bo', 'L0_ffn_clip_x', 'L0_ffn_clip_down', 'L0_ffn_w_gate', 'L0_ffn_w_up', 'L0_ffn_w_down', 'L1_xattn_Wq', 'L1_xattn_bq', 'L1_xattn_Wk', 'L1_xattn_bk', 'L1_xattn_Wv', 'L1_xattn_bv', 'L1_ffn_gate_w', 'L1_ffn_lb_bias', 'L1_ffn_w1', 'L1_ffn_w2', 'L1_ffn_cfc', 'L1_ffn_cproj', 'L2_xattn_Wq', 'L2_xattn_bq', 'L2_xattn_Wk', 'L2_xattn_bk', 'L2_xattn_Wv', 'L2_xattn_bv', 'L2_xattn_Wfc', 'L2_xattn_bfc', 'L2_ffn_w_gate', 'L2_ffn_w_expert', 'L2_ffn_b_expert', 'L3_xattn_ln_l_w', 'L3_xattn_ln_l_b', 'L3_xattn_ln_c_w', 'L3_xattn_ln_c_b', 'L3_xattn_Wq', 'L3_xattn_Wkv', 'L3_xattn_Wo', 'L3_xattn_bo', 'L3_ffn_router_w', 'L3_ffn_w1', 'L3_ffn_w2', 'L3_ffn_shared_gate_up', 'L3_ffn_shared_down', 'L3_ffn_shared_gate_w']


def kernel(**inputs):
    import numpy as _np
    import concourse.bacc as _bacc
    from concourse import mybir as _mybir
    from concourse.bass_utils import run_bass_kernel_spmd as _run

    nc = _bacc.Bacc("TRN2", target_bir_lowering=False, num_devices=1)
    arrays, args = {}, {}
    for name in _INS:
        a = _np.ascontiguousarray(inputs[name])
        arrays[f"in_{name}"] = a
        args[name] = nc.dram_tensor(f"in_{name}", a.shape, _mybir.dt.from_np(a.dtype), kind="ExternalInput").ap()
    out = nc.dram_tensor("out_0", (NB, S, D), F32, kind="ExternalOutput").ap()
    layers_kernel(nc, args, out)
    r = _run(nc, [arrays], core_ids=[0])
    return r.results[0]["out_0"]
```
